# Optimizing a Trainium2 kernel written in Bass

```python
import numpy as np
import jax
import jax.numpy as jnp

def _softmax(x, axis=-1):
    return jax.nn.softmax(x, axis=axis)

def _gelu(x):
    return jax.nn.gelu(x, approximate=True)

def _silu(x):
    return jax.nn.silu(x)

def _sigmoid(x):
    return jax.nn.sigmoid(x)

def _layernorm(x, axis=-1, eps=1e-05):
    m = jnp.mean(x, axis=axis, keepdims=True)
    v = jnp.var(x, axis=axis, keepdims=True)
    return (x - m) / jnp.sqrt(v + eps)

def _scatter_add(tgt, idx, src, axis=0):
    return tgt.at[idx].add(src)

def _segment_sum(src, seg, n):
    return jax.ops.segment_sum(src, seg, n)
kernel_name = 'mk_xattn_ffn_d4_seqx_r8_83ad1a'

def setup_inputs(seed: int=0):
    np.random.seed(seed)
    _w = jnp.asarray

    def _rec_inputs():
        import jax
        import jax.numpy as jnp
        _rk = jax.random.key(seed)
        x = -0.0002928 + 1 * jax.random.normal(jax.random.fold_in(_rk, 1), (32, 100, 128), jnp.float32)
        _lenS = 100 - jax.random.randint(jax.random.fold_in(_rk, 7), (32,), 0, max(1, 100 // 4) + 1, jnp.int32)
        _lenS2 = 1444 - jax.random.randint(jax.random.fold_in(_rk, 8), (32,), 0, max(1, 1444 // 4) + 1, jnp.int32)
        _ctx_1024P = jax.random.normal(jax.random.fold_in(_rk, 11), (32, 16, 128), jnp.float32)
        _ctx_1024c = jax.random.dirichlet(jax.random.fold_in(_rk, 511), 0.3 * jnp.ones((16,), jnp.float32), (32, 1444))
        _ctx_1024t = jnp.einsum('bsk,bkd->bsd', _ctx_1024c, _ctx_1024P)
        _ctx_1024t = _ctx_1024t * jax.lax.rsqrt(jnp.mean(jnp.square(_ctx_1024t)) + 1e-12) * 0.953939
        ctx_1024 = -1.39393e-06 + 0.999914 * (_ctx_1024t + 0.3 * jax.random.normal(jax.random.fold_in(_rk, 611), (32, 1444, 128), jnp.float32))
        _validS = jnp.arange(100)[None, :] < _lenS[:, None]
        _validS2 = jnp.arange(1444)[None, :] < _lenS2[:, None]
        _causal = jnp.tril(jnp.ones((100, 100), dtype=bool))
        mask_1x1xSxS2_bk0 = jnp.logical_not(jnp.broadcast_to(_validS2[0:1, None, None, :], (1, 1, 100, 1444)))
        mask_BxS2_bk0 = jnp.logical_not(jnp.broadcast_to(_validS2[:, :], (32, 1444)))
        mask_BxS2_if1 = jnp.where(jnp.ones((32, 1444), dtype=bool), 1, 0).astype(jnp.int32)
        return (x, ctx_1024, mask_1x1xSxS2_bk0, mask_BxS2_bk0, mask_BxS2_if1)
    x, ctx_1024, mask_1x1xSxS2_bk0, mask_BxS2_bk0, mask_BxS2_if1 = _rec_inputs()

    def _L0_xattn_setup():
        import jax, jax.numpy as jnp
        import numpy as np
        D_MODEL = 128
        NUM_HEADS = 16
        HEAD_DIM = D_MODEL // NUM_HEADS
        B, S = (2, 256)

        def _split_heads(x):
            b, s, _ = x.shape
            return x.reshape(b, s, NUM_HEADS, HEAD_DIM).transpose(0, 2, 1, 3)
        key = jax.random.key(seed)
        ks = jax.random.split(key, 8)
        scale = 1.0 / np.sqrt(D_MODEL)
        inp = {'query': jax.random.normal(ks[0], (B, S, D_MODEL), jnp.float32), 'key': jax.random.normal(ks[1], (B, S, D_MODEL), jnp.float32), 'value': jax.random.normal(ks[2], (B, S, D_MODEL), jnp.float32), 'mask': jnp.tril(jnp.ones((S, S), dtype=bool))[None, None, :, :], 'Wq': jax.random.normal(ks[3], (D_MODEL, D_MODEL), jnp.float32) * scale, 'Wk': jax.random.normal(ks[4], (D_MODEL, D_MODEL), jnp.float32) * scale, 'Wv': jax.random.normal(ks[5], (D_MODEL, D_MODEL), jnp.float32) * scale, 'Wo': jax.random.normal(ks[6], (D_MODEL, D_MODEL), jnp.float32) * scale, 'bo': jax.random.normal(ks[7], (D_MODEL,), jnp.float32) * scale}
        return inp
    _L0_xattn_all = _L0_xattn_setup()
    _L0_xattn_in = {k: v for k, v in _L0_xattn_all.items() if k in ('Wq', 'Wk', 'Wv', 'Wo', 'bo')}
    del _L0_xattn_all

    def _L0_ffn_setup():
        import jax, jax.numpy as jnp
        import numpy as np
        BLOCK = 32
        W_BITS = 4
        ACT_BITS = 16

        def act_qdq(x):
            qmax = 2.0 ** (ACT_BITS - 1) - 1.0
            scale = jnp.maximum(jnp.max(jnp.abs(x)) / qmax, 1e-12)
            return jnp.clip(jnp.round(x / scale), -qmax - 1.0, qmax) * scale

        def fixed_qdq_u16(x):
            scale = 1.0 / 65536.0
            return jnp.clip(jnp.round(x / scale), 0.0, 65535.0) * scale

        def lpbq_dequant(w):
            O, I = w.shape
            qmax = 2.0 ** (W_BITS - 1) - 1.0
            wb = w.reshape(O, I // BLOCK, BLOCK)
            s = jnp.maximum(jnp.max(jnp.abs(wb), axis=-1, keepdims=True) / qmax, 1e-12)
            wq = jnp.clip(jnp.round(wb / s), -qmax - 1.0, qmax) * s
            return wq.reshape(O, I)
        key = jax.random.key(seed)
        k1, k2, k3, k4 = jax.random.split(key, 4)
        B, S, H, I = (2, 512, 128, 384)
        x = jax.random.normal(k1, (B, S, H), jnp.float32)
        w_gate = jax.random.normal(k2, (I, H), jnp.float32) * 0.02
        w_up = jax.random.normal(k3, (I, H), jnp.float32) * 0.02
        w_down = jax.random.normal(k4, (H, I), jnp.float32) * 0.02
        return {'x': x, 'w_gate': w_gate, 'w_up': w_up, 'w_down': w_down}
    _L0_ffn_all = _L0_ffn_setup()
    _L0_ffn_in = {k: v for k, v in _L0_ffn_all.items() if k in ('w_gate', 'w_up', 'w_down')}
    del _L0_ffn_all

    def _L1_xattn_setup():
        import jax, jax.numpy as jnp
        import numpy as np
        B, TQ, TK, D, H = (2, 256, 256, 128, 16)
        HD = D // H
        NUM_PAD = 32
        key = jax.random.key(seed)
        ks = jax.random.split(key, 8)
        s = 0.02
        q = jax.random.normal(ks[0], (B, TQ, D), dtype=jnp.float32)
        kv = jax.random.normal(ks[1], (B, TK, D), dtype=jnp.float32)
        key_padding_mask = jnp.broadcast_to(jnp.arange(TK) >= TK - NUM_PAD, (B, TK))
        Wq = jax.random.normal(ks[2], (D, D), dtype=jnp.float32) * s
        bq = jax.random.normal(ks[3], (D,), dtype=jnp.float32) * s
        Wkv = jax.random.normal(ks[4], (D, 2 * D), dtype=jnp.float32) * s
        bkv = jax.random.normal(ks[5], (2 * D,), dtype=jnp.float32) * s
        Wo = jax.random.normal(ks[6], (D, D), dtype=jnp.float32) * s
        bo = jax.random.normal(ks[7], (D,), dtype=jnp.float32) * s
        return {'q': q, 'kv': kv, 'key_padding_mask': key_padding_mask, 'Wq': Wq, 'bq': bq, 'Wkv': Wkv, 'bkv': bkv, 'Wo': Wo, 'bo': bo}
    _L1_xattn_all = _L1_xattn_setup()
    _L1_xattn_in = {k: v for k, v in _L1_xattn_all.items() if k in ('Wq', 'bq', 'Wkv', 'bkv', 'Wo', 'bo')}
    del _L1_xattn_all

    def _L1_ffn_setup():
        import jax, jax.numpy as jnp
        import numpy as np
        GROUP = 16
        EPS = 1e-05

        def _dequant(q, scale):
            w = q.astype(jnp.float32) / 7.5 - 1.0
            return w * jnp.repeat(scale, GROUP, axis=1)

        def _qlora_linear(x, q, scale, bias, la, lb):
            w = _dequant(q, scale)
            base = jnp.einsum('btd,od->bto', x, w) + bias
            lora = jnp.einsum('btr,or->bto', jnp.einsum('btd,rd->btr', x, la), lb)
            return base + lora

        def _layernorm(x, g, b):
            mu = jnp.mean(x, axis=-1, keepdims=True)
            var = jnp.mean(jnp.square(x - mu), axis=-1, keepdims=True)
            return (x - mu) * jax.lax.rsqrt(var + EPS) * g + b
        key = jax.random.key(seed)
        ks = jax.random.split(key, 6)
        D, R, B, T = (128, 32, 8, 512)
        x = jax.random.normal(ks[0], (B, T, D), dtype=jnp.float32)
        qweights = jax.random.randint(ks[1], (6, D, D), 0, 16, dtype=jnp.int32)
        scales = jax.random.uniform(ks[2], (6, D, D // GROUP), dtype=jnp.float32)
        biases = jax.random.normal(ks[3], (6, D), dtype=jnp.float32) * 0.02
        lora_a = jax.random.normal(ks[4], (6, R, D), dtype=jnp.float32) * 0.02
        lora_b = jax.random.normal(ks[5], (6, D, R), dtype=jnp.float32) * 0.02
        ln_gamma = jnp.ones((3, D), dtype=jnp.float32)
        ln_beta = jnp.zeros((3, D), dtype=jnp.float32)
        return {'x': x, 'qweights': qweights, 'scales': scales, 'biases': biases, 'lora_a': lora_a, 'lora_b': lora_b, 'ln_gamma': ln_gamma, 'ln_beta': ln_beta}
    _L1_ffn_all = _L1_ffn_setup()
    _L1_ffn_in = {k: v for k, v in _L1_ffn_all.items() if k in ('qweights', 'scales', 'biases', 'lora_a', 'lora_b', 'ln_gamma', 'ln_beta')}
    del _L1_ffn_all

    def _L2_xattn_setup():
        import jax, jax.numpy as jnp
        import numpy as np
        B, T, D, H = (2, 256, 128, 16)
        DK = D // H
        key = jax.random.key(seed)
        ks = jax.random.split(key, 11)
        w_scale = 1.0 / np.sqrt(D)
        return {'q': jax.random.normal(ks[0], (B, T, D), dtype=jnp.float32), 'k': jax.random.normal(ks[1], (B, T, D), dtype=jnp.float32), 'v': jax.random.normal(ks[2], (B, T, D), dtype=jnp.float32), 'Wq': jax.random.normal(ks[3], (D, D), dtype=jnp.float32) * w_scale, 'bq': jnp.zeros((D,), dtype=jnp.float32), 'Wk': jax.random.normal(ks[4], (D, D), dtype=jnp.float32) * w_scale, 'bk': jnp.zeros((D,), dtype=jnp.float32), 'Wv': jax.random.normal(ks[5], (D, D), dtype=jnp.float32) * w_scale, 'bv': jnp.zeros((D,), dtype=jnp.float32), 'Wo': jax.random.normal(ks[6], (D, D), dtype=jnp.float32) * w_scale, 'bo': jnp.zeros((D,), dtype=jnp.float32), 'mask': jnp.ones((B, T), dtype=jnp.int32), 'causal': 1}
    _L2_xattn_all = _L2_xattn_setup()
    _L2_xattn_in = {k: v for k, v in _L2_xattn_all.items() if k in ('Wq', 'bq', 'Wk', 'bk', 'Wv', 'bv', 'Wo', 'bo')}
    del _L2_xattn_all

    def _L2_ffn_setup():
        import jax, jax.numpy as jnp
        import numpy as np
        H = 128
        RH = 64
        E = 16
        B, S = (4, 256)
        TEMP = 1.0
        key = jax.random.key(seed)
        ks = jax.random.split(key, 12)
        sc = lambda fan_in: 1.0 / np.sqrt(fan_in)
        return {'hidden_states': jax.random.normal(ks[0], (B, S, H), dtype=jnp.float32), 'W1': jax.random.uniform(ks[1], (H, RH), jnp.float32, -sc(H), sc(H)), 'b1': jax.random.uniform(ks[2], (RH,), jnp.float32, -sc(H), sc(H)), 'W2': jax.random.uniform(ks[3], (RH, E), jnp.float32, -sc(RH), sc(RH)), 'b2': jax.random.uniform(ks[4], (E,), jnp.float32, -sc(RH), sc(RH)), 'Wg1': jax.random.uniform(ks[5], (H, RH), jnp.float32, -sc(H), sc(H)), 'bg1': jax.random.uniform(ks[6], (RH,), jnp.float32, -sc(H), sc(H)), 'Wg2': jax.random.uniform(ks[7], (RH, 1), jnp.float32, -sc(RH), sc(RH)), 'bg2': jax.random.uniform(ks[8], (1,), jnp.float32, -sc(RH), sc(RH)), 'expert_scales': jax.random.normal(ks[9], (E, H), dtype=jnp.float32), 'expert_biases': jax.random.normal(ks[10], (E, H), dtype=jnp.float32)}
    _L2_ffn_all = _L2_ffn_setup()
    _L2_ffn_in = {k: v for k, v in _L2_ffn_all.items() if k in ('W1', 'b1', 'W2', 'b2', 'Wg1', 'bg1', 'Wg2', 'bg2', 'expert_scales', 'expert_biases')}
    del _L2_ffn_all

    def _L3_xattn_setup():
        import jax, jax.numpy as jnp
        import numpy as np
        H = 8
        D = 128
        DQ = D // H
        BN = 64
        HID = 128
        B = 16
        S_T = 128
        S_M = 256
        SCALE = DQ ** 0.25
        EPS = 1e-05

        def _ln(x, g, b):
            m = jnp.mean(x, axis=-1, keepdims=True)
            v = jnp.mean(jnp.square(x - m), axis=-1, keepdims=True)
            return (x - m) * jax.lax.rsqrt(v + EPS) * g + b

        def _mhla(xq, xk, xv, Wq, Wk, Wv, Wo, masked):
            Q = jnp.einsum('bsq,hqd->bhsd', xq, Wq)
            K = jnp.einsum('bsq,hqd->bhsd', xk, Wk)
            V = jnp.einsum('bsq,hqd->bhsd', xv, Wv)
            if masked:
                s, d = (Q.shape[-2], Q.shape[-1])
                m = jnp.where(jnp.arange(d)[None, :] <= jnp.arange(s)[:, None], 0.0, -jnp.inf)
                Q = Q + m.astype(Q.dtype)
            A = jnp.einsum('bhsd,bhse->bhde', jax.nn.softmax(K / SCALE, axis=-1), V)
            Bm = jnp.einsum('bhsd,bhde->bhse', jax.nn.softmax(Q / SCALE, axis=-1), A)
            b, h, w, dd = Bm.shape
            Bm = Bm.reshape(b, w, h * dd)
            return Bm @ Wo.T
        key = jax.random.key(seed)
        ks = jax.random.split(key, 24)
        r = lambda k, sh, s=0.02: jax.random.normal(k, sh, jnp.float32) * s
        return {'mem': jax.random.normal(ks[0], (B, S_M, D), jnp.float32), 'y': jax.random.normal(ks[1], (B, S_T, D), jnp.float32), 'Wq1': r(ks[2], (H, D, DQ)), 'Wk1': r(ks[3], (H, D, DQ)), 'Wv1': r(ks[4], (H, D, DQ)), 'Wo1': r(ks[5], (D, D)), 'Wq2': r(ks[6], (H, D, DQ)), 'Wk2': r(ks[7], (H, D, DQ)), 'Wv2': r(ks[8], (H, D, DQ)), 'Wo2': r(ks[9], (D, D)), 'E1': r(ks[10], (BN, D)), 'D1': r(ks[11], (HID, BN)), 'E2': r(ks[12], (BN, HID)), 'D2': r(ks[13], (D, BN)), 'g1': jnp.ones((D,), jnp.float32), 'b1': jnp.zeros((D,), jnp.float32), 'g2': jnp.ones((D,), jnp.float32), 'b2': jnp.zeros((D,), jnp.float32), 'g3': jnp.ones((D,), jnp.float32), 'b3': jnp.zeros((D,), jnp.float32)}
    _L3_xattn_all = _L3_xattn_setup()
    _L3_xattn_in = {k: v for k, v in _L3_xattn_all.items() if k in ('Wq1', 'Wk1', 'Wv1', 'Wo1', 'Wq2', 'Wk2', 'Wv2', 'Wo2', 'E1', 'D1', 'E2', 'D2', 'g1', 'b1', 'g2', 'b2', 'g3', 'b3')}
    del _L3_xattn_all

    def _L3_ffn_setup():
        import jax, jax.numpy as jnp
        import numpy as np
        EPS = 1e-06
        LN_EPS = 1e-05

        def _absmean_core(W):
            gamma = jnp.mean(jnp.abs(W)) + EPS
            Ws = W / gamma
            Wq = jnp.sign(Ws) * jnp.minimum(jnp.round(jnp.abs(Ws)), 1.0)
            return (Wq, gamma)

        @jax.custom_vjp
        def absmean(W):
            return _absmean_core(W)[0]

        def _absmean_fwd(W):
            Wq, gamma = _absmean_core(W)
            return (Wq, gamma)

        def _absmean_bwd(gamma, g):
            return (g / gamma,)
        absmean.defvjp(_absmean_fwd, _absmean_bwd)

        def layernorm(x, w, b, eps=LN_EPS):
            mu = jnp.mean(x, axis=-1, keepdims=True)
            var = jnp.mean((x - mu) ** 2, axis=-1, keepdims=True)
            return (x - mu) * jax.lax.rsqrt(var + eps) * w + b
        key = jax.random.key(seed)
        k1, k2, k3 = jax.random.split(key, 3)
        d, h = (128, 512)
        B, T = (8, 256)
        return {'x': jax.random.normal(k1, (B, T, d), jnp.float32), 'W_fc': jax.random.normal(k2, (h, d), jnp.float32), 'ln_w': jnp.ones((h,), jnp.float32), 'ln_b': jnp.zeros((h,), jnp.float32), 'W_proj': jax.random.normal(k3, (d, h), jnp.float32)}
    _L3_ffn_all = _L3_ffn_setup()
    _L3_ffn_in = {k: v for k, v in _L3_ffn_all.items() if k in ('W_fc', 'ln_w', 'ln_b', 'W_proj')}
    del _L3_ffn_all
    return {'x': x, 'ctx_1024': ctx_1024, 'mask_1x1xSxS2_bk0': mask_1x1xSxS2_bk0, 'mask_BxS2_bk0': mask_BxS2_bk0, 'mask_BxS2_if1': mask_BxS2_if1, 'L0_xattn_Wq': _L0_xattn_in['Wq'], 'L0_xattn_Wk': _L0_xattn_in['Wk'], 'L0_xattn_Wv': _L0_xattn_in['Wv'], 'L0_xattn_Wo': _L0_xattn_in['Wo'], 'L0_xattn_bo': _L0_xattn_in['bo'], 'L0_ffn_w_gate': _L0_ffn_in['w_gate'], 'L0_ffn_w_up': _L0_ffn_in['w_up'], 'L0_ffn_w_down': _L0_ffn_in['w_down'], 'L1_xattn_Wq': _L1_xattn_in['Wq'], 'L1_xattn_bq': _L1_xattn_in['bq'], 'L1_xattn_Wkv': _L1_xattn_in['Wkv'], 'L1_xattn_bkv': _L1_xattn_in['bkv'], 'L1_xattn_Wo': _L1_xattn_in['Wo'], 'L1_xattn_bo': _L1_xattn_in['bo'], 'L1_ffn_qweights': _L1_ffn_in['qweights'], 'L1_ffn_scales': _L1_ffn_in['scales'], 'L1_ffn_biases': _L1_ffn_in['biases'], 'L1_ffn_lora_a': _L1_ffn_in['lora_a'], 'L1_ffn_lora_b': _L1_ffn_in['lora_b'], 'L1_ffn_ln_gamma': _L1_ffn_in['ln_gamma'], 'L1_ffn_ln_beta': _L1_ffn_in['ln_beta'], 'L2_xattn_Wq': _L2_xattn_in['Wq'], 'L2_xattn_bq': _L2_xattn_in['bq'], 'L2_xattn_Wk': _L2_xattn_in['Wk'], 'L2_xattn_bk': _L2_xattn_in['bk'], 'L2_xattn_Wv': _L2_xattn_in['Wv'], 'L2_xattn_bv': _L2_xattn_in['bv'], 'L2_xattn_Wo': _L2_xattn_in['Wo'], 'L2_xattn_bo': _L2_xattn_in['bo'], 'L2_ffn_W1': _L2_ffn_in['W1'], 'L2_ffn_b1': _L2_ffn_in['b1'], 'L2_ffn_W2': _L2_ffn_in['W2'], 'L2_ffn_b2': _L2_ffn_in['b2'], 'L2_ffn_Wg1': _L2_ffn_in['Wg1'], 'L2_ffn_bg1': _L2_ffn_in['bg1'], 'L2_ffn_Wg2': _L2_ffn_in['Wg2'], 'L2_ffn_bg2': _L2_ffn_in['bg2'], 'L2_ffn_expert_scales': _L2_ffn_in['expert_scales'], 'L2_ffn_expert_biases': _L2_ffn_in['expert_biases'], 'L3_xattn_Wq1': _L3_xattn_in['Wq1'], 'L3_xattn_Wk1': _L3_xattn_in['Wk1'], 'L3_xattn_Wv1': _L3_xattn_in['Wv1'], 'L3_xattn_Wo1': _L3_xattn_in['Wo1'], 'L3_xattn_Wq2': _L3_xattn_in['Wq2'], 'L3_xattn_Wk2': _L3_xattn_in['Wk2'], 'L3_xattn_Wv2': _L3_xattn_in['Wv2'], 'L3_xattn_Wo2': _L3_xattn_in['Wo2'], 'L3_xattn_E1': _L3_xattn_in['E1'], 'L3_xattn_D1': _L3_xattn_in['D1'], 'L3_xattn_E2': _L3_xattn_in['E2'], 'L3_xattn_D2': _L3_xattn_in['D2'], 'L3_xattn_g1': _L3_xattn_in['g1'], 'L3_xattn_b1': _L3_xattn_in['b1'], 'L3_xattn_g2': _L3_xattn_in['g2'], 'L3_xattn_b2': _L3_xattn_in['b2'], 'L3_xattn_g3': _L3_xattn_in['g3'], 'L3_xattn_b3': _L3_xattn_in['b3'], 'L3_ffn_W_fc': _L3_ffn_in['W_fc'], 'L3_ffn_ln_w': _L3_ffn_in['ln_w'], 'L3_ffn_ln_b': _L3_ffn_in['ln_b'], 'L3_ffn_W_proj': _L3_ffn_in['W_proj']}

def reference(x, ctx_1024, mask_1x1xSxS2_bk0, mask_BxS2_bk0, mask_BxS2_if1, L0_xattn_Wq, L0_xattn_Wk, L0_xattn_Wv, L0_xattn_Wo, L0_xattn_bo, L0_ffn_w_gate, L0_ffn_w_up, L0_ffn_w_down, L1_xattn_Wq, L1_xattn_bq, L1_xattn_Wkv, L1_xattn_bkv, L1_xattn_Wo, L1_xattn_bo, L1_ffn_qweights, L1_ffn_scales, L1_ffn_biases, L1_ffn_lora_a, L1_ffn_lora_b, L1_ffn_ln_gamma, L1_ffn_ln_beta, L2_xattn_Wq, L2_xattn_bq, L2_xattn_Wk, L2_xattn_bk, L2_xattn_Wv, L2_xattn_bv, L2_xattn_Wo, L2_xattn_bo, L2_ffn_W1, L2_ffn_b1, L2_ffn_W2, L2_ffn_b2, L2_ffn_Wg1, L2_ffn_bg1, L2_ffn_Wg2, L2_ffn_bg2, L2_ffn_expert_scales, L2_ffn_expert_biases, L3_xattn_Wq1, L3_xattn_Wk1, L3_xattn_Wv1, L3_xattn_Wo1, L3_xattn_Wq2, L3_xattn_Wk2, L3_xattn_Wv2, L3_xattn_Wo2, L3_xattn_E1, L3_xattn_D1, L3_xattn_E2, L3_xattn_D2, L3_xattn_g1, L3_xattn_b1, L3_xattn_g2, L3_xattn_b2, L3_xattn_g3, L3_xattn_b3, L3_ffn_W_fc, L3_ffn_ln_w, L3_ffn_ln_b, L3_ffn_W_proj):
    import jax
    import jax.numpy as jnp

    def _L0_xattn_ref(query, key, value, mask, Wq, Wk, Wv, Wo, bo):
        import jax, jax.numpy as jnp
        import numpy as np
        D_MODEL = 128
        NUM_HEADS = 16
        HEAD_DIM = D_MODEL // NUM_HEADS
        B, S = (2, 256)

        def _split_heads(x):
            b, s, _ = x.shape
            return x.reshape(b, s, NUM_HEADS, HEAD_DIM).transpose(0, 2, 1, 3)
        q = _split_heads(query @ Wq.T)
        k = _split_heads(key @ Wk.T)
        v = _split_heads(value @ Wv.T)
        scores = jnp.einsum('bhqd,bhkd->bhqk', q, k) / jnp.sqrt(jnp.float32(HEAD_DIM))
        scores = jnp.where(mask, scores, jnp.float32(-jnp.inf))
        attn = jax.nn.softmax(scores, axis=-1)
        out = jnp.einsum('bhqk,bhkd->bhqd', attn, v)
        out = out.transpose(0, 2, 1, 3).reshape(query.shape[0], q.shape[2], D_MODEL)
        return out @ Wo.T + bo

    def _L0_ffn_ref(x, w_gate, w_up, w_down):
        import jax, jax.numpy as jnp
        import numpy as np
        BLOCK = 32
        W_BITS = 4
        ACT_BITS = 16

        def act_qdq(x):
            qmax = 2.0 ** (ACT_BITS - 1) - 1.0
            scale = jnp.maximum(jnp.max(jnp.abs(x)) / qmax, 1e-12)
            return jnp.clip(jnp.round(x / scale), -qmax - 1.0, qmax) * scale

        def fixed_qdq_u16(x):
            scale = 1.0 / 65536.0
            return jnp.clip(jnp.round(x / scale), 0.0, 65535.0) * scale

        def lpbq_dequant(w):
            O, I = w.shape
            qmax = 2.0 ** (W_BITS - 1) - 1.0
            wb = w.reshape(O, I // BLOCK, BLOCK)
            s = jnp.maximum(jnp.max(jnp.abs(wb), axis=-1, keepdims=True) / qmax, 1e-12)
            wq = jnp.clip(jnp.round(wb / s), -qmax - 1.0, qmax) * s
            return wq.reshape(O, I)
        x = act_qdq(x)
        up = act_qdq(x @ lpbq_dequant(w_up).T)
        gate = act_qdq(x @ lpbq_dequant(w_gate).T)
        sig = fixed_qdq_u16(jax.nn.sigmoid(gate))
        gate = act_qdq(gate * sig)
        o = act_qdq(gate * up)
        return o @ lpbq_dequant(w_down).T

    def _L1_xattn_ref(q, kv, key_padding_mask, Wq, bq, Wkv, bkv, Wo, bo):
        import jax, jax.numpy as jnp
        import numpy as np
        B, TQ, TK, D, H = (2, 256, 256, 128, 16)
        HD = D // H
        NUM_PAD = 32
        Bc, Tq, Dm = q.shape
        Tk = kv.shape[1]
        scale = HD ** (-0.5)
        Q = (q @ Wq + bq).reshape(Bc, Tq, H, HD).transpose(0, 2, 1, 3)
        KV = (kv @ Wkv + bkv).reshape(Bc, Tk, 2, H, HD).transpose(2, 0, 3, 1, 4)
        K, V = (KV[0], KV[1])
        attn = jnp.einsum('bhqd,bhkd->bhqk', Q, K) * scale
        attn = jnp.where(key_padding_mask[:, None, None, :], -jnp.inf, attn)
        attn = jax.nn.softmax(attn, axis=-1)
        out = jnp.einsum('bhqk,bhkd->bhqd', attn, V)
        out = out.transpose(0, 2, 1, 3).reshape(Bc, Tq, Dm)
        return out @ Wo + bo

    def _L1_ffn_ref(x, qweights, scales, biases, lora_a, lora_b, ln_gamma, ln_beta):
        import jax, jax.numpy as jnp
        import numpy as np
        GROUP = 16
        EPS = 1e-05

        def _dequant(q, scale):
            w = q.astype(jnp.float32) / 7.5 - 1.0
            return w * jnp.repeat(scale, GROUP, axis=1)

        def _qlora_linear(x, q, scale, bias, la, lb):
            w = _dequant(q, scale)
            base = jnp.einsum('btd,od->bto', x, w) + bias
            lora = jnp.einsum('btr,or->bto', jnp.einsum('btd,rd->btr', x, la), lb)
            return base + lora

        def _layernorm(x, g, b):
            mu = jnp.mean(x, axis=-1, keepdims=True)
            var = jnp.mean(jnp.square(x - mu), axis=-1, keepdims=True)
            return (x - mu) * jax.lax.rsqrt(var + EPS) * g + b
        h = x
        for blk in range(3):
            i0, i1 = (2 * blk, 2 * blk + 1)
            y = _qlora_linear(h, qweights[i0], scales[i0], biases[i0], lora_a[i0], lora_b[i0])
            y = _layernorm(y, ln_gamma[blk], ln_beta[blk])
            y = jax.nn.gelu(y, approximate=False)
            y = _qlora_linear(y, qweights[i1], scales[i1], biases[i1], lora_a[i1], lora_b[i1])
            h = y + h
        return h

    def _L2_xattn_ref(q, k, v, Wq, bq, Wk, bk, Wv, bv, Wo, bo, mask, causal):
        import jax, jax.numpy as jnp
        import numpy as np
        B, T, D, H = (2, 256, 128, 16)
        DK = D // H
        Bq, Tq, _ = q.shape
        Tk = k.shape[1]
        qh = (q @ Wq.T + bq).reshape(Bq, Tq, H, DK).transpose(0, 2, 1, 3)
        kh = (k @ Wk.T + bk).reshape(Bq, Tk, H, DK).transpose(0, 2, 1, 3)
        vh = (v @ Wv.T + bv).reshape(Bq, Tk, H, DK).transpose(0, 2, 1, 3)
        logits = jnp.einsum('bhqd,bhkd->bhqk', qh, kh) / jnp.sqrt(jnp.float32(DK))
        neg_inf = jnp.float32(-jnp.inf)
        if causal:
            causal_mask = jnp.tril(jnp.ones((Tq, Tk), dtype=jnp.bool_))
            logits = jnp.where(causal_mask[None, None, :, :], logits, neg_inf)
        if mask is not None:
            logits = jnp.where(mask[:, None, None, :] != 0, logits, neg_inf)
        alphas = jax.nn.softmax(logits, axis=-1)
        context = jnp.einsum('bhqk,bhkd->bhqd', alphas, vh)
        context = context.transpose(0, 2, 1, 3).reshape(Bq, Tq, D)
        return context @ Wo.T + bo

    def _L2_ffn_ref(hidden_states, W1, b1, W2, b2, Wg1, bg1, Wg2, bg2, expert_scales, expert_biases):
        import jax, jax.numpy as jnp
        import numpy as np
        H = 128
        RH = 64
        E = 16
        B, S = (4, 256)
        TEMP = 1.0
        b, s, h = hidden_states.shape
        flat = hidden_states.reshape(-1, h)
        routing_scores = jax.nn.relu(flat @ W1 + b1) @ W2 + b2
        routing_scores = routing_scores / TEMP
        gate = jax.nn.sigmoid(jnp.tanh(flat @ Wg1 + bg1) @ Wg2 + bg2)
        routing_scores = routing_scores * gate
        expert_probs = jax.nn.softmax(routing_scores, axis=-1)
        top_idx = jnp.argmax(expert_probs, axis=-1)
        scales = expert_scales[top_idx]
        biases = expert_biases[top_idx]
        routed = flat * scales + biases
        return routed.reshape(b, s, h)

    def _L3_xattn_ref(mem, y, Wq1, Wk1, Wv1, Wo1, Wq2, Wk2, Wv2, Wo2, E1, D1, E2, D2, g1, b1, g2, b2, g3, b3):
        import jax, jax.numpy as jnp
        import numpy as np
        H = 8
        D = 128
        DQ = D // H
        BN = 64
        HID = 128
        B = 16
        S_T = 128
        S_M = 256
        SCALE = DQ ** 0.25
        EPS = 1e-05

        def _ln(x, g, b):
            m = jnp.mean(x, axis=-1, keepdims=True)
            v = jnp.mean(jnp.square(x - m), axis=-1, keepdims=True)
            return (x - m) * jax.lax.rsqrt(v + EPS) * g + b

        def _mhla(xq, xk, xv, Wq, Wk, Wv, Wo, masked):
            Q = jnp.einsum('bsq,hqd->bhsd', xq, Wq)
            K = jnp.einsum('bsq,hqd->bhsd', xk, Wk)
            V = jnp.einsum('bsq,hqd->bhsd', xv, Wv)
            if masked:
                s, d = (Q.shape[-2], Q.shape[-1])
                m = jnp.where(jnp.arange(d)[None, :] <= jnp.arange(s)[:, None], 0.0, -jnp.inf)
                Q = Q + m.astype(Q.dtype)
            A = jnp.einsum('bhsd,bhse->bhde', jax.nn.softmax(K / SCALE, axis=-1), V)
            Bm = jnp.einsum('bhsd,bhde->bhse', jax.nn.softmax(Q / SCALE, axis=-1), A)
            b, h, w, dd = Bm.shape
            Bm = Bm.reshape(b, w, h * dd)
            return Bm @ Wo.T
        y = y + _mhla(y, y, y, Wq1, Wk1, Wv1, Wo1, masked=True)
        y = _ln(y, g1, b1)
        y = y + _mhla(y, mem, mem, Wq2, Wk2, Wv2, Wo2, masked=False)
        y = _ln(y, g2, b2)
        h = y @ E1.T @ D1.T
        h = h * jax.nn.sigmoid(h)
        ffn = h @ E2.T @ D2.T
        y = _ln(y + ffn, g3, b3)
        return y

    def _L3_ffn_ref(x, W_fc, ln_w, ln_b, W_proj):
        import jax, jax.numpy as jnp
        import numpy as np
        EPS = 1e-06
        LN_EPS = 1e-05

        def _absmean_core(W):
            gamma = jnp.mean(jnp.abs(W)) + EPS
            Ws = W / gamma
            Wq = jnp.sign(Ws) * jnp.minimum(jnp.round(jnp.abs(Ws)), 1.0)
            return (Wq, gamma)

        @jax.custom_vjp
        def absmean(W):
            return _absmean_core(W)[0]

        def _absmean_fwd(W):
            Wq, gamma = _absmean_core(W)
            return (Wq, gamma)

        def _absmean_bwd(gamma, g):
            return (g / gamma,)
        absmean.defvjp(_absmean_fwd, _absmean_bwd)

        def layernorm(x, w, b, eps=LN_EPS):
            mu = jnp.mean(x, axis=-1, keepdims=True)
            var = jnp.mean((x - mu) ** 2, axis=-1, keepdims=True)
            return (x - mu) * jax.lax.rsqrt(var + eps) * w + b
        h = jnp.einsum('btd,hd->bth', x, absmean(W_fc))
        h = jax.nn.gelu(h, approximate=False)
        h = layernorm(h, ln_w, ln_b)
        return jnp.einsum('bth,dh->btd', h, absmean(W_proj))
    x = x + _L0_xattn_ref(_layernorm(x, axis=-1), ctx_1024, ctx_1024, mask_1x1xSxS2_bk0, L0_xattn_Wq, L0_xattn_Wk, L0_xattn_Wv, L0_xattn_Wo, L0_xattn_bo)
    x = x + _L0_ffn_ref(_layernorm(x, axis=-1), L0_ffn_w_gate, L0_ffn_w_up, L0_ffn_w_down)
    x = x + _L1_xattn_ref(_layernorm(x, axis=-1), ctx_1024, mask_BxS2_bk0, L1_xattn_Wq, L1_xattn_bq, L1_xattn_Wkv, L1_xattn_bkv, L1_xattn_Wo, L1_xattn_bo)
    x = x + _L1_ffn_ref(_layernorm(x, axis=-1), L1_ffn_qweights, L1_ffn_scales, L1_ffn_biases, L1_ffn_lora_a, L1_ffn_lora_b, L1_ffn_ln_gamma, L1_ffn_ln_beta)
    x = x + _L2_xattn_ref(_layernorm(x, axis=-1), ctx_1024, ctx_1024, L2_xattn_Wq, L2_xattn_bq, L2_xattn_Wk, L2_xattn_bk, L2_xattn_Wv, L2_xattn_bv, L2_xattn_Wo, L2_xattn_bo, mask_BxS2_if1, 1)
    x = x + _L2_ffn_ref(_layernorm(x, axis=-1), L2_ffn_W1, L2_ffn_b1, L2_ffn_W2, L2_ffn_b2, L2_ffn_Wg1, L2_ffn_bg1, L2_ffn_Wg2, L2_ffn_bg2, L2_ffn_expert_scales, L2_ffn_expert_biases)
    x = x + _L3_xattn_ref(ctx_1024, _layernorm(x, axis=-1), L3_xattn_Wq1, L3_xattn_Wk1, L3_xattn_Wv1, L3_xattn_Wo1, L3_xattn_Wq2, L3_xattn_Wk2, L3_xattn_Wv2, L3_xattn_Wo2, L3_xattn_E1, L3_xattn_D1, L3_xattn_E2, L3_xattn_D2, L3_xattn_g1, L3_xattn_b1, L3_xattn_g2, L3_xattn_b2, L3_xattn_g3, L3_xattn_b3)
    x = x + _L3_ffn_ref(_layernorm(x, axis=-1), L3_ffn_W_fc, L3_ffn_ln_w, L3_ffn_ln_b, L3_ffn_W_proj)
    return x

_drawn_inputs = setup_inputs


def setup_inputs(seed=0):
    import zlib

    import numpy as np

    out = dict(_drawn_inputs(seed))
    spreads = {'L1_ffn_ln_gamma': (1.0, 0.2),
     'L1_ffn_ln_beta': (0.0, 0.1),
     'L2_xattn_bq': (0.0, 0.29),
     'L2_xattn_bk': (0.0, 2.0),
     'L2_xattn_bv': (0.0, 0.1),
     'L2_xattn_bo': (0.0, 0.1),
     'L3_xattn_g1': (1.0, 0.6),
     'L3_xattn_b1': (0.0, 0.8),
     'L3_xattn_g2': (1.0, 0.2),
     'L3_xattn_b2': (0.0, 0.436),
     'L3_xattn_g3': (1.0, 0.2),
     'L3_xattn_b3': (0.0, 0.4),
     'L3_ffn_ln_w': (1.0, 0.2),
     'L3_ffn_ln_b': (0.0, 0.1)}
    factors = {'L1_xattn_Wq': 17.822,
     'L1_xattn_bq': 200.0,
     'L1_xattn_bkv': 2.707,
     'L3_xattn_Wq1': 35.47,
     'L3_xattn_Wk1': 28.954,
     'L3_xattn_Wv1': 3.298,
     'L3_xattn_Wo1': 3.183,
     'L3_xattn_Wq2': 8.0,
     'L3_xattn_Wk2': 8.0,
     'L3_xattn_E1': 8.0,
     'L3_xattn_D1': 8.0,
     'L3_xattn_E2': 8.0,
     'L3_xattn_D2': 8.0}
    for name, (base, spread) in spreads.items():
        noise = np.random.default_rng([zlib.crc32(name.encode()), seed]).standard_normal(out[name].shape)
        drawn = base * np.exp(spread * noise) if base else spread * noise
        out[name] = jnp.asarray(drawn.astype(out[name].dtype))
    for name, factor in factors.items():
        out[name] = (out[name] * factor).astype(out[name].dtype)
    return out
```

```python
from contextlib import ExitStack

import concourse.bass as bass
from concourse import mybir

ALU = mybir.AluOpType
ACT = mybir.ActivationFunctionType
AX = mybir.AxisListType
F32 = mybir.dt.float32
BF16 = mybir.dt.bfloat16
I32 = mybir.dt.int32
U8 = mybir.dt.uint8
RMAX = bass.bass_isa.ReduceOp.max

P = 128
B, S, S2 = 32, 100, 1444
N = B * S
CH = 400
NC = N // CH
NPAIR = NC // 2
H, HD = 16, 8
SCALE = float(HD) ** -0.5
KT = 121
NT = (S2 + KT - 1) // KT
NP = H // 2
TERMS = 6
K_PART = [0, 0, 1, 1, 0, 2]
Q_PART = [0, 1, 0, 1, 2, 0]
R_MASK = 16 * TERMS
R_ALL = R_MASK + 7
KC = 482
NEG = -1e30
ROUND = 12582912.0


def keys_of(t):
    return min(KT, S2 - t * KT)


def keys_in_chunk(c):
    return min(KC, S2 - c * KC)


class Tally:

    def __init__(self, sem, base=0):
        self.sem, self.value = sem, base

    def inc(self, instruction):
        instruction.then_inc(self.sem, 1)
        self.value = self.value + 1

    def wait(self, engine):
        engine.wait_ge(self.sem, self.value)


class Kernel:
    def __init__(self, nc, d, out):
        self.nc, self.d, self.out = nc, d, out
        self.uid = 0
        self.used = []

    def sb(self, ctx, name, shape, dt=F32):
        self.uid += 1
        return ctx.enter_context(self.nc.sbuf_tensor(f"{name}_{self.uid}", shape, dt))

    def banks(self, ctx, name, n, dt=F32):
        self.uid += 1
        return [ctx.enter_context(self.nc.psum_tensor(f"{name}{k}_{self.uid}", [P, 512], dt)) for k in range(n)]

    def sem(self, ctx, name):
        self.uid += 1
        sem = ctx.enter_context(self.nc.semaphore(f"{name}_{self.uid}"))
        self.used.append(sem)
        return sem

    def clear_semaphores(self):
        used, self.used = self.used, []
        block = ExitStack()
        with block as c:
            b = c.enter_context(self.nc.Block())

            @b.sync
            def _(sp):
                for sem in used:
                    sp.sem_clear(sem)

    def load_all(self, ctx):
        nc, d = self.nc, self.d
        self.xT = self.sb(ctx, "xT", [P, N])
        self.yT = self.sb(ctx, "yT", [P, N])
        self.ident = self.sb(ctx, "ident", [P, P])
        self.mean = self.sb(ctx, "mean", [P, P])
        self.eps = self.sb(ctx, "eps", [P, 1])
        with ExitStack() as c:
            loaded = self.sem(c, "loaded")
            block = c.enter_context(nc.Block())

            @block.sync
            def _(sp):
                sp.dma_start(self.xT[:, :], d["xT"]).then_inc(loaded, 16)
                sp.dma_start(self.ident[:, :], d["ident"]).then_inc(loaded, 16)
                sp.wait_ge(loaded, 32)

            @block.vector
            def _(dve):
                dve.memset(self.mean[:, :], 1.0 / P)
                dve.memset(self.eps[:, :], 1e-5)

    def store_out(self):
        nc = self.nc
        with ExitStack() as c:
            stored = self.sem(c, "stored")
            block = c.enter_context(nc.Block())

            @block.sync
            def _(sp):
                sp.dma_start(self.out, self.xT[:, :]).then_inc(stored, 16)
                sp.wait_ge(stored, 16)

    def layernorm(self, src, dst, tiles=1, mean=None, gamma=None, beta=None):
        nc = self.nc
        mean = mean or self.mean
        with ExitStack() as c:
            mu = self.banks(c, "mu", 2)
            var = self.banks(c, "var", 2)
            sq = [self.sb(c, "sq", [P, tiles, CH]) for _ in range(2)]
            sd = [self.sb(c, "sd", [P, CH]) for _ in range(2)]
            rs = [self.sb(c, "rs", [P, CH]) for _ in range(2)]
            mean_ready, centered, squared, var_ready, sd_ready, scaled = (
                self.sem(c, n) for n in ("mean_ready", "centered", "squared", "var_ready", "sd_ready", "scaled"))
            block = c.enter_context(nc.Block())

            def chunk(a, i, u):
                return a[:, :, bass.ds(i * (2 * CH) + u * CH, CH)]

            @block.tensor
            def _(pe):
                with pe.Fori(0, NPAIR) as i:
                    for u in range(2):
                        x = chunk(src, i, u)
                        for t in range(tiles):
                            ins = pe.matmul(mu[u][:, 0:CH], mean[:, :], x[:, t, :], start=t == 0, stop=t == tiles - 1)
                        ins.then_inc(mean_ready, 1)
                    for u in range(2):
                        pe.wait_ge(squared, 2 * i + (u + 1))
                        for t in range(tiles):
                            ins = pe.matmul(var[u][:, 0:CH], mean[:, :], sq[u][:, t, :], start=t == 0, stop=t == tiles - 1)
                        ins.then_inc(var_ready, 1)

            @block.scalar
            def _(act):
                with act.Fori(0, NPAIR) as i:
                    for u in range(2):
                        act.wait_ge(centered, 2 * i + (u + 1))
                        act.activation(sq[u][:, :, :], chunk(dst, i, u), ACT.Square).then_inc(squared, 1)
                    for u in range(2):
                        act.wait_ge(var_ready, 2 * i + (u + 1))
                        act.activation(sd[u][:, :], var[u][:, 0:CH], ACT.Sqrt, bias=self.eps[:, 0:1]).then_inc(sd_ready, 1)

            per = 2 if gamma is None else 2 + tiles

            @block.vector
            def _(dve):
                with dve.Fori(0, NPAIR) as i:
                    for u in range(2):
                        dve.wait_ge(mean_ready, 2 * i + (u + 1))
                        dve.tensor_tensor(chunk(dst, i, u), chunk(src, i, u),
                                          mu[u][:, 0:CH].unsqueeze(1).to_broadcast([P, tiles, CH]),
                                          ALU.subtract).then_inc(centered, 1)
                    for u in range(2):
                        done = Tally(scaled, i * (2 * per) + u * per)
                        y = chunk(dst, i, u)
                        dve.wait_ge(sd_ready, 2 * i + (u + 1))
                        done.inc(dve.reciprocal(rs[u][:, :], sd[u][:, :]))
                        done.wait(dve)
                        done.inc(dve.tensor_tensor(y, y, rs[u][:, :].unsqueeze(1).to_broadcast([P, tiles, CH]), ALU.mult))
                        if gamma is not None:
                            done.wait(dve)
                            for t in range(tiles):
                                done.inc(dve.tensor_scalar(y[:, t, :], y[:, t, :], gamma[:, t:t + 1], beta[:, t:t + 1],
                                                           ALU.mult, ALU.add))

    def linear(self, src, w, dst, bias=None, func=ACT.Identity, add=None, gate=False, rows=P):
        nc = self.nc
        kt, mt = src.shape[1], dst.shape[1]
        with ExitStack() as c:
            ps = self.banks(c, "lin", 4)
            product, moved = self.sem(c, "product"), self.sem(c, "moved")
            block = c.enter_context(nc.Block())
            n = 2 * mt

            @block.tensor
            def _(pe):
                pe.sem_inc(moved, 4)
                with pe.Fori(0, NPAIR) as i:
                    for k in range(n):
                        u, m = divmod(k, mt)
                        bank = ps[k % 4] if n % 4 == 0 else ps[k % 2]
                        ahead = 4 if n % 4 == 0 else 2
                        pe.wait_ge(moved, n * i + (k + 1 + 4 - ahead))
                        x = src[:, :, bass.ds(i * (2 * CH) + u * CH, CH)]
                        for t in range(kt):
                            ins = pe.matmul(bank[:, 0:CH], w[:, t, m * P:(m + 1) * P], x[:, t, :],
                                            start=t == 0, stop=t == kt - 1)
                        ins.then_inc(product, 1)

            def takes(eng, put):
                with eng.Fori(0, NPAIR) as i:
                    for k in range(n):
                        u, m = divmod(k, mt)
                        bank = ps[k % 4] if n % 4 == 0 else ps[k % 2]
                        eng.wait_ge(product, n * i + (k + 1))
                        put(dst[:, m, bass.ds(i * (2 * CH) + u * CH, CH)], bank[:, 0:CH], m, i, u).then_inc(moved, 1)

            if add is None:
                @block.scalar
                def _(act):
                    takes(act, lambda y, x, m, i, u: act.activation(
                        y, x, func, bias=0.0 if bias is None else bias[:, m:m + 1]))
            else:
                @block.vector
                def _(dve):
                    def put(y, x, m, i, u):
                        a = add[:, m, bass.ds(i * (2 * CH) + u * CH, CH)]
                        if bias is None:
                            return dve.tensor_tensor(y, a, x, ALU.add)
                        return dve.scalar_tensor_tensor(y, x, bias[:, m:m + 1], a, ALU.add, ALU.add)
                    takes(dve, put)

    def loads(self, pairs):
        nc = self.nc
        with ExitStack() as c:
            loaded = self.sem(c, "weights")
            block = c.enter_context(nc.Block())

            @block.sync
            def _(sp):
                for t, s in pairs:
                    sp.dma_start(t, s).then_inc(loaded, 16)
                sp.wait_ge(loaded, 16 * len(pairs))

    def split_queries(self, w, bias, parts):
        nc = self.nc
        with ExitStack() as c:
            ps = self.banks(c, "qps", 2)
            q = [self.sb(c, "q", [P, CH]) for _ in range(2)]
            r = [self.sb(c, "r", [P, CH]) for _ in range(2)]
            product, split = self.sem(c, "q_product"), self.sem(c, "q_split")
            per = 6 if bias is not None else 5
            block = c.enter_context(nc.Block())

            @block.tensor
            def _(pe):
                pe.sem_inc(split, 2 * per)
                with pe.Fori(0, NPAIR) as i:
                    for u in range(2):
                        pe.wait_ge(split, 2 * per * i + per * (u + 1))
                        pe.matmul(ps[u][:, 0:CH], w[:, :], self.yT[:, bass.ds(i * (2 * CH) + u * CH, CH)],
                                  start=True, stop=True).then_inc(product, 1)

            @block.vector
            def _(dve):
                with dve.Fori(0, NPAIR) as i:
                    for u in range(2):
                        done = Tally(split, 2 * per * i + (2 * per + per * u))
                        p1, p2, p3 = (p[:, bass.ds(i * (2 * CH) + u * CH, CH)] for p in parts)
                        dve.wait_ge(product, 2 * i + (u + 1))
                        if bias is None:
                            done.inc(dve.tensor_scalar(q[u][:, :], ps[u][:, 0:CH], SCALE, None, ALU.mult))
                        else:
                            done.inc(dve.tensor_scalar(q[u][:, :], ps[u][:, 0:CH], bias[:, 0:1], None, ALU.add))
                            done.wait(dve)
                            done.inc(dve.tensor_scalar(q[u][:, :], q[u][:, :], SCALE, None, ALU.mult))
                        done.wait(dve)
                        done.inc(dve.tensor_copy(p1, q[u][:, :]))
                        done.wait(dve)
                        done.inc(dve.tensor_tensor(r[u][:, :], q[u][:, :], p1, ALU.subtract))
                        done.wait(dve)
                        done.inc(dve.tensor_copy(p2, r[u][:, :]))
                        done.wait(dve)
                        done.inc(dve.tensor_tensor(p3, r[u][:, :], p2, ALU.subtract))

    def long_attention(self, wq, wk, wv, wo, bo, bq=None, bk=None, bv=None, wo_full=None, query_mask=None, key_mask=None):
        nc, d = self.nc, self.d
        with ExitStack() as c:
            sb = lambda name, shape, dt=F32: self.sb(c, name, shape, dt)
            wq_t, wk_t, wv_t = sb("wq", [P, P]), sb("wk", [P, P]), sb("wv", [P, P])
            wo_t = sb("wo", [P, 4, P])
            den_sel = sb("den_sel", [P, P])
            bo_t = sb("bo", [P, 1])
            q_parts = [sb(f"q{k}_", [P, N], BF16) for k in range(3)]
            pairs = [(wq_t[:, :], wq), (wk_t[:, :], wk), (wv_t[:, :], wv), (wo_t[:, :, :], wo.rearrange("s p o -> p s o")),
                     (den_sel[:, :], d["den_sel"]), (bo_t[:, :], bo)]
            bq_t = bk_t = None
            if bq is not None:
                bq_t, bk_t = sb("bq", [P, 1]), sb("bk", [P, 1])
                bv_t, wo_full_t = sb("bv", [P, 1]), sb("wo_full", [P, P])
                pairs += [(bq_t[:, :], bq), (bk_t[:, :], bk), (bv_t[:, :], bv), (wo_full_t[:, :], wo_full)]
            self.loads(pairs)
            if bq is not None:
                self.fold_bias(bo_t[:, :], wo_full_t[:, :], bv_t[:, :], bo_t[:, :])
            self.split_queries(wq_t, bq_t, q_parts)
            self.long_attention_loop(wk_t, wv_t, wo_t, den_sel, bo_t, bk_t, q_parts, query_mask, key_mask)

    def long_attention_loop(self, wk, wv, wo, den_sel, bo, bk, q_parts, query_mask, key_mask):
        nc, d, xT = self.nc, self.d, self.xT
        with ExitStack() as c:
            sb = lambda name, shape, dt=F32: self.sb(c, name, shape, dt)
            ctx = [sb(f"ctx{v}", [P, S2]) for v in range(2)]
            k_parts = [sb(f"k{k}_", [P, S2], BF16) for k in range(3)]
            k_rest = sb("k_rest", [P, S2])
            k_pack = [sb(f"k_pack{v}", [R_ALL, NP, S2], BF16) for v in range(2)]
            q_blk = [sb(f"q_blk{v}", [R_ALL, NP, 2, S], BF16) for v in range(2)]
            v_ext = [sb(f"v_ext{v}", [KT, NT, H, HD + 1]) for v in range(2)]
            probs = sb("probs", [KT, 4, NP * S])
            row_max3 = sb("row_max3", [S, 2, NP, 3])
            neg_max = sb("neg_max", [S, 2, NP])
            max_rest = sb("max_rest", [S, 2, NP])
            max_parts = sb("max_parts", [S, 2, 3, NP], BF16)
            max_rows = sb("max_rows", [2 * 3 * NP, S], BF16)
            ident_b = sb("ident_b", [S, 4, S], BF16)
            acc_sb = sb("acc_sb", [P, 4 * S])
            den_inv = sb("den_inv", [P, 4 * S])
            heads_out = sb("heads_out", [P, 4, S])
            score2 = [c.enter_context(nc.psum_tensor(f"score2_{self.uid}_{g}", [P, 2, 512], F32))
                      for g in range(2)]
            score1 = self.banks(c, "score1_", 2)
            acc = self.banks(c, "acc", 1)[0]
            misc = self.banks(c, "misc", 1)[0]
            if query_mask is not None:
                qm_u8 = sb("qm_u8", [S, S2], U8)
                qm_bias = sb("qm_bias", [S, S2], BF16)
            if key_mask is not None:
                km_u8 = sb("km_u8", [B, S2], U8)
                km_bias = sb("km_bias", [B, S2], BF16)
                km_dram = nc.dram_tensor("key_mask_bias", [B, S2], BF16, kind="Internal").ap()

            rows_set, mask_made = self.sem(c, "rows_set"), self.sem(c, "mask_made")
            with ExitStack() as c2:
                mask_in, mask_out = self.sem(c2, "mask_in"), self.sem(c2, "mask_out")
                block = c2.enter_context(nc.Block())

                @block.sync
                def _(sp):
                    if query_mask is not None:
                        sp.dma_start(qm_u8[:, :], query_mask).then_inc(mask_in, 16)
                        sp.wait_ge(mask_in, 16)
                    if key_mask is not None:
                        sp.dma_start(km_u8[:, :], key_mask).then_inc(mask_in, 16)
                        sp.wait_ge(mask_made, 1)
                        sp.dma_start(km_dram, km_bias[:, :]).then_inc(mask_out, 16)
                        sp.wait_ge(mask_out, 16)

                @block.gpsimd
                def _(pool):
                    done = Tally(rows_set)
                    for v in range(2):
                        for tile, value in ((k_pack[v][R_MASK:R_ALL, :, :], 1.0), (k_pack[v][R_MASK:R_MASK + 1, :, :], 0.0),
                                            (q_blk[v][:, :, :, :], 0.0), (q_blk[v][R_MASK:R_MASK + 1, :, :, :], 1.0),
                                            (v_ext[v][:, :, :, :], 1.0)):
                            done.inc(pool.memset(tile, value))
                            done.wait(pool)

                @block.vector
                def _(dve):
                    dve.memset(acc[:, :], 0.0)
                    for k in range(4):
                        dve.tensor_copy(ident_b[:, k, :], self.ident[0:S, 0:S])
                    if query_mask is not None:
                        dve.wait_ge(mask_in, 16)
                        dve.tensor_scalar(qm_bias[:, :], qm_u8[:, :], -1.0, -NEG, ALU.add, ALU.mult).then_inc(mask_made, 1)
                    if key_mask is not None:
                        dve.wait_ge(mask_in, 16)
                        dve.tensor_scalar(km_bias[:, :], km_u8[:, :], NEG, None, ALU.mult).then_inc(mask_made, 1)

            ctx_in = [self.sem(c, f"ctx_in{v}") for v in range(2)]
            packed = [self.sem(c, f"packed{v}") for v in range(2)]
            max_in = [self.sem(c, f"max_in{v}") for v in range(2)]
            (k_ready, k1_made, k2_made, r1_made, k_split, v_ready, v_made, score1_ready, score1_used, chain, maxed,
             max_turned, max_rows_made, scored, exps, avs, acc_out, den_ready, den_made, heads_made, out_ready,
             added, seen, pool_seen) = (self.sem(c, n) for n in (
                "k_ready", "k1_made", "k2_made", "r1_made", "k_split", "v_ready", "v_made", "score1_ready",
                "score1_used", "chain", "maxed", "max_turned", "max_rows_made", "scored", "exps", "avs", "acc_out",
                "den_ready", "den_made", "heads_made", "out_ready", "added", "seen", "pool_seen"))
            n_pack = 16 * (TERMS * 3 + (key_mask is not None))
            NQ = 3 * 2 * NP
            CHAIN = 5

            block = c.enter_context(nc.Block())

            def following(i, u):
                return (2 * i + u + 1, 1 - u, i + u)

            @block.sync
            def _(sp):
                def load_ctx(n, v):
                    sp.dma_start(ctx[v][:, :], d["ctxT"][:, bass.ds(n * S2, S2)]).then_inc(ctx_in[v], 16)

                def pack_q(n, v):
                    for s in range(TERMS):
                        for a in range(2):
                            sp.dma_start(q_blk[v][16 * s + 8 * a:16 * s + 8 * a + 8, :, a, :],
                                         q_parts[Q_PART[s]][64 * a:64 * a + 64, bass.ds(n * S, S)]).then_inc(packed[v], 16)

                def pack_k(n, v):
                    sp.wait_ge(k_split, 3 * n + 3)
                    for s in range(TERMS):
                        sp.dma_start(k_pack[v][16 * s:16 * s + 16, :, :], k_parts[K_PART[s]][:, :]).then_inc(packed[v], 16)
                    if key_mask is not None:
                        sp.dma_start(k_pack[v][R_MASK:R_MASK + 1, :, :],
                                     km_dram[bass.ds(n, 1), :].unsqueeze(1).to_broadcast([1, NP, S2])).then_inc(packed[v], 16)

                def max_to_rows(n, v):
                    sp.wait_ge(max_rows_made, n + 1)
                    for a in range(2):
                        sp.dma_start(q_blk[v][R_MASK + 1 + 3 * a:R_MASK + 4 + 3 * a, :, a, :],
                                     max_rows[24 * a:24 * a + 24, :]).then_inc(max_in[v], 16)

                def turn(i, u, ahead=2):
                    n, v, _ = following(i, u)
                    if ahead >= 1:
                        sp.wait_ge(scored, 24 * (n - 1) + 1)
                        pack_q(n, v)
                    if ahead >= 2:
                        sp.wait_ge(v_ready, 3 * n)
                        load_ctx(n + 1, 1 - v)
                    if ahead >= 1:
                        pack_k(n, v)
                        max_to_rows(n, v)

                load_ctx(0, 0)
                load_ctx(1, 1)
                pack_q(0, 0)
                pack_k(0, 0)
                max_to_rows(0, 0)
                with sp.Fori(0, B // 2 - 1) as i:
                    turn(i, 0)
                    turn(i, 1)
                turn(B // 2 - 1, 0, ahead=1)

            @block.tensor
            def _(pe):
                def k_chunk(n, v, m, c_):
                    if c_ == 0:
                        pe.wait_ge(ctx_in[v], 16 * m + 16)
                        if not isinstance(n, int) or n > 0:
                            pe.wait_ge(added, n)
                            pe.wait_ge(max_rows_made, n)
                    else:
                        pe.wait_ge(r1_made, 3 * n + c_)
                    w = keys_in_chunk(c_)
                    pe.matmul(misc[:, 0:w], wk[:, :], ctx[v][:, c_ * KC:c_ * KC + w], start=True, stop=True).then_inc(k_ready, 1)

                def v_tiles(n, v, g):
                    if g == 0:
                        pe.wait_ge(r1_made, 3 * n + 3)
                    else:
                        pe.wait_ge(v_made, 3 * n + g)
                    for t in range(4 * g, 4 * g + 4):
                        w = keys_of(t)
                        ins = pe.matmul(misc[0:w, (t % 4) * P:(t % 4 + 1) * P], ctx[v][:, t * KT:t * KT + w], wv[:, :],
                                        start=True, stop=True)
                    ins.then_inc(v_ready, 1)

                def first_product(n, v, m, qs):
                    for q in qs:
                        if q == 0:
                            pe.wait_ge(packed[v], n_pack * m + n_pack)
                        if not isinstance(n, int) or NQ * n + q - 1 > 0:
                            pe.wait_ge(score1_used, NQ * n + (q - 1))
                        h, c_ = divmod(q, 3)
                        w = keys_in_chunk(c_)
                        pe.matmul(score1[q % 2][0:S, 0:w], q_blk[v][0:R_MASK + 1, h // 2, h % 2, :],
                                  k_pack[v][0:R_MASK + 1, h // 2, c_ * KC:c_ * KC + w], start=True, stop=True)\
                            .then_inc(score1_ready, 1)

                def max_transpose(n):
                    pe.wait_ge(v_made, 3 * n + 3)
                    pe.wait_ge(maxed, n + 1)
                    pe.matmul(misc[0:6 * NP, 0:S], max_parts[:, :, :, :].rearrange("q a i p -> q (a i p)"),
                              ident_b[:, 0, :], start=True, stop=True).then_inc(max_turned, 1)

                def second_product(b, u, m, t):
                    w = keys_of(t)
                    if t == 0:
                        pe.wait_ge(max_in[u], 32 * m + 32)
                    for g in range(2):
                        pe.wait_ge(exps, 24 * b + (2 * t + g + 1))
                        for k in range(2):
                            bank = score2[g][:, k, :]
                            for pp in range(2):
                                p = 4 * g + 2 * k + pp
                                ins = pe.matmul(bank[0:w, 2 * S * pp:2 * S * (pp + 1)],
                                                k_pack[u][:, p, t * KT:t * KT + w],
                                                q_blk[u][:, p, :, :].rearrange("r a q -> r (a q)"),
                                                start=pp == 0, stop=query_mask is None and pp == 1, skip_group_check=True)
                            if query_mask is not None:
                                ins = pe.matmul(bank[0:w, 0:4 * S], qm_bias[:, t * KT:t * KT + w],
                                                ident_b[:, :, :].rearrange("q k c -> q (k c)"),
                                                start=False, stop=True, skip_group_check=True)
                        ins.then_inc(scored, 1)

                def weighted_values(b, u, t):
                    w = keys_of(t)
                    if t == 0:
                        pe.wait_ge(acc_out, b + 1)
                    pe.wait_ge(exps, 24 * b + (2 * t + 4))
                    for s in range(4):
                        for g in range(4):
                            h = 4 * s + g
                            ins = pe.matmul(acc[32 * g:32 * g + HD + 1, S * s:S * s + S], v_ext[u][0:w, t, h, :],
                                            probs[0:w, 2 * (t % 2) + h // 8, (h % 8) * S:(h % 8 + 1) * S],
                                            start=t == 0 and s == 0, stop=t == NT - 1 and s == 3, skip_group_check=True)
                    ins.then_inc(avs, 1)

                def denominators(b, ahead):
                    if ahead:
                        pe.wait_ge(max_rows_made, b + 2)
                    else:
                        pe.wait_ge(added, b + 1)
                    pe.wait_ge(acc_out, b + 2)
                    pe.matmul(misc[:, 0:4 * S], den_sel[:, :], acc_sb[:, :], start=True, stop=True).then_inc(den_ready, 1)

                def output(b):
                    pe.wait_ge(heads_made, b + 2)
                    for s in range(4):
                        ins = pe.matmul(misc[:, 0:S], wo[:, s, :], heads_out[:, s, :], start=s == 0, stop=s == 3)
                    ins.then_inc(out_ready, 1)

                def turn(i, u, ahead=True):
                    b = 2 * i + u
                    n, v, m = following(i, u)
                    q = 0
                    for t in range(NT):
                        if ahead and t < 3:
                            k_chunk(n, v, m, t)
                        second_product(b, u, i, t)
                        if ahead and 3 <= t < 6:
                            v_tiles(n, v, t - 3)
                        if t:
                            weighted_values(b, u, t - 1)
                        if ahead and 5 <= t < 11:
                            first_product(n, v, m, range(8 * (t - 5), 8 * (t - 4)))
                    weighted_values(b, u, NT - 1)
                    if ahead:
                        max_transpose(n)
                    denominators(b, ahead)
                    output(b)

                pe.sem_inc(exps, 2)
                pe.sem_inc(avs, 2)
                pe.sem_inc(acc_out, 1)
                pe.sem_inc(scored, 1)
                pe.sem_inc(added, 1)
                pe.sem_inc(heads_made, 1)
                for k in range(3):
                    k_chunk(0, 0, 0, k)
                for k in range(3):
                    v_tiles(0, 0, k)
                first_product(0, 0, 0, range(NQ))
                max_transpose(0)
                with pe.Fori(0, B // 2 - 1) as i:
                    turn(i, 0)
                    turn(i, 1)
                turn(B // 2 - 1, 0)
                turn(B // 2 - 1, 1, ahead=False)

            @block.scalar
            def _(act):
                def k1(n, c_):
                    w = keys_in_chunk(c_)
                    act.wait_ge(k_ready, 3 * n + (c_ + 1))
                    act.activation(k_parts[0][:, c_ * KC:c_ * KC + w], misc[:, 0:w], ACT.Identity,
                                   bias=0.0 if bk is None else bk[:, 0:1]).then_inc(k1_made, 1)

                def v_out(n, v, g):
                    act.wait_ge(v_ready, 3 * n + (g + 1))
                    if g < 2:
                        act.activation(v_ext[v][:, 4 * g:4 * g + 4, :, 0:HD],
                                       misc[0:KT, :].rearrange("p (t h d) -> p t h d", t=4, h=H), ACT.Copy).then_inc(v_made, 1)
                    else:
                        act.activation(v_ext[v][:, 8:11, :, 0:HD],
                                       misc[0:KT, 0:3 * P].rearrange("p (t h d) -> p t h d", t=3, h=H), ACT.Copy)
                        w = keys_of(NT - 1)
                        act.activation(v_ext[v][0:w, 11, :, 0:HD],
                                       misc[0:w, 3 * P:4 * P].rearrange("p (h d) -> p h d", h=H), ACT.Copy).then_inc(v_made, 1)

                def exp_tile(b, t):
                    w = keys_of(t)
                    act.wait_ge(avs, 12 * b + (t + 1))
                    for g in range(2):
                        act.wait_ge(scored, 24 * b + (2 * t + g + 2))
                        src = score2[g][0:w, :, 0:4 * S]
                        act.activation(probs[0:w, 2 * (t % 2) + g, :].rearrange("p (k c) -> p k c", k=2), src, ACT.Exp)\
                            .then_inc(exps, 1)

                def sums_out(b):
                    act.wait_ge(avs, 12 * b + 14)
                    act.wait_ge(heads_made, b + 1)
                    act.activation(acc_sb[:, :], acc[:, 0:4 * S], ACT.Copy).then_inc(acc_out, 1)

                def turn(i, u, ahead=True):
                    b = 2 * i + u
                    n, v, m = following(i, u)
                    for t in range(NT):
                        if ahead and t < 3:
                            if t == 0:
                                act.wait_ge(packed[u], n_pack * i + n_pack)
                            k1(n, t)
                        exp_tile(b, t)
                        if ahead and 3 <= t < 6:
                            v_out(n, v, t - 3)
                    sums_out(b)

                for k in range(3):
                    k1(0, k)
                for k in range(3):
                    v_out(0, 0, k)
                with act.Fori(0, B // 2 - 1) as i:
                    turn(i, 0)
                    turn(i, 1)
                turn(B // 2 - 1, 0)
                turn(B // 2 - 1, 1, ahead=False)

            @block.gpsimd
            def _(pool):
                def split(n, c_):
                    w = keys_in_chunk(c_)
                    k2, k3, r = (x[:, c_ * KC:c_ * KC + w] for x in (k_parts[1], k_parts[2], k_rest))
                    pool.wait_ge(r1_made, 3 * n + (c_ + 1))
                    pool.sem_inc(pool_seen, 1)
                    pool.tensor_scalar(k2, r, 1.0, 0.0, ALU.mult, ALU.add).then_inc(k2_made, 1)
                    pool.wait_ge(k2_made, 3 * n + (c_ + 1))
                    pool.tensor_tensor(k3, r, k2, ALU.subtract).then_inc(k_split, 1)

                def turn(i, u):
                    n = 2 * i + u + 1
                    pool.wait_ge(packed[u], n_pack * i + n_pack)
                    for k in range(3):
                        split(n, k)

                for k in range(3):
                    split(0, k)
                with pool.Fori(0, B // 2 - 1) as i:
                    turn(i, 0)
                    turn(i, 1)
                turn(B // 2 - 1, 0)

            @block.vector
            def _(dve):
                def r1(n, c_):
                    w = keys_in_chunk(c_)
                    if not isinstance(n, int) or n > 0:
                        dve.wait_ge(k_split, 3 * n)
                    dve.wait_ge(k1_made, 3 * n + (c_ + 1))
                    out, k1_ = k_rest[:, c_ * KC:c_ * KC + w], k_parts[0][:, c_ * KC:c_ * KC + w]
                    if bk is None:
                        ins = dve.tensor_tensor(out, misc[:, 0:w], k1_, ALU.subtract)
                    else:
                        ins = dve.scalar_tensor_tensor(out, misc[:, 0:w], bk[:, 0:1], k1_, ALU.add, ALU.subtract)
                    ins.then_inc(r1_made, 1)

                def chunk_max(n, q):
                    h, c_ = divmod(q, 3)
                    w = keys_in_chunk(c_)
                    dve.wait_ge(score1_ready, NQ * n + (q + 1))
                    to = row_max3[:, h % 2, h // 2, c_:c_ + 1]
                    if query_mask is not None:
                        dve.sem_inc(seen, 1)
                        ins = dve.tensor_tensor_reduce(score1[q % 2][0:S, 0:w], score1[q % 2][0:S, 0:w], qm_bias[:, c_ * KC:c_ * KC + w],
                                                       1.0, -3e38, ALU.add, ALU.max, to)
                    else:
                        ins = dve.tensor_reduce(to, score1[q % 2][0:S, 0:w], AX.X, ALU.max)
                    ins.then_inc(score1_used, 1)

                def max_chain(n):
                    done = Tally(chain, CHAIN * n)
                    dve.wait_ge(score1_used, NQ * n + NQ)
                    done.inc(dve.tensor_reduce(neg_max[:, :, :], row_max3[:, :, :, :], AX.X, ALU.max, negate=True))
                    done.wait(dve)
                    done.inc(dve.tensor_scalar(neg_max[:, :, :], neg_max[:, :, :], 1e20, None, ALU.min))
                    done.wait(dve)
                    done.inc(dve.tensor_copy(max_parts[:, :, 0, :], neg_max[:, :, :]))
                    done.wait(dve)
                    done.inc(dve.tensor_tensor(max_rest[:, :, :], neg_max[:, :, :], max_parts[:, :, 0, :], ALU.subtract))
                    done.wait(dve)
                    done.inc(dve.tensor_copy(max_parts[:, :, 1, :], max_rest[:, :, :]))
                    done.wait(dve)
                    dve.tensor_tensor(max_parts[:, :, 2, :], max_rest[:, :, :], max_parts[:, :, 1, :], ALU.subtract)\
                        .then_inc(maxed, 1)
                    dve.wait_ge(max_turned, n + 1)
                    dve.tensor_copy(max_rows[:, :], misc[0:6 * NP, 0:S]).then_inc(max_rows_made, 1)

                def divide(b):
                    dve.wait_ge(den_ready, b + 1)
                    dve.reciprocal(den_inv[:, :], misc[:, 0:4 * S]).then_inc(den_made, 1)
                    dve.wait_ge(den_made, b + 1)
                    dve.tensor_tensor(heads_out[:, :, :].rearrange("p s q -> p (s q)"), acc_sb[:, :], den_inv[:, :], ALU.mult)\
                        .then_inc(heads_made, 1)

                def add_output(b):
                    dve.wait_ge(out_ready, b + 1)
                    x = xT[:, bass.ds(b * S, S)]
                    dve.scalar_tensor_tensor(x, misc[:, 0:S], bo[:, 0:1], x, ALU.add, ALU.add).then_inc(added, 1)

                def turn(i, u, ahead=True):
                    b = 2 * i + u
                    n = b + 1
                    if ahead:
                        for k in range(3):
                            r1(n, k)
                        for q in range(NQ):
                            chunk_max(n, q)
                        max_chain(n)
                    divide(b)
                    add_output(b)

                for k in range(3):
                    r1(0, k)
                for q in range(NQ):
                    chunk_max(0, q)
                max_chain(0)
                with dve.Fori(0, B // 2 - 1) as i:
                    turn(i, 0)
                    turn(i, 1)
                turn(B // 2 - 1, 0)
                turn(B // 2 - 1, 1, ahead=False)


    def on_vector(self, steps):
        with ExitStack() as c:
            stepped = self.sem(c, "stepped")
            block = c.enter_context(self.nc.Block())

            @block.vector
            def _(dve):
                done = Tally(stepped)
                for step in steps:
                    done.inc(step(dve))
                    done.wait(dve)

    def on_scalar(self, dst, src, func):
        with ExitStack() as c:
            block = c.enter_context(self.nc.Block())

            @block.scalar
            def _(act):
                act.activation(dst, src, func)

    def global_scale(self, x, part, whole, scale, inv, op, reduce, finish):
        with ExitStack() as c:
            reduced, joined, stepped = (self.sem(c, n) for n in ("reduced", "joined", "stepped"))
            block = c.enter_context(self.nc.Block())

            @block.vector
            def _(dve):
                dve.tensor_reduce(part, x, AX.X, op, apply_absolute_value=True).then_inc(reduced, 1)
                dve.wait_ge(joined, 1)
                done = Tally(stepped)
                done.inc(finish(dve, scale, whole))
                done.wait(dve)
                done.inc(dve.reciprocal(inv, scale))

            @block.gpsimd
            def _(pool):
                pool.wait_ge(reduced, 1)
                pool.partition_all_reduce(whole, part, P, reduce).then_inc(joined, 1)

    def act_qdq(self, c, x):
        part, whole, scale, inv = (self.sb(c, n, [P, 1])[:, :] for n in ("part", "whole", "scale", "inv"))
        self.global_scale(x, part, whole, scale, inv, ALU.max, RMAX,
                          lambda dve, s, w: dve.tensor_scalar(s, w, 1.0 / 32767.0, 1e-12, ALU.mult, ALU.max))
        self.on_vector([
            lambda dve: dve.tensor_scalar(x, x, inv, ROUND, ALU.mult, ALU.add),
            lambda dve: dve.tensor_scalar(x, x, ROUND, 32767.0, ALU.subtract, ALU.min),
            lambda dve: dve.tensor_scalar(x, x, -32768.0, scale, ALU.max, ALU.mult)])

    def turn_weights(self, jobs):
        with ExitStack() as c:
            ps = self.banks(c, "turn", 2)
            turned, moved = self.sem(c, "turned"), self.sem(c, "moved")
            block = c.enter_context(self.nc.Block())

            @block.tensor
            def _(pe):
                for n, (out, pairs) in enumerate(jobs):
                    rows, cols = out.shape
                    if n >= 2:
                        pe.wait_ge(moved, n - 1)
                    for k, (a, b) in enumerate(pairs):
                        ins = pe.matmul(ps[n % 2][0:rows, 0:cols], a, b, start=k == 0, stop=k == len(pairs) - 1)
                    ins.then_inc(turned, 1)

            @block.scalar
            def _(act):
                for n, (out, pairs) in enumerate(jobs):
                    rows, cols = out.shape
                    act.wait_ge(turned, n + 1)
                    act.activation(out, ps[n % 2][0:rows, 0:cols], ACT.Copy).then_inc(moved, 1)

    def fold_bias(self, total, w, b, bias):
        with ExitStack() as c:
            ps = self.banks(c, "fold", 1)[0]
            product = self.sem(c, "product")
            block = c.enter_context(self.nc.Block())

            @block.tensor
            def _(pe):
                pe.matmul(ps[:, 0:1], w, b, start=True, stop=True).then_inc(product, 1)

            @block.vector
            def _(dve):
                dve.wait_ge(product, 1)
                dve.tensor_tensor(total, bias, ps[:, 0:1], ALU.add)

    def ffn0(self, x3, y3):
        d = self.d
        with ExitStack() as c:
            sb = lambda name, shape, dt=F32: self.sb(c, name, shape, dt)
            F = 3
            up_t, gate_t, down_t = sb("up_t", [P, 1, F * P]), sb("gate_t", [P, 1, F * P]), sb("down_t", [P, F, P])
            with ExitStack() as c2:
                nat = self.sb(c2, "nat", [P, 3, F * P])
                step, inv = self.sb(c2, "step", [P, 36]), self.sb(c2, "inv", [P, 36])
                tiles = lambda w: w.rearrange("(t o) i -> o t i", o=P)
                split = lambda x: x.rearrange("o (t i) -> o t i", t=F)
                self.loads([(split(nat[:, 0, :]), tiles(d["w_up"])), (split(nat[:, 1, :]), tiles(d["w_gate"])),
                            (nat[:, 2, :], d["w_down"])])
                w = nat[:, :, :].rearrange("o k (n e) -> o (k n) e", e=32)
                wide = lambda x: x[:, :].unsqueeze(2).to_broadcast([P, 36, 32])
                self.on_vector([
                    lambda dve: dve.tensor_reduce(step[:, :], w, AX.X, ALU.max, apply_absolute_value=True),
                    lambda dve: dve.tensor_scalar(step[:, :], step[:, :], 1.0 / 7.0, 1e-12, ALU.mult, ALU.max),
                    lambda dve: dve.reciprocal(inv[:, :], step[:, :]),
                    lambda dve: dve.tensor_tensor(w, w, wide(inv), ALU.mult),
                    lambda dve: dve.tensor_scalar(w, w, ROUND, ROUND, ALU.add, ALU.subtract),
                    lambda dve: dve.tensor_scalar(w, w, -8.0, 7.0, ALU.max, ALU.min),
                    lambda dve: dve.tensor_tensor(w, w, wide(step), ALU.mult)])
                i_ = self.ident[:, :]
                self.turn_weights(
                    [(up_t[:, 0, t * P:(t + 1) * P], [(nat[:, 0, t * P:(t + 1) * P], i_)]) for t in range(F)]
                    + [(gate_t[:, 0, t * P:(t + 1) * P], [(nat[:, 1, t * P:(t + 1) * P], i_)]) for t in range(F)]
                    + [(down_t[:, t, :], [(nat[:, 2, t * P:(t + 1) * P], i_)]) for t in range(F)])
            self.layernorm(x3, y3)
            self.act_qdq(c, self.yT[:, :])
            up, gate = sb("up", [P, F, N]), sb("gate", [P, F, N])
            sig = sb("sig", [P, F, N])
            flat = lambda x: x[:, :, :].rearrange("p f n -> p (f n)")
            self.linear(y3, up_t, up)
            self.linear(y3, gate_t, gate)
            self.act_qdq(c, flat(up))
            self.act_qdq(c, flat(gate))
            self.on_scalar(flat(sig), flat(gate), ACT.Sigmoid)
            self.on_vector([
                lambda dve: dve.tensor_scalar(flat(sig), flat(sig), 65536.0, ROUND, ALU.mult, ALU.add),
                lambda dve: dve.tensor_scalar(flat(sig), flat(sig), ROUND, 0.0, ALU.subtract, ALU.max),
                lambda dve: dve.tensor_scalar(flat(sig), flat(sig), 65535.0, 1.0 / 65536.0, ALU.min, ALU.mult),
                lambda dve: dve.tensor_tensor(flat(gate), flat(gate), flat(sig), ALU.mult)])
            self.act_qdq(c, flat(gate))
            self.on_vector([lambda dve: dve.tensor_tensor(flat(gate), flat(gate), flat(up), ALU.mult)])
            self.act_qdq(c, flat(gate))
            self.linear(gate, down_t, x3, add=x3)

    def ffn1(self, x3, y3):
        d = self.d
        with ExitStack() as c:
            sb = lambda name, shape, dt=F32: self.sb(c, name, shape, dt)
            wt, bias = sb("wt", [P, 6, P]), sb("bias", [P, 6])
            gamma, beta = sb("gamma", [P, 3]), sb("beta", [P, 3])
            with ExitStack() as c2:
                q, w, sc = self.sb(c2, "q", [P, 6, P], I32), self.sb(c2, "w", [P, 6, P]), self.sb(c2, "sc", [P, 6, 8])
                la, lb = self.sb(c2, "la", [32, 6, P]), self.sb(c2, "lb", [32, 6, P])
                self.loads([(q[:, :, :], d["l1_q"].rearrange("k o i -> o k i")), (sc[:, :, :], d["l1_scales"].rearrange("k o g -> o k g")),
                            (la[:, :, :], d["l1_la"].rearrange("k r i -> r k i")), (lb[:, :, :], d["l1_lbT"].rearrange("k r o -> r k o")),
                            (bias[:, :], d["l1_biasT"]), (gamma[:, :], d["l1_gammaT"]), (beta[:, :], d["l1_betaT"])])
                grouped = w[:, :, :].rearrange("o k (g e) -> o (k g) e", e=16)
                steps = sc[:, :, :].rearrange("o k g -> o (k g)").unsqueeze(2).to_broadcast([P, 48, 16])
                self.on_vector([
                    lambda dve: dve.tensor_scalar(w[:, :, :], q[:, :, :], 1.0 / 7.5, 1.0, ALU.mult, ALU.subtract),
                    lambda dve: dve.tensor_tensor(grouped, grouped, steps, ALU.mult)])
                self.turn_weights([(wt[:, k, :], [(w[:, k, :], self.ident[:, :]), (la[:, k, :], lb[:, k, :])]) for k in range(6)])
            z = sb("z", [P, 1, N])
            self.layernorm(x3, y3)
            for k in range(3):
                self.linear(y3, wt[:, 2 * k:2 * k + 1, :], z, bias=bias[:, 2 * k:2 * k + 1])
                self.layernorm(z, z, gamma=gamma[:, k:k + 1], beta=beta[:, k:k + 1])
                self.on_scalar(z[:, :, :], z[:, :, :], ACT.Gelu)
                self.linear(z, wt[:, 2 * k + 1:2 * k + 2, :], y3, bias=bias[:, 2 * k + 1:2 * k + 2], add=y3)
            self.on_vector([lambda dve: dve.tensor_tensor(self.xT[:, :], self.xT[:, :], self.yT[:, :], ALU.add)])

    def short_attention(self):
        nc, d, xT, yT = self.nc, self.d, self.xT, self.yT
        with ExitStack() as c:
            sb = lambda name, shape, dt=F32: self.sb(c, name, shape, dt)
            wq, wk, wv, wo, wo_full = sb("wq", [P, P]), sb("wk", [P, P]), sb("wv", [P, P]), sb("wo", [P, 4, P]), sb("wo_full", [P, P])
            bq, bk, bv, bo = (sb(n, [P, 1]) for n in ("bq", "bk", "bv", "bo"))
            head_mask, den_sel = sb("head_mask", [P, H]), sb("den_sel", [P, P])
            mask_i, bias, causal = sb("mask_i", [S, B, S], I32), sb("bias", [S, B, S]), sb("causal", [S, S])
            key_mask = d["mask_if1"].rearrange("b (a k) -> a b k", a=1)[:, :, 0:S].to_broadcast([S, B, S])
            self.loads([(wq[:, :], d["l2_wq"]), (wk[:, :], d["l2_wk"]), (wv[:, :], d["l2_wv"]),
                        (wo[:, :, :], d["l2_wo"].rearrange("s p o -> p s o")), (wo_full[:, :], d["l2_wo_full"]),
                        (bq[:, :], d["l2_bq"]), (bk[:, :], d["l2_bk"]), (bv[:, :], d["l2_bv"]), (bo[:, :], d["l2_bo"]),
                        (head_mask[:, :], d["head_mask"]), (den_sel[:, :], d["den_sel"]), (causal[:, :], d["causal"]),
                        (mask_i[:, :, :], key_mask)])
            self.fold_bias(bo[:, :], wo_full[:, :], bv[:, :], bo[:, :])
            q_sb = [sb(f"q_sb{u}", [P, S]) for u in range(2)]
            k_sb = [sb(f"k_sb{u}", [P, S]) for u in range(2)]
            q_m = [sb(f"q_m{u}", [P, H, S]) for u in range(2)]
            v_ext = [sb(f"v_ext{u}", [S, H, HD + 1]) for u in range(2)]
            ctx = [sb(f"ctx{u}", [P, S]) for u in range(2)]
            probs = sb("probs", [S, H, S])
            probs_t = sb("probs_t", [S, H, S])
            top = sb("top", [S, H])
            acc_sb, den_inv, heads_out = sb("acc_sb", [P, 4 * S]), sb("den_inv", [P, 4 * S]), sb("heads_out", [P, 4, S])
            qkv = self.banks(c, "qkv", 2)
            big = c.enter_context(nc.psum_tensor(f"big_{self.uid}", [P, 4, 512], F32))
            acc = self.banks(c, "acc", 1)[0]
            misc = self.banks(c, "misc", 1)[0]
            self.on_vector([
                lambda dve: dve.tensor_scalar(bias[:, :, :], mask_i[:, :, :], 0.0, NEG, ALU.is_equal, ALU.mult),
                lambda dve: dve.tensor_tensor(bias[:, :, :], bias[:, :, :], causal[:, :].unsqueeze(1).to_broadcast([S, B, S]), ALU.min),
                lambda dve: dve.memset(v_ext[0][:, :, :], 1.0),
                lambda dve: dve.memset(v_ext[1][:, :, :], 1.0),
                lambda dve: dve.memset(acc[:, :], 0.0)])
            ctx_in = [self.sem(c, f"ctx_in{u}") for u in range(2)]
            (qkv_ready, q_made, k_made, v_made, q_masked, scored, steps, lowered, exped, turned, turned_out, summed,
             sums_out, den_ready, den_made, heads_made, out_ready, added) = (self.sem(c, n) for n in (
                "qkv_ready", "q_made", "k_made", "v_made", "q_masked", "scored", "steps", "lowered", "exped", "turned",
                "turned_out", "summed", "sums_out", "den_ready", "den_made", "heads_made", "out_ready", "added"))
            four = lambda x: x.rearrange("q (k h) s -> q k h s", k=4)
            scores = big[0:S, :, 0:4 * S].rearrange("q k (h s) -> q k h s", h=4)
            block = c.enter_context(nc.Block())

            @block.sync
            def _(sp):
                sp.sem_inc(v_made, 1)
                with sp.Fori(0, B // 2) as i:
                    for u in range(2):
                        b = 2 * i + u
                        sp.wait_ge(v_made, b + 1)
                        sp.dma_start(ctx[u][:, :], d["ctxT"][:, bass.ds(b * S2, S)]).then_inc(ctx_in[u], 16)

            @block.tensor
            def _(pe):
                with pe.Fori(0, B // 2) as i:
                    for u in range(2):
                        b = 2 * i + u
                        pe.wait_ge(ctx_in[u], 16 * i + 16)
                        pe.matmul(qkv[u][:, 0:S], wq[:, :], yT[:, bass.ds(b * S, S)], start=True, stop=True)
                        pe.matmul(qkv[u][:, P:P + S], wk[:, :], ctx[u][:, :], start=True, stop=True)
                        pe.matmul(qkv[u][0:S, 2 * P:3 * P], ctx[u][:, :], wv[:, :], start=True, stop=True).then_inc(qkv_ready, 1)
                        pe.wait_ge(k_made, b + 1)
                        pe.wait_ge(q_masked, b + 1)
                        for h in range(H):
                            ins = pe.matmul(big[0:S, h // 4, (h % 4) * S:(h % 4 + 1) * S], q_m[u][:, h, :], k_sb[u][:, :],
                                            start=True, stop=True)
                        ins.then_inc(scored, 1)
                        pe.wait_ge(exped, b + 1)
                        for h in range(H):
                            ins = pe.transpose(big[0:S, h // 4, (h % 4) * S:(h % 4 + 1) * S], probs[:, h, :], self.ident[0:S, 0:S])
                        ins.then_inc(turned, 1)
                        pe.wait_ge(turned_out, b + 1)
                        for s in range(4):
                            for g in range(4):
                                h = 4 * s + g
                                ins = pe.matmul(acc[32 * g:32 * g + HD + 1, S * s:S * s + S], v_ext[u][:, h, :], probs_t[:, h, :],
                                                start=s == 0, stop=s == 3, skip_group_check=True)
                        ins.then_inc(summed, 1)
                        pe.wait_ge(sums_out, b + 1)
                        pe.matmul(misc[:, 0:4 * S], den_sel[:, :], acc_sb[:, :], start=True, stop=True).then_inc(den_ready, 1)
                        pe.wait_ge(heads_made, b + 1)
                        for s in range(4):
                            ins = pe.matmul(misc[:, 0:S], wo[:, s, :], heads_out[:, s, :], start=s == 0, stop=s == 3)
                        ins.then_inc(out_ready, 1)
                        pe.wait_ge(added, b + 1)

            @block.scalar
            def _(act):
                with act.Fori(0, B // 2) as i:
                    for u in range(2):
                        b = 2 * i + u
                        act.wait_ge(qkv_ready, b + 1)
                        act.activation(q_sb[u][:, :], qkv[u][:, 0:S], ACT.Identity, bias=bq[:, 0:1]).then_inc(q_made, 1)
                        act.activation(k_sb[u][:, :], qkv[u][:, P:P + S], ACT.Identity, bias=bk[:, 0:1]).then_inc(k_made, 1)
                        act.activation(v_ext[u][:, :, 0:HD], qkv[u][0:S, 2 * P:3 * P].rearrange("p (h d) -> p h d", h=H), ACT.Copy)\
                            .then_inc(v_made, 1)
                        act.wait_ge(lowered, b + 1)
                        act.activation(probs[:, :, :], probs[:, :, :], ACT.Exp).then_inc(exped, 1)
                        act.wait_ge(turned, b + 1)
                        act.activation(four(probs_t[:, :, :]), scores, ACT.Copy).then_inc(turned_out, 1)
                        act.wait_ge(summed, b + 1)
                        act.activation(acc_sb[:, :], acc[:, 0:4 * S], ACT.Copy).then_inc(sums_out, 1)

            @block.gpsimd
            def _(pool):
                with pool.Fori(0, B // 2) as i:
                    for u in range(2):
                        pool.wait_ge(q_made, 2 * i + (u + 1))
                        pool.tensor_tensor(q_m[u][:, :, :], q_sb[u][:, :].unsqueeze(1).to_broadcast([P, H, S]),
                                           head_mask[:, :].unsqueeze(2).to_broadcast([P, H, S]), ALU.mult).then_inc(q_masked, 1)

            @block.vector
            def _(dve):
                with dve.Fori(0, B // 2) as i:
                    for u in range(2):
                        b = 2 * i + u
                        done = Tally(steps, 6 * i + 3 * u)
                        m = bias[:, bass.ds(b, 1), :].to_broadcast([S, H, S])
                        dve.wait_ge(scored, b + 1)
                        done.inc(dve.tensor_tensor(four(probs[:, :, :]), scores, four(m), ALU.add))
                        done.wait(dve)
                        done.inc(dve.tensor_reduce(top[:, :], probs[:, :, :], AX.X, ALU.max))
                        done.wait(dve)
                        done.inc(dve.tensor_scalar(top[:, :], top[:, :], -1e20, None, ALU.max))
                        done.wait(dve)
                        dve.tensor_tensor(probs[:, :, :], probs[:, :, :], top[:, :].unsqueeze(2).to_broadcast([S, H, S]),
                                          ALU.subtract).then_inc(lowered, 1)
                        dve.wait_ge(den_ready, b + 1)
                        dve.reciprocal(den_inv[:, :], misc[:, 0:4 * S]).then_inc(den_made, 1)
                        dve.wait_ge(den_made, b + 1)
                        dve.tensor_tensor(heads_out[:, :, :].rearrange("p s q -> p (s q)"), acc_sb[:, :], den_inv[:, :], ALU.mult)\
                            .then_inc(heads_made, 1)
                        dve.wait_ge(out_ready, b + 1)
                        x = xT[:, bass.ds(b * S, S)]
                        dve.scalar_tensor_tensor(x, misc[:, 0:S], bo[:, 0:1], x, ALU.add, ALU.add).then_inc(added, 1)

    def ffn2(self, x3, y3):
        nc, d, xT, yT = self.nc, self.d, self.xT, self.yT
        E = 16
        self.layernorm(x3, y3)
        with ExitStack() as c:
            sb = lambda name, shape, dt=F32: self.sb(c, name, shape, dt)
            w1, b1, w2, b2 = sb("w1", [P, P]), sb("b1", [P, 1]), sb("w2", [P, E + 1]), sb("b2", [1, E + 1])
            scales, biases, rank, ones = sb("scales", [E, P]), sb("biases", [E, P]), sb("rank", [S, E]), sb("ones", [1, S])
            self.loads([(w1[:, :], d["l2f_w1"]), (b1[:, :], d["l2f_b1"]), (w2[:, :], d["l2f_w2"]), (b2[:, :], d["l2f_b2"]),
                        (scales[:, :], d["l2f_scales"]), (biases[:, :], d["l2f_biases"]), (rank[:, :], d["rank"]),
                        (ones[:, :], d["ones"])])
            hid = [sb(f"hid{u}", [P, CH]) for u in range(2)]
            gate = [sb(f"gate{u}", [S, 4]) for u in range(2)]
            score = [sb(f"score{u}", [S, 4, E]) for u in range(2)]
            cand = [sb(f"cand{u}", [S, 4, E]) for u in range(2)]
            top = [sb(f"top{u}", [S, 4]) for u in range(2)]
            chosen = [sb(f"chosen{u}", [E, CH]) for u in range(2)]
            routed = [sb(f"routed{u}", [P, CH]) for u in range(2)]
            hp = self.banks(c, "hp", 2)
            sp_ = self.banks(c, "scores", 2)
            one = self.banks(c, "one", 2)
            gain, shift = self.banks(c, "gain", 2)
            (hid_ready, relu_made, tanh_made, scored, gated, steps, chosen_made, turned, turned_out, expert_ready,
             routed_made) = (self.sem(c, n) for n in (
                "hid_ready", "relu_made", "tanh_made", "scored", "gated", "steps", "chosen_made", "turned", "turned_out",
                "expert_ready", "routed_made"))
            R_ = P // 2
            block = c.enter_context(nc.Block())

            @block.tensor
            def _(pe):
                pe.sem_inc(routed_made, 1)
                with pe.Fori(0, NPAIR) as i:
                    for u in range(2):
                        pe.matmul(hp[u][:, 0:CH], w1[:, :], yT[:, bass.ds(i * (2 * CH) + u * CH, CH)], start=True, stop=True)\
                            .then_inc(hid_ready, 1)
                    for u in range(2):
                        pe.wait_ge(relu_made, 2 * i + (u + 1))
                        pe.wait_ge(tanh_made, 2 * i + (u + 1))
                        for k in range(4):
                            o = sp_[u][0:S, 32 * k:32 * k + E + 1]
                            pe.matmul(o, hid[u][:, S * k:S * (k + 1)], w2[:, :], start=True, stop=False)
                            ins = pe.matmul(o, ones[:, :], b2[:, :], start=False, stop=True)
                        ins.then_inc(scored, 1)
                    for u in range(2):
                        pe.wait_ge(chosen_made, 2 * i + (u + 1))
                        for k in range(4):
                            ins = pe.transpose(one[u][0:E, S * k:S * (k + 1)], cand[u][:, k, :], self.ident[0:S, 0:S])
                        ins.then_inc(turned, 1)
                    for u in range(2):
                        pe.wait_ge(turned_out, 2 * i + (u + 1))
                        pe.wait_ge(routed_made, 6 * i + (3 * u + 1))
                        pe.matmul(gain[:, 0:CH], scales[:, :], chosen[u][:, :], start=True, stop=True)
                        pe.matmul(shift[:, 0:CH], biases[:, :], chosen[u][:, :], start=True, stop=True).then_inc(expert_ready, 1)

            @block.scalar
            def _(act):
                with act.Fori(0, NPAIR) as i:
                    for u in range(2):
                        act.wait_ge(hid_ready, 2 * i + (u + 1))
                        act.activation(hid[u][0:R_, :], hp[u][0:R_, 0:CH], ACT.Relu, bias=b1[0:R_, 0:1]).then_inc(relu_made, 1)
                        act.activation(hid[u][R_:P, :], hp[u][R_:P, 0:CH], ACT.Tanh, bias=b1[R_:P, 0:1]).then_inc(tanh_made, 1)
                    for u in range(2):
                        act.wait_ge(scored, 2 * i + (u + 1))
                        act.activation(gate[u][:, :], sp_[u][0:S, 0:128].rearrange("q (k e) -> q k e", k=4)[:, :, E],
                                       ACT.Sigmoid).then_inc(gated, 1)
                    for u in range(2):
                        act.wait_ge(turned, 2 * i + (u + 1))
                        act.activation(chosen[u][:, :], one[u][0:E, 0:CH], ACT.Copy).then_inc(turned_out, 1)

            @block.vector
            def _(dve):
                with dve.Fori(0, NPAIR) as i:
                    for u in range(2):
                        done = Tally(steps, 10 * i + 5 * u)
                        wide = top[u][:, :].unsqueeze(2).to_broadcast([S, 4, E])
                        dve.wait_ge(gated, 2 * i + (u + 1))
                        done.inc(dve.tensor_tensor(score[u][:, :, :], sp_[u][0:S, 0:128].rearrange("q (k e) -> q k e", k=4)[:, :, 0:E],
                                                   gate[u][:, :].unsqueeze(2).to_broadcast([S, 4, E]), ALU.mult))
                        done.wait(dve)
                        done.inc(dve.tensor_reduce(top[u][:, :], score[u][:, :, :], AX.X, ALU.max))
                        done.wait(dve)
                        done.inc(dve.tensor_tensor(cand[u][:, :, :], score[u][:, :, :], wide, ALU.is_ge))
                        done.wait(dve)
                        done.inc(dve.tensor_tensor(cand[u][:, :, :], cand[u][:, :, :], rank[:, :].unsqueeze(1).to_broadcast([S, 4, E]), ALU.mult))
                        done.wait(dve)
                        done.inc(dve.tensor_reduce(top[u][:, :], cand[u][:, :, :], AX.X, ALU.max))
                        done.wait(dve)
                        dve.tensor_tensor(cand[u][:, :, :], cand[u][:, :, :], wide, ALU.is_ge).then_inc(chosen_made, 1)
                    for u in range(2):
                        done = Tally(routed_made, 6 * i + (3 * u + 1))
                        y, x = (t[:, bass.ds(i * (2 * CH) + u * CH, CH)] for t in (yT, xT))
                        dve.wait_ge(expert_ready, 2 * i + (u + 1))
                        done.inc(dve.tensor_tensor(routed[u][:, :], y, gain[:, 0:CH], ALU.mult))
                        done.wait(dve)
                        done.inc(dve.tensor_tensor(routed[u][:, :], routed[u][:, :], shift[:, 0:CH], ALU.add))
                        done.wait(dve)
                        done.inc(dve.tensor_tensor(x, x, routed[u][:, :], ALU.add))

    def context_sums(self, a2, wkv, diag):
        nc, d = self.nc, self.d
        with ExitStack() as c:
            sb = lambda name, shape, dt=F32: self.sb(c, name, shape, dt)
            ctx = [sb(f"ctx{u}", [P, S2]) for u in range(2)]
            TG = 4
            G = NT // TG
            keys, vals = ([sb(f"{n}{k}", [KT, TG, 8, 16]) for k in range(2)] for n in ("keys", "vals"))
            top, total = ([sb(f"{n}{k}", [KT, TG, 8]) for k in range(2)] for n in ("top", "total"))
            kv = [c.enter_context(nc.psum_tensor(f"kv{k}_{self.uid}", [P, TG, 2, P], F32)) for k in range(2)]
            acc = self.banks(c, "acc", 2)
            ctx_in = [self.sem(c, f"ctx_in{u}") for u in range(2)]
            kv_ready, topped, lowered, exped, summed, inverted, vals_made, acc_ready, acc_out = (self.sem(c, n) for n in (
                "kv_ready", "topped", "lowered", "exped", "summed", "inverted", "vals_made", "acc_ready", "acc_out"))
            block = c.enter_context(nc.Block())

            heads = lambda x: x.rearrange("q t (h e) -> q t h e", h=8)
            wide = lambda x: x[:, :, :].unsqueeze(3).to_broadcast([KT, TG, 8, 16])

            @block.sync
            def _(sp):
                with sp.Fori(0, B // 2) as i:
                    for u in range(2):
                        b = 2 * i + u
                        sp.wait_ge(acc_ready, b + 1)
                        sp.dma_start(ctx[u][:, :], d["ctxT"][:, bass.ds(b * S2, S2)]).then_inc(ctx_in[u], 16)

            @block.tensor
            def _(pe):
                def project(i, k):
                    u, g = divmod(k, G)
                    if g == 0:
                        pe.wait_ge(ctx_in[u], 16 * i + 16)
                    pe.wait_ge(vals_made, 2 * G * i + (k + 1))
                    for t in range(TG):
                        w = keys_of(TG * g + t)
                        s = (TG * g + t) * KT
                        ins = pe.matmul(kv[k % 2][0:w, t, :, :], ctx[u][:, s:s + w], wkv[:, :], start=True, stop=True)
                    ins.then_inc(kv_ready, 1)

                def add_up(i, k):
                    u, g = divmod(k, G)
                    pe.wait_ge(vals_made, 2 * G * i + (k + 3))
                    for t in range(TG):
                        w = keys_of(TG * g + t)
                        ins = pe.matmul(acc[u][:, 0:P], keys[k % 2][0:w, t, :, :].rearrange("q h e -> q (h e)"),
                                        vals[k % 2][0:w, t, :, :].rearrange("q h e -> q (h e)"),
                                        start=g == 0 and t == 0, stop=g == G - 1 and t == TG - 1)
                    if g == G - 1:
                        ins.then_inc(acc_ready, 1)

                pe.sem_inc(acc_ready, 2)
                with pe.Fori(0, B // 2) as i:
                    project(i, 0)
                    for k in range(2 * G):
                        if k + 1 < 2 * G:
                            project(i, k + 1)
                        add_up(i, k)

            @block.scalar
            def _(act):
                with act.Fori(0, B // 2) as i:
                    for k in range(2 * G):
                        act.wait_ge(lowered, 2 * G * i + (k + 1))
                        act.activation(keys[k % 2][:, :, :, :], keys[k % 2][:, :, :, :], ACT.Exp, scale=0.5).then_inc(exped, 1)

            @block.vector
            def _(dve):
                def front(i, k):
                    n = 2 * G * i + (k + 1)
                    raw = heads(kv[k % 2][0:KT, :, 0, :])
                    dve.wait_ge(kv_ready, n)
                    dve.tensor_reduce(top[k % 2][:, :, :], raw, AX.X, ALU.max).then_inc(topped, 1)
                    dve.wait_ge(topped, n)
                    dve.tensor_tensor(keys[k % 2][:, :, :, :], raw, wide(top[k % 2]), ALU.subtract).then_inc(lowered, 1)

                def back(i, k):
                    n = 2 * G * i + (k + 1)
                    u, g = divmod(k, G)
                    dve.wait_ge(exped, n)
                    dve.tensor_reduce(total[k % 2][:, :, :], keys[k % 2][:, :, :, :], AX.X, ALU.add).then_inc(summed, 1)
                    dve.wait_ge(summed, n)
                    dve.reciprocal(total[k % 2][:, :, :], total[k % 2][:, :, :]).then_inc(inverted, 1)
                    dve.wait_ge(inverted, n)
                    dve.tensor_tensor(vals[k % 2][:, :, :, :], heads(kv[k % 2][0:KT, :, 1, :]), wide(total[k % 2]), ALU.mult)\
                        .then_inc(vals_made, 1)
                    if g == G - 1:
                        dve.wait_ge(acc_ready, 2 * i + (u + 3))
                        dve.tensor_tensor(a2[:, bass.ds(2 * i + u, 1), :].rearrange("p a e -> p (a e)"), acc[u][:, 0:P],
                                          diag[:, :], ALU.mult).then_inc(acc_out, 1)

                dve.memset(kv[0][:, :, :, :], 0.0).then_inc(vals_made, 1)
                dve.memset(kv[1][:, :, :, :], 0.0).then_inc(vals_made, 1)
                with dve.Fori(0, B // 2) as i:
                    front(i, 0)
                    for k in range(2 * G):
                        if k + 1 < 2 * G:
                            front(i, k + 1)
                        back(i, k)

    def linear_attention(self, w, nh, mask, a2, wo, diag):
        nc, yT = self.nc, self.yT
        with ExitStack() as c:
            sb = lambda name, shape, dt=F32: self.sb(c, name, shape, dt)
            y_b, qk = [sb(f"y_b{u}", [P, S]) for u in range(2)], [sb(f"qk{u}", [S, nh, 16]) for u in range(2)]
            v_sb = [sb(f"v_sb{u}", [S, P]) for u in range(2)]
            top = [sb(f"top{u}", [S, nh]) for u in range(2)]
            q_t = [sb(f"q_t{u}", [P, S]) for u in range(2)]
            a_m = [sb(f"a_m{u}", [P, P]) for u in range(2)]
            mixed = [sb(f"mixed{u}", [16, 2, 4 * S]) for u in range(2)]
            ps, op = self.banks(c, "proj", 2), self.banks(c, "outp", 2)
            tr, ap = self.banks(c, "tr", 2)
            self.uid += 1
            bm = c.enter_context(nc.psum_tensor(f"bm_{self.uid}", [P, 2, 512], F32))
            (y_made, proj, steps, norm_steps, lowered, exped, v_made, normed, q_turned, a_ready, q_out, a_made, bm_ready, bm_out,
             out_ready, added) = (self.sem(c, n) for n in (
                "y_made", "proj", "steps", "norm_steps", "lowered", "exped", "v_made", "normed", "q_turned", "a_ready", "q_out",
                "a_made", "bm_ready", "bm_out", "out_ready", "added"))
            cols = w.shape[1]
            block = c.enter_context(nc.Block())

            @block.tensor
            def _(pe):
                pe.sem_inc(bm_out, 1)
                with pe.Fori(0, B // 2) as i:
                    for u in range(2):
                        pe.wait_ge(y_made, 2 * i + (u + 1))
                        pe.matmul(ps[u][0:S, 0:cols], y_b[u][:, :], w[:, :], start=True, stop=True).then_inc(proj, 1)
                    for u in range(2):
                        pe.wait_ge(normed, 2 * i + (u + 1))
                        if u:
                            pe.wait_ge(q_out, 2 * i + 1)
                            pe.wait_ge(a_made, 2 * i + 1)
                        if a2 is None:
                            pe.wait_ge(v_made, 2 * i + (u + 1))
                            pe.matmul(ap[:, 0:P], qk[u][:, 8:16, :].rearrange("q h e -> q (h e)"), v_sb[u][:, :],
                                      start=True, stop=True).then_inc(a_ready, 1)
                        pe.transpose(tr[:, 0:S], qk[u][:, 0:8, :].rearrange("q h e -> q (h e)"), self.ident[0:S, 0:S])\
                            .then_inc(q_turned, 1)
                    for u in range(2):
                        pe.wait_ge(q_out, 2 * i + (u + 1))
                        pe.wait_ge(a_made, 2 * i + (u + 1))
                        pe.wait_ge(bm_out, 2 * i + (u + 1))
                        for h in range(8):
                            ins = pe.matmul(bm[0:16, h // 4, (h % 4) * S:(h % 4 + 1) * S], a_m[u][:, 16 * h:16 * h + 16], q_t[u][:, :],
                                            start=True, stop=True)
                        ins.then_inc(bm_ready, 1)
                    for u in range(2):
                        pe.wait_ge(bm_out, 2 * i + (u + 2))
                        flat = mixed[u][:, :, :].rearrange("e k s -> e (k s)").rearrange("e (w k) -> e k w", k=8)
                        for k in range(8):
                            ins = pe.matmul(op[u][:, 0:S], wo[:, k, :], flat[:, k, :], start=k == 0, stop=k == 7)
                        ins.then_inc(out_ready, 1)

            @block.scalar
            def _(act):
                with act.Fori(0, B // 2) as i:
                    for u in range(2):
                        act.activation(y_b[u][:, :], yT[:, bass.ds((2 * i + u) * S, S)], ACT.Copy).then_inc(y_made, 1)
                    for u in range(2):
                        if a2 is not None:
                            act.activation(a_m[u][:, :], a2[:, bass.ds(2 * i + u, 1), :].rearrange("p a e -> p (a e)"), ACT.Copy)\
                                .then_inc(a_made, 1)
                    for u in range(2):
                        act.wait_ge(lowered, 2 * i + (u + 1))
                        act.activation(qk[u][:, :, :], qk[u][:, :, :], ACT.Exp, scale=0.5).then_inc(exped, 1)
                        if a2 is None:
                            act.activation(v_sb[u][:, :], ps[u][0:S, 2 * P:3 * P], ACT.Copy).then_inc(v_made, 1)
                    for u in range(2):
                        act.wait_ge(q_turned, 2 * i + (u + 1))
                        act.activation(q_t[u][:, :], tr[:, 0:S], ACT.Copy).then_inc(q_out, 1)
                    for u in range(2):
                        act.wait_ge(bm_ready, 2 * i + (u + 1))
                        act.activation(mixed[u][:, :, :], bm[0:16, :, 0:4 * S], ACT.Copy).then_inc(bm_out, 1)

            @block.vector
            def _(dve):
                with dve.Fori(0, B // 2) as i:
                    for u in range(2):
                        done = Tally(steps, 4 * i + 2 * u)
                        raw = ps[u][0:S, 0:16 * nh].rearrange("q (h e) -> q h e", e=16)
                        dve.wait_ge(proj, 2 * i + (u + 1))
                        if mask is not None:
                            done.inc(dve.tensor_tensor(qk[u][:, :, :], raw, mask[:, :, :], ALU.add))
                        else:
                            done.inc(dve.tensor_copy(qk[u][:, :, :], raw))
                        done.wait(dve)
                        done.inc(dve.tensor_reduce(top[u][:, :], qk[u][:, :, :], AX.X, ALU.max))
                        done.wait(dve)
                        dve.tensor_tensor(qk[u][:, :, :], qk[u][:, :, :], top[u][:, :].unsqueeze(2).to_broadcast([S, nh, 16]),
                                          ALU.subtract).then_inc(lowered, 1)
                    for u in range(2):
                        done = Tally(norm_steps, 4 * i + 2 * u)
                        dve.wait_ge(exped, 2 * i + (u + 1))
                        done.inc(dve.tensor_reduce(top[u][:, :], qk[u][:, :, :], AX.X, ALU.add))
                        done.wait(dve)
                        done.inc(dve.reciprocal(top[u][:, :], top[u][:, :]))
                        done.wait(dve)
                        dve.tensor_tensor(qk[u][:, :, :], qk[u][:, :, :], top[u][:, :].unsqueeze(2).to_broadcast([S, nh, 16]),
                                          ALU.mult).then_inc(normed, 1)
                    if a2 is None:
                        for u in range(2):
                            dve.wait_ge(a_ready, 2 * i + (u + 1))
                            dve.tensor_tensor(a_m[u][:, :], ap[:, 0:P], diag[:, :], ALU.mult).then_inc(a_made, 1)
                    for u in range(2):
                        dve.wait_ge(out_ready, 2 * i + (u + 1))
                        y = yT[:, bass.ds((2 * i + u) * S, S)]
                        dve.tensor_tensor(y, y, op[u][:, 0:S], ALU.add).then_inc(added, 1)

    def attention3(self, x3, y3):
        d = self.d
        with ExitStack() as c:
            sb = lambda name, shape, dt=F32: self.sb(c, name, shape, dt)
            w1, w2q, w2kv = sb("w1", [P, 3 * P]), sb("w2q", [P, P]), sb("w2kv", [P, 2 * P])
            wo1, wo2 = sb("wo1", [16, 8, P]), sb("wo2", [16, 8, P])
            diag, mask = sb("diag", [P, P]), sb("mask", [S, 16, 16])
            gains = sb("gains", [P, 6])
            e1, e2 = sb("e1", [P // 2, P]), sb("e2", [P // 2, P])
            d1, d2 = sb("d1", [P // 2, P]), sb("d2", [P // 2, P])
            f1, f2 = sb("f1", [P, 1, P]), sb("f2", [P, 1, P])
            a2 = sb("a2", [P, B, P])
            h = sb("h", [P, 1, N])
            self.loads([(w1[:, :], d["l3_w1"]), (w2q[:, :], d["l3_w2q"]), (w2kv[:, :], d["l3_w2kv"]),
                        (wo1[:, :, :], d["l3_wo1"].rearrange("(k e) o -> e k o", e=16)),
                        (wo2[:, :, :], d["l3_wo2"].rearrange("(k e) o -> e k o", e=16)),
                        (diag[:, :], d["diag"]), (mask[:, :, :], d["mask3"]), (gains[:, :], d["l3_gains"]),
                        (e1[:, :], d["l3_e1"]), (e2[:, :], d["l3_e2"]), (d1[:, :], d["l3_d1T"]), (d2[:, :], d["l3_d2T"])])
            self.turn_weights([(f1[:, 0, :], [(e1[:, :], d1[:, :])]), (f2[:, 0, :], [(e2[:, :], d2[:, :])])])
            self.context_sums(a2, w2kv, diag)
            self.layernorm(x3, y3)
            self.linear_attention(w1, 16, mask, None, wo1, diag)
            self.layernorm(y3, y3, gamma=gains[:, 0:1], beta=gains[:, 1:2])
            self.linear_attention(w2q, 8, None, a2, wo2, diag)
            self.layernorm(y3, y3, gamma=gains[:, 2:3], beta=gains[:, 3:4])
            self.linear(y3, f1, h, func=ACT.Silu)
            self.linear(h, f2, y3, add=y3)
            self.layernorm(y3, y3, gamma=gains[:, 4:5], beta=gains[:, 5:6])
            self.on_vector([lambda dve: dve.tensor_tensor(self.xT[:, :], self.xT[:, :], self.yT[:, :], ALU.add)])

    def ffn3(self, x3, y3):
        d = self.d
        F = 4
        with ExitStack() as c:
            sb = lambda name, shape, dt=F32: self.sb(c, name, shape, dt)
            w = [sb("w_fc", [P, 1, F * P]), sb("w_proj", [P, F, P])]
            gain, bias = sb("gain", [P, F]), sb("bias", [P, F])
            mean4 = sb("mean4", [P, P])
            part, whole, scale, inv = (sb(n, [P, 1])[:, :] for n in ("part", "whole", "scale", "inv"))
            self.loads([(w[0][:, 0, :], d["l3f_fcT"]), (w[1][:, :, :], d["l3f_projT"].rearrange("(t h) o -> h t o", h=P)),
                        (gain[:, :], d["l3f_w"]), (bias[:, :], d["l3f_b"])])
            for t in w:
                x = t[:, :, :].rearrange("p a b -> p (a b)")
                self.global_scale(x, part, whole, scale, inv, ALU.add, bass.bass_isa.ReduceOp.add,
                                  lambda dve, s, v: dve.tensor_scalar(s, v, 1.0 / (F * P * P), 1e-6, ALU.mult, ALU.add))
                self.on_vector([
                    lambda dve: dve.tensor_scalar(x, x, inv, ROUND, ALU.mult, ALU.add),
                    lambda dve: dve.tensor_scalar(x, x, ROUND, 1.0, ALU.subtract, ALU.min),
                    lambda dve: dve.tensor_scalar(x, x, -1.0, None, ALU.max),
                    lambda dve: dve.memset(mean4[:, :], 1.0 / (F * P))])
            h = sb("h", [P, F, N])
            self.layernorm(x3, y3)
            self.linear(y3, w[0], h, func=ACT.Gelu)
            self.layernorm(h, h, tiles=F, mean=mean4, gamma=gain, beta=bias)
            self.linear(h, w[1], x3, add=x3)

    def build(self, upto=99, first=0):
        nc, d = self.nc, self.d
        with ExitStack() as ctx:
            self.load_all(ctx)
            x3 = self.xT[:, :].unsqueeze(1)
            y3 = self.yT[:, :].unsqueeze(1)
            stages = [self.attention0, self.ffn0, self.attention1, self.ffn1, self.attention2, self.ffn2, self.attention3,
                      self.ffn3]
            for n, stage in enumerate(stages):
                if first <= n < upto:
                    stage(x3, y3)
                    self.clear_semaphores()
            self.store_out()

    def attention0(self, x3, y3):
        d = self.d
        self.layernorm(x3, y3)
        self.long_attention(d["l0_wq"], d["l0_wk"], d["l0_wv"], d["l0_wo"], d["l0_bo"], query_mask=d["query_mask"])

    def attention1(self, x3, y3):
        d = self.d
        self.layernorm(x3, y3)
        self.long_attention(d["l1_wq"], d["l1_wk"], d["l1_wv"], d["l1_wo"], d["l1_bo"], d["l1_bq"], d["l1_bk"],
                            d["l1_bv"], d["l1_wo_full"], key_mask=d["key_mask"])

    def attention2(self, x3, y3):
        self.layernorm(x3, y3)
        self.short_attention()


def _layout(inputs):
    import numpy as np

    g = {k: np.asarray(v) for k, v in inputs.items()}
    a = {}
    order = np.array([(2 * p + q) * HD + dd for q in range(2) for dd in range(HD) for p in range(NP)])

    def col(x):
        return np.ascontiguousarray(x.reshape(-1, 1))

    def out_rows(w_io):
        o = np.zeros((4, P, w_io.shape[1]), w_io.dtype)
        for h in range(H):
            o[h // 4, 32 * (h % 4):32 * (h % 4) + HD] = w_io[h * HD:(h + 1) * HD]
        return o

    a["xT"] = g["x"].reshape(N, P).T
    a["ctxT"] = g["ctx_1024"].reshape(B * S2, P).T
    a["ident"] = np.eye(P, dtype=np.float32)
    sel = np.zeros((P, P), np.float32)
    for k in range(4):
        sel[32 * k + HD, 32 * k:32 * k + 32] = 1.0
    a["den_sel"] = sel
    a["query_mask"] = g["mask_1x1xSxS2_bk0"].reshape(S, S2)
    a["key_mask"] = g["mask_BxS2_bk0"]
    a["l0_wq"] = g["L0_xattn_Wq"].T[:, order]
    a["l0_wk"] = g["L0_xattn_Wk"].T[:, order]
    a["l0_wv"] = g["L0_xattn_Wv"].T
    a["l0_wo"] = out_rows(g["L0_xattn_Wo"].T)
    a["l0_bo"] = col(g["L0_xattn_bo"])

    def bias_rows(prefix, bq, bk, bv, bo, order_):
        for n, b in (("bq", bq[order_]), ("bk", bk[order_]), ("bv", bv), ("bo", bo)):
            a[f"{prefix}_{n}"] = col(b)

    a["w_up"], a["w_gate"], a["w_down"] = g["L0_ffn_w_up"], g["L0_ffn_w_gate"], g["L0_ffn_w_down"]
    a["l1_wq"] = g["L1_xattn_Wq"][:, order]
    a["l1_wk"] = g["L1_xattn_Wkv"][:, :P][:, order]
    a["l1_wv"] = g["L1_xattn_Wkv"][:, P:]
    a["l1_wo"], a["l1_wo_full"] = out_rows(g["L1_xattn_Wo"]), g["L1_xattn_Wo"]
    bias_rows("l1", g["L1_xattn_bq"], g["L1_xattn_bkv"][:P], g["L1_xattn_bkv"][P:], g["L1_xattn_bo"], order)
    a["l1_q"], a["l1_scales"], a["l1_la"] = g["L1_ffn_qweights"], g["L1_ffn_scales"], g["L1_ffn_lora_a"]
    a["l1_lbT"] = g["L1_ffn_lora_b"].transpose(0, 2, 1)
    a["l1_biasT"], a["l1_gammaT"], a["l1_betaT"] = (g[f"L1_ffn_{n}"].T for n in ("biases", "ln_gamma", "ln_beta"))
    for n in "qkv":
        a[f"l2_w{n}"] = g[f"L2_xattn_W{n}"].T
    a["l2_wo"], a["l2_wo_full"] = out_rows(g["L2_xattn_Wo"].T), g["L2_xattn_Wo"].T
    bias_rows("l2", *(g[f"L2_xattn_b{n}"] for n in "qkvo"), np.arange(P))
    a["mask_if1"] = g["mask_BxS2_if1"]
    head = np.arange(P) // HD
    a["head_mask"] = np.where(head[:, None] == np.arange(H)[None, :], SCALE, 0.0).astype(np.float32)
    a["causal"] = np.where(np.arange(S)[None, :] <= np.arange(S)[:, None], 0.0, NEG).astype(np.float32)
    a["l2f_w1"] = np.concatenate([g["L2_ffn_W1"], g["L2_ffn_Wg1"]], 1)
    a["l2f_b1"] = col(np.concatenate([g["L2_ffn_b1"], g["L2_ffn_bg1"]]))
    w2 = np.zeros((P, 17), np.float32)
    w2[:64, :16], w2[64:, 16:] = g["L2_ffn_W2"], g["L2_ffn_Wg2"]
    a["l2f_w2"] = w2
    a["l2f_b2"] = np.concatenate([g["L2_ffn_b2"], g["L2_ffn_bg2"]]).reshape(1, 17)
    a["l2f_scales"], a["l2f_biases"] = g["L2_ffn_expert_scales"], g["L2_ffn_expert_biases"]
    a["rank"] = np.broadcast_to(16.0 - np.arange(16), (S, 16)).astype(np.float32)
    a["ones"] = np.ones((1, S), np.float32)
    heads_in = lambda w: w.transpose(1, 0, 2).reshape(P, P)
    a["l3_w1"] = np.concatenate([heads_in(g[f"L3_xattn_W{n}1"]) for n in "qkv"], 1)
    a["l3_w2q"] = heads_in(g["L3_xattn_Wq2"])
    a["l3_w2kv"] = np.concatenate([heads_in(g[f"L3_xattn_W{n}2"]) for n in "kv"], 1)
    a["l3_wo1"], a["l3_wo2"] = g["L3_xattn_Wo1"].T, g["L3_xattn_Wo2"].T
    block = np.arange(P) // 16
    a["diag"] = (block[:, None] == block[None, :]).astype(np.float32)
    mask3 = np.zeros((S, 16, 16), np.float32)
    mask3[:, :8] = np.where(np.arange(16)[None, :] <= np.arange(S)[:, None], 0.0, NEG)[:, None, :]
    a["mask3"] = mask3
    a["l3_gains"] = np.stack([g[f"L3_xattn_{n}"] for n in ("g1", "b1", "g2", "b2", "g3", "b3")], 1)
    a["l3_e1"], a["l3_e2"] = g["L3_xattn_E1"], g["L3_xattn_E2"]
    a["l3_d1T"], a["l3_d2T"] = g["L3_xattn_D1"].T, g["L3_xattn_D2"].T
    a["l3f_fcT"], a["l3f_projT"] = g["L3_ffn_W_fc"].T, g["L3_ffn_W_proj"].T
    a["l3f_w"], a["l3f_b"] = g["L3_ffn_ln_w"].reshape(4, P).T, g["L3_ffn_ln_b"].reshape(4, P).T
    return {k: np.ascontiguousarray(v) for k, v in a.items()}


def kernel(**inputs):
    import numpy as _np
    import concourse.bacc as _bacc
    from concourse import mybir as _mybir
    from concourse.bass_utils import run_bass_kernel_spmd as _run

    nc = _bacc.Bacc("TRN2", target_bir_lowering=False, num_devices=1)
    arrays, args = {}, {}
    for name, a in _layout(inputs).items():
        arrays[f"in_{name}"] = a
        args[name] = nc.dram_tensor(f"in_{name}", a.shape, _mybir.dt.from_np(a.dtype), kind="ExternalInput").ap()
    out = nc.dram_tensor("out_xT", (P, N), F32, kind="ExternalOutput").ap()
    Kernel(nc, args, out).build()
    r = _run(nc, [arrays], core_ids=[0])
    return _np.ascontiguousarray(r.results[0]["out_xT"].T).reshape(B, S, P)
```

```python
from contextlib import ExitStack

import concourse.bass as bass
from concourse import mybir

ALU = mybir.AluOpType
ACT = mybir.ActivationFunctionType
AX = mybir.AxisListType
F32 = mybir.dt.float32
BF16 = mybir.dt.bfloat16
I32 = mybir.dt.int32
U8 = mybir.dt.uint8
RMAX = bass.bass_isa.ReduceOp.max

P = 128
B, S, S2 = 32, 100, 1444
N = B * S
CH = 400
NC = N // CH
NPAIR = NC // 2
H, HD = 16, 8
SCALE = float(HD) ** -0.5
KT = 121
NT = (S2 + KT - 1) // KT
NP = H // 2
TERMS = 6
K_PART = [0, 0, 1, 1, 0, 2]
Q_PART = [0, 1, 0, 1, 2, 0]
R_MASK = 16 * TERMS
R_ALL = R_MASK + 7
TG = 4
LATE = 8
KC = TG * KT
NEG = -1e30
ROUND = 12582912.0


def keys_of(t):
    return min(KT, S2 - t * KT)


class Tally:

    def __init__(self, sem, base=0):
        self.sem, self.value = sem, base

    def inc(self, instruction):
        instruction.then_inc(self.sem, 1)
        self.value = self.value + 1

    def wait(self, engine):
        engine.wait_ge(self.sem, self.value)


class Kernel:
    def __init__(self, nc, d, out):
        self.nc, self.d, self.out = nc, d, out
        self.uid = 0
        self.used = []

    def sb(self, ctx, name, shape, dt=F32):
        self.uid += 1
        return ctx.enter_context(self.nc.sbuf_tensor(f"{name}_{self.uid}", shape, dt))

    def banks(self, ctx, name, n, dt=F32):
        self.uid += 1
        return [ctx.enter_context(self.nc.psum_tensor(f"{name}{k}_{self.uid}", [P, 512], dt)) for k in range(n)]

    def sem(self, ctx, name):
        self.uid += 1
        sem = ctx.enter_context(self.nc.semaphore(f"{name}_{self.uid}"))
        self.used.append(sem)
        return sem

    def clear_semaphores(self):
        used, self.used = self.used, []
        block = ExitStack()
        with block as c:
            b = c.enter_context(self.nc.Block())

            @b.sync
            def _(sp):
                for sem in used:
                    sp.sem_clear(sem)

    def load_all(self, ctx):
        nc, d = self.nc, self.d
        self.xT = self.sb(ctx, "xT", [P, N])
        self.yT = self.sb(ctx, "yT", [P, N])
        self.ident = self.sb(ctx, "ident", [P, P])
        self.mean = self.sb(ctx, "mean", [P, P])
        self.eps = self.sb(ctx, "eps", [P, 1])
        self.ones = self.sb(ctx, "ones", [P, P])
        with ExitStack() as c:
            loaded = self.sem(c, "loaded")
            block = c.enter_context(nc.Block())

            @block.sync
            def _(sp):
                sp.dma_start(self.xT[:, :], d["xT"]).then_inc(loaded, 16)
                sp.dma_start(self.ident[:, :], d["ident"]).then_inc(loaded, 16)
                sp.wait_ge(loaded, 32)

            @block.vector
            def _(dve):
                dve.memset(self.mean[:, :], 1.0 / P)
                dve.memset(self.eps[:, :], 1e-5)
                dve.memset(self.ones[:, :], 1.0)

    def store_out(self):
        nc = self.nc
        with ExitStack() as c:
            stored = self.sem(c, "stored")
            block = c.enter_context(nc.Block())

            @block.sync
            def _(sp):
                sp.dma_start(self.out, self.xT[:, :]).then_inc(stored, 16)
                sp.wait_ge(stored, 16)

    def layernorm(self, src, dst, tiles=1, mean=None, gamma=None, beta=None):
        nc = self.nc
        mean = mean or self.mean
        U = 4
        with ExitStack() as c:
            mu = self.banks(c, "mu", U)
            var = self.banks(c, "var", U)
            sq = [self.sb(c, "sq", [P, tiles, CH]) for _ in range(U)]
            sd = [self.sb(c, "sd", [S, CH // S]) for _ in range(U)]
            rs = [self.sb(c, "rs", [S, CH // S]) for _ in range(U)]
            diag = [self.sb(c, "diag", [S, CH // S, S]) for _ in range(U)]
            mean_ready, centered, squared, var_ready, sd_ready, inverted, diagonal, spread, scaled = (self.sem(c, n) for n in (
                "mean_ready", "centered", "squared", "var_ready", "sd_ready", "inverted", "diagonal", "spread", "scaled"))
            block = c.enter_context(nc.Block())

            def chunk(a, i, u):
                return a[:, :, bass.ds(i * (U * CH) + u * CH, CH)]

            @block.tensor
            def _(pe):
                with pe.Fori(0, NC // U) as i:
                    for u in range(U):
                        x = chunk(src, i, u)
                        for t in range(tiles):
                            ins = pe.matmul(mu[u][:, 0:CH], mean[:, :], x[:, t, :], start=t == 0, stop=t == tiles - 1)
                        ins.then_inc(mean_ready, 1)
                    for u in range(U):
                        pe.wait_ge(squared, U * i + (u + 1))
                        for k in range(CH // S):
                            for t in range(tiles):
                                ins = pe.matmul(var[u][0:S, k:k + 1], sq[u][:, t, S * k:S * (k + 1)], mean[:, 0:1],
                                                start=t == 0, stop=t == tiles - 1)
                        ins.then_inc(var_ready, 1)
                    for u in range(U):
                        pe.wait_ge(diagonal, U * i + (u + 1))
                        pe.matmul(var[u][:, 0:CH], self.ones[0:S, :], diag[u][:, :, :].rearrange("q k s -> q (k s)"),
                                  start=True, stop=True).then_inc(spread, 1)

            @block.scalar
            def _(act):
                with act.Fori(0, NC // U) as i:
                    for u in range(U):
                        act.wait_ge(var_ready, U * i + (u + 1))
                        act.activation(sd[u][:, :], var[u][0:S, 0:CH // S], ACT.Sqrt, bias=self.eps[0:S, 0:1]).then_inc(sd_ready, 1)

            @block.gpsimd
            def _(pool):
                with pool.Fori(0, NC // U) as i:
                    for u in range(U):
                        pool.wait_ge(inverted, U * i + (u + 1))
                        pool.tensor_tensor(diag[u][:, :, :], self.ident[0:S, 0:S].unsqueeze(1).to_broadcast([S, CH // S, S]),
                                           rs[u][:, :].unsqueeze(2).to_broadcast([S, CH // S, S]), ALU.mult).then_inc(diagonal, 1)

            per = 1 if gamma is None else 1 + tiles

            @block.vector
            def _(dve):
                with dve.Fori(0, NC // U) as i:
                    for u in range(U):
                        dve.wait_ge(mean_ready, U * i + (u + 1))
                        dve.tensor_tensor(chunk(dst, i, u), chunk(src, i, u),
                                          mu[u][:, 0:CH].unsqueeze(1).to_broadcast([P, tiles, CH]),
                                          ALU.subtract).then_inc(centered, 1)
                    for u in range(U):
                        dve.wait_ge(centered, U * i + (u + 1))
                        dve.tensor_tensor(sq[u][:, :, :], chunk(dst, i, u), chunk(dst, i, u), ALU.mult).then_inc(squared, 1)
                    for u in range(U):
                        dve.wait_ge(sd_ready, U * i + (u + 1))
                        dve.reciprocal(rs[u][:, :], sd[u][:, :]).then_inc(inverted, 1)
                    for u in range(U):
                        done = Tally(scaled, i * (U * per) + u * per)
                        y = chunk(dst, i, u)
                        dve.wait_ge(spread, U * i + (u + 1))
                        done.inc(dve.tensor_tensor(y, y, var[u][:, 0:CH].unsqueeze(1).to_broadcast([P, tiles, CH]), ALU.mult))
                        if gamma is not None:
                            done.wait(dve)
                            for t in range(tiles):
                                done.inc(dve.tensor_scalar(y[:, t, :], y[:, t, :], gamma[:, t:t + 1], beta[:, t:t + 1],
                                                           ALU.mult, ALU.add))

    def linear(self, src, w, dst, bias=None, func=ACT.Identity, add=None, gate=False, rows=P):
        nc = self.nc
        kt, mt = src.shape[1], dst.shape[1]
        with ExitStack() as c:
            ps = self.banks(c, "lin", 4)
            product, moved = self.sem(c, "product"), self.sem(c, "moved")
            block = c.enter_context(nc.Block())
            n = 2 * mt

            @block.tensor
            def _(pe):
                pe.sem_inc(moved, 4)
                with pe.Fori(0, NPAIR) as i:
                    for k in range(n):
                        u, m = divmod(k, mt)
                        bank = ps[k % 4] if n % 4 == 0 else ps[k % 2]
                        ahead = 4 if n % 4 == 0 else 2
                        pe.wait_ge(moved, n * i + (k + 1 + 4 - ahead))
                        x = src[:, :, bass.ds(i * (2 * CH) + u * CH, CH)]
                        for t in range(kt):
                            ins = pe.matmul(bank[:, 0:CH], w[:, t, m * P:(m + 1) * P], x[:, t, :],
                                            start=t == 0, stop=t == kt - 1)
                        ins.then_inc(product, 1)

            def takes(eng, put):
                with eng.Fori(0, NPAIR) as i:
                    for k in range(n):
                        u, m = divmod(k, mt)
                        bank = ps[k % 4] if n % 4 == 0 else ps[k % 2]
                        eng.wait_ge(product, n * i + (k + 1))
                        put(dst[:, m, bass.ds(i * (2 * CH) + u * CH, CH)], bank[:, 0:CH], m, i, u).then_inc(moved, 1)

            if add is None:
                @block.scalar
                def _(act):
                    takes(act, lambda y, x, m, i, u: act.activation(
                        y, x, func, bias=0.0 if bias is None else bias[:, m:m + 1]))
            else:
                @block.vector
                def _(dve):
                    def put(y, x, m, i, u):
                        a = add[:, m, bass.ds(i * (2 * CH) + u * CH, CH)]
                        if bias is None:
                            return dve.tensor_tensor(y, a, x, ALU.add)
                        return dve.scalar_tensor_tensor(y, x, bias[:, m:m + 1], a, ALU.add, ALU.add)
                    takes(dve, put)

    def loads(self, pairs):
        nc = self.nc
        with ExitStack() as c:
            loaded = self.sem(c, "weights")
            block = c.enter_context(nc.Block())

            @block.sync
            def _(sp):
                for t, s in pairs:
                    sp.dma_start(t, s).then_inc(loaded, 16)
                sp.wait_ge(loaded, 16 * len(pairs))

    def split_queries(self, w, bias, parts):
        nc = self.nc
        with ExitStack() as c:
            ps = self.banks(c, "qps", 2)
            q = [self.sb(c, "q", [P, CH]) for _ in range(2)]
            r = [self.sb(c, "r", [P, CH]) for _ in range(2)]
            product, split = self.sem(c, "q_product"), self.sem(c, "q_split")
            per = 6 if bias is not None else 5
            block = c.enter_context(nc.Block())

            @block.tensor
            def _(pe):
                pe.sem_inc(split, 2 * per)
                with pe.Fori(0, NPAIR) as i:
                    for u in range(2):
                        pe.wait_ge(split, 2 * per * i + per * (u + 1))
                        pe.matmul(ps[u][:, 0:CH], w[:, :], self.yT[:, bass.ds(i * (2 * CH) + u * CH, CH)],
                                  start=True, stop=True).then_inc(product, 1)

            @block.vector
            def _(dve):
                with dve.Fori(0, NPAIR) as i:
                    for u in range(2):
                        done = Tally(split, 2 * per * i + (2 * per + per * u))
                        p1, p2, p3 = (p[:, bass.ds(i * (2 * CH) + u * CH, CH)] for p in parts)
                        dve.wait_ge(product, 2 * i + (u + 1))
                        if bias is None:
                            done.inc(dve.tensor_scalar(q[u][:, :], ps[u][:, 0:CH], SCALE, None, ALU.mult))
                        else:
                            done.inc(dve.tensor_scalar(q[u][:, :], ps[u][:, 0:CH], bias[:, 0:1], None, ALU.add))
                            done.wait(dve)
                            done.inc(dve.tensor_scalar(q[u][:, :], q[u][:, :], SCALE, None, ALU.mult))
                        done.wait(dve)
                        done.inc(dve.tensor_copy(p1, q[u][:, :]))
                        done.wait(dve)
                        done.inc(dve.tensor_tensor(r[u][:, :], q[u][:, :], p1, ALU.subtract))
                        done.wait(dve)
                        done.inc(dve.tensor_copy(p2, r[u][:, :]))
                        done.wait(dve)
                        done.inc(dve.tensor_tensor(p3, r[u][:, :], p2, ALU.subtract))

    def long_attention(self, wq, wk, wv, wo, bo, bq=None, bk=None, bv=None, wo_full=None, query_mask=None, key_mask=None):
        nc, d = self.nc, self.d
        with ExitStack() as c:
            sb = lambda name, shape, dt=F32: self.sb(c, name, shape, dt)
            wq_t, wk_t, wv_t = sb("wq", [P, P]), sb("wk", [P, P]), sb("wv", [P, P])
            wo_t = sb("wo", [P, 4, P])
            den_col = sb("den_col", [P, 4])
            bo_t = sb("bo", [P, 1])
            q_parts = [sb(f"q{k}_", [P, N], BF16) for k in range(3)]
            pairs = [(wq_t[:, :], wq), (wk_t[:, :], wk), (wv_t[:, :], wv), (wo_t[:, :, :], wo.rearrange("s p o -> p s o")),
                     (den_col[:, :], d["den_col"]), (bo_t[:, :], bo)]
            bq_t = bk_t = None
            if bq is not None:
                bq_t, bk_t = sb("bq", [P, 1]), sb("bk", [P, 1])
                bv_t, wo_full_t = sb("bv", [P, 1]), sb("wo_full", [P, P])
                pairs += [(bq_t[:, :], bq), (bk_t[:, :], bk), (bv_t[:, :], bv), (wo_full_t[:, :], wo_full)]
            self.loads(pairs)
            if bq is not None:
                self.fold_bias(bo_t[:, :], wo_full_t[:, :], bv_t[:, :], bo_t[:, :])
            self.split_queries(wq_t, bq_t, q_parts)
            loop = lambda first_tile, turns: self.long_attention_loop(
                wk_t, wv_t, wo_t, den_col, bo_t, bk_t, q_parts, query_mask, key_mask, first_tile, turns)
            if query_mask is None:
                loop(0, 2)
                return
            early = self.count_allowed(c, query_mask, LATE * KT)
            with nc.If(early > 0):
                loop(0, 2)
            with nc.Else():
                loop(LATE, 4)

    def count_allowed(self, c, query_mask, width):
        nc = self.nc
        flag = self.sb(c, "flag", [1, 1], I32)
        with ExitStack() as c2:
            mask, some, ones = self.sb(c2, "mask", [S, width], U8), self.sb(c2, "some", [S, 1]), self.sb(c2, "ones", [S, 1])
            count = self.banks(c2, "count", 1)[0]
            mask_in, reduced, counted, flag_set = (self.sem(c2, n) for n in ("mask_in", "reduced", "counted", "flag_set"))
            block = c2.enter_context(nc.Block())

            @block.sync
            def _(sp):
                sp.dma_start(mask[:, :], query_mask[:, 0:width]).then_inc(mask_in, 16)
                sp.wait_ge(flag_set, 1)

            @block.tensor
            def _(pe):
                pe.wait_ge(reduced, 2)
                pe.matmul(count[0:1, 0:1], some[:, :], ones[:, :], start=True, stop=True).then_inc(counted, 1)
                pe.wait_ge(flag_set, 1)

            @block.vector
            def _(dve):
                dve.memset(ones[:, :], 1.0).then_inc(reduced, 1)
                dve.wait_ge(mask_in, 16)
                dve.tensor_reduce(some[:, :], mask[:, :], AX.X, ALU.max).then_inc(reduced, 1)
                dve.wait_ge(counted, 1)
                dve.tensor_copy(flag[:, :], count[0:1, 0:1]).then_inc(flag_set, 1)
                dve.wait_ge(flag_set, 1)

            @block.scalar
            def _(act):
                act.wait_ge(flag_set, 1)

            @block.gpsimd
            def _(pool):
                pool.wait_ge(flag_set, 1)
        return nc.values_load(flag[0:1, 0:1], min_val=0, max_val=S)

    def long_attention_loop(self, wk, wv, wo, den_col, bo, bk, q_parts, query_mask, key_mask, first_tile, turns):
        nc, d, xT = self.nc, self.d, self.xT
        U = turns
        nt = NT - first_tile
        ncc = nt // TG
        key0 = first_tile * KT
        nkeys = S2 - key0
        NK = 4 if ncc == 1 else 2

        def keys_of(t):
            return min(KT, nkeys - t * KT)

        def keys_in_chunk(k):
            return min(KC, nkeys - k * KC)

        with ExitStack() as c:
            sb = lambda name, shape, dt=F32: self.sb(c, name, shape, dt)
            ctx = [sb(f"ctx{v}", [P, nkeys]) for v in range(2)]
            k_parts = [sb(f"k{k}_", [P, nkeys], BF16) for k in range(3)]
            k_rest = sb("k_rest", [P, nkeys])
            k_pack = [sb(f"k_pack{v}", [R_ALL, NP, nkeys], BF16) for v in range(NK)]
            q1_blk = [sb(f"q1_blk{v}", [R_MASK + 1, NP, 2, S], BF16) for v in range(2)]
            q2_blk = [sb(f"q2_blk{v}", [R_ALL, NP, 2, S], BF16) for v in range(2)]
            v_ext = [sb(f"v_ext{v}", [KT, nt, H, HD + 1]) for v in range(2)]
            probs = sb("probs", [KT, 4, NP * S])
            row_max3 = sb("row_max3", [S, 2, NP, ncc])
            neg_max = sb("neg_max", [S, 2, NP])
            max_rest = sb("max_rest", [S, 2, NP])
            max_parts = sb("max_parts", [S, 2, 3, NP], BF16)
            max_rows = sb("max_rows", [2 * 3 * NP, S], BF16)
            ident_b = sb("ident_b", [S, 4, S], BF16)
            acc_sb = sb("acc_sb", [P, 4 * S])
            den_inv, den_wide = sb("den_inv", [S, H]), sb("den_wide", [S, H, 32])
            heads_out = sb("heads_out", [P, 4, S])
            score2 = [c.enter_context(nc.psum_tensor(f"score2_{self.uid}_{g}", [P, 2, 512], F32))
                      for g in range(2)]
            score1 = self.banks(c, "score1_", 2)
            acc = self.banks(c, "acc", 1)[0]
            misc = self.banks(c, "misc", 1)[0]
            if query_mask is not None:
                qm_u8 = sb("qm_u8", [S, nkeys], U8)
                qm_bias = sb("qm_bias", [S, nkeys], BF16)
            if key_mask is not None:
                km_u8 = sb("km_u8", [B, nkeys], U8)
                km_bias = sb("km_bias", [B, nkeys], BF16)
                km_dram = nc.dram_tensor(f"key_mask_bias_{self.uid}", [B, nkeys], BF16, kind="Internal").ap()

            rows_set, mask_made = self.sem(c, "rows_set"), self.sem(c, "mask_made")
            with ExitStack() as c2:
                mask_in, mask_out = self.sem(c2, "mask_in"), self.sem(c2, "mask_out")
                block = c2.enter_context(nc.Block())

                @block.sync
                def _(sp):
                    if query_mask is not None:
                        sp.dma_start(qm_u8[:, :], query_mask[:, key0:]).then_inc(mask_in, 16)
                        sp.wait_ge(mask_in, 16)
                    if key_mask is not None:
                        sp.dma_start(km_u8[:, :], key_mask[:, key0:]).then_inc(mask_in, 16)
                        sp.wait_ge(mask_made, 1)
                        sp.dma_start(km_dram, km_bias[:, :]).then_inc(mask_out, 16)
                        sp.wait_ge(mask_out, 16)

                @block.gpsimd
                def _(pool):
                    done = Tally(rows_set)
                    fills = [(t[R_MASK:R_ALL, :, :], 1.0) for t in k_pack] + [(t[R_MASK:R_MASK + 1, :, :], 0.0) for t in k_pack]
                    for t in q1_blk + q2_blk:
                        fills += [(t[:, :, :, :], 0.0), (t[R_MASK:R_MASK + 1, :, :, :], 1.0)]
                    for tile, value in fills + [(t[:, :, :, :], 1.0) for t in v_ext]:
                        done.inc(pool.memset(tile, value))
                        done.wait(pool)

                @block.tensor
                def _(pe):
                    pe.wait_ge(rows_set, 1)

                @block.scalar
                def _(act):
                    act.wait_ge(rows_set, 1)

                @block.vector
                def _(dve):
                    dve.memset(acc[:, :], 0.0)
                    for k in range(4):
                        dve.tensor_copy(ident_b[:, k, :], self.ident[0:S, 0:S])
                    if query_mask is not None:
                        dve.wait_ge(mask_in, 16)
                        dve.tensor_scalar(qm_bias[:, :], qm_u8[:, :], -1.0, -NEG, ALU.add, ALU.mult).then_inc(mask_made, 1)
                    if key_mask is not None:
                        dve.wait_ge(mask_in, 16)
                        dve.tensor_scalar(km_bias[:, :], km_u8[:, :], NEG, None, ALU.mult).then_inc(mask_made, 1)

            ctx_in = [self.sem(c, f"ctx_in{v}") for v in range(2)]
            q_in = [self.sem(c, f"q_in{v}") for v in range(2)]
            packed = [[self.sem(c, f"packed{v}_{k}") for k in range(ncc)] for v in range(NK)]
            max_in = [self.sem(c, f"max_in{v}") for v in range(2)]
            (k_ready, k1_made, k2_made, r1_made, k_split, v_ready, v_made, score1_ready, score1_used, chain, maxed,
             max_turned, max_rows_made, q2_made, scored, exps, avs, acc_out, den_ready, inverted, spread, den_made, heads_made, out_ready,
             added, seen, pool_seen, sp_seen) = (self.sem(c, n) for n in (
                "k_ready", "k1_made", "k2_made", "r1_made", "k_split", "v_ready", "v_made", "score1_ready",
                "score1_used", "chain", "maxed", "max_turned", "max_rows_made", "q2_made", "scored", "exps", "avs",
                "acc_out", "den_ready", "inverted", "spread", "den_made", "heads_made", "out_ready", "added", "seen", "pool_seen", "sp_seen"))
            n_pack = 16 * (TERMS + (key_mask is not None))
            n_q = 16 * TERMS * 2
            NQ = H * ncc
            CHAIN = 5

            class Seq:

                def __init__(self, i, j):
                    self.n, self.i, self.j = U * i + j, i, j
                    self.v, self.nk = j % 2, j % NK
                    self.fill, self.fill_k = i * (U // 2) + j // 2, i * (U // NK) + j // NK

                def later(self, k):
                    return Seq(self.i, self.j + k)

                def within(self):
                    return not isinstance(self.n, int) or 0 <= self.n < B

            def all_turns(eng, turn):
                for b in range(U):
                    turn(Seq(0, b))
                with eng.Fori(1, (B - 4) // U) as i:
                    for u in range(U):
                        turn(Seq(i, u))
                for b in range(B - 4, B):
                    turn(Seq(b // U, b % U))

            SLOT_MAX = max(nt - 3, 2)
            HEAD = 5 if ncc == 1 else 0
            share = [0] + [HEAD + (NQ - HEAD) * t // SLOT_MAX for t in range(1, SLOT_MAX)] + [NQ] * (nt - SLOT_MAX + 1)
            SLOT_TURN = min(SLOT_MAX + 1, nt - 1)
            SLOT_DEN, SLOT_OUT = 2 * ncc, min(2 * ncc + 1, nt - 1)
            PIECE_SPREAD = 5
            block = c.enter_context(nc.Block())

            @block.sync
            def _(sp):
                def load_ctx(q):
                    sp.dma_start(ctx[q.v][:, :], d["ctxT"][:, bass.ds(q.n * S2 + key0, nkeys)]).then_inc(ctx_in[q.v], 16)

                def load_q(q):
                    for s in range(TERMS):
                        for a in range(2):
                            sp.dma_start(q1_blk[q.v][16 * s + 8 * a:16 * s + 8 * a + 8, :, a, :],
                                         q_parts[Q_PART[s]][64 * a:64 * a + 64, bass.ds(q.n * S, S)]).then_inc(q_in[q.v], 16)

                def pack_k(q, k):
                    w = keys_in_chunk(k)
                    sp.wait_ge(k_split, ncc * q.n + (k + 1))
                    for s in range(TERMS):
                        sp.dma_start(k_pack[q.nk][16 * s:16 * s + 16, :, k * KC:k * KC + w],
                                     k_parts[K_PART[s]][:, k * KC:k * KC + w]).then_inc(packed[q.nk][k], 16)
                    if key_mask is not None:
                        sp.dma_start(k_pack[q.nk][R_MASK:R_MASK + 1, :, k * KC:k * KC + w],
                                     km_dram[bass.ds(q.n, 1), k * KC:k * KC + w].unsqueeze(1).to_broadcast([1, NP, w]))\
                            .then_inc(packed[q.nk][k], 16)

                def max_to_rows(q):
                    sp.wait_ge(max_rows_made, q.n + 1)
                    for a in range(2):
                        sp.dma_start(q2_blk[q.v][R_MASK + 1 + 3 * a:R_MASK + 4 + 3 * a, :, a, :],
                                     max_rows[24 * a:24 * a + 24, :]).then_inc(max_in[q.v], 16)

                def turn(b):
                    n, m, l = b.later(1), b.later(2), b.later(3)
                    if m.within():
                        sp.wait_ge(score1_ready, NQ * b.n + NQ)
                        sp.sem_inc(sp_seen, 1)
                        sp.wait_ge(q2_made, b.n + 1)
                        load_q(m)
                    for k in range(ncc):
                        if m.within() and k < ncc - 1:
                            sp.wait_ge(scored, 2 * nt * b.n + (2 * TG * (k + 1) + 1))
                            sp.sem_inc(sp_seen, 1)
                            pack_k(m, k)
                        if l.within() and k == 0:
                            sp.wait_ge(v_ready, ncc * n.n + ncc)
                            load_ctx(l)
                    if ncc == 1 and m.within():
                        pack_k(m, 0)
                    if n.within():
                        max_to_rows(n)
                    if ncc > 1 and m.within():
                        sp.wait_ge(scored, 2 * nt * b.n + (2 * nt + 1))
                        sp.sem_inc(sp_seen, 1)
                        pack_k(m, ncc - 1)

                s0, s1 = Seq(0, 0), Seq(0, 1)
                load_ctx(s0)
                load_ctx(s1)
                load_q(s0)
                load_q(s1)
                for k in range(ncc):
                    pack_k(s0, k)
                sp.wait_ge(v_ready, ncc)
                load_ctx(Seq(0, 2))
                for k in range(ncc):
                    pack_k(s1, k)
                max_to_rows(s0)
                all_turns(sp, turn)

            @block.tensor
            def _(pe):
                def keys(q, k):
                    if k == 0:
                        pe.wait_ge(ctx_in[q.v], 16 * q.fill + 16)
                    w = keys_in_chunk(k)
                    pe.matmul(misc[:, 0:w], wk[:, :], ctx[q.v][:, k * KC:k * KC + w], start=True, stop=True).then_inc(k_ready, 1)

                def values(q, g):
                    for t in range(TG * g, TG * g + TG):
                        w = keys_of(t)
                        ins = pe.matmul(misc[0:w, (t % TG) * P:(t % TG + 1) * P], ctx[q.v][:, t * KT:t * KT + w], wv[:, :],
                                        start=True, stop=True)
                    ins.then_inc(v_ready, 1)

                def first_product(q, chunks, prologue=False):
                    for x in chunks:
                        k, h = divmod(x, H)
                        if h == 0:
                            pe.wait_ge(packed[q.nk][k], n_pack * q.fill_k + n_pack)
                        if x == 0:
                            pe.wait_ge(q_in[q.v], n_q * q.fill + n_q)
                        if not prologue or x > 1:
                            pe.wait_ge(score1_used, NQ * q.n + (x - 1))
                        w = keys_in_chunk(k)
                        pe.matmul(score1[x % 2][0:S, 0:w], q1_blk[q.v][0:R_MASK + 1, h // 2, h % 2, :],
                                  k_pack[q.nk][0:R_MASK + 1, h // 2, k * KC:k * KC + w], start=True, stop=True)\
                            .then_inc(score1_ready, 1)

                def max_transpose(q):
                    pe.wait_ge(maxed, q.n + 1)
                    pe.matmul(misc[0:6 * NP, 0:S], max_parts[:, :, :, :].rearrange("q a i p -> q (a i p)"),
                              ident_b[:, 0, :], start=True, stop=True).then_inc(max_turned, 1)

                def second_product(b, t, g, k):
                    w = keys_of(t)
                    if t == 0 and g == 0 and k == 0:
                        pe.wait_ge(q2_made, b.n + 1)
                        pe.wait_ge(max_in[b.v], 32 * b.fill + 32)
                    if k == 0:
                        pe.wait_ge(exps, 2 * nt * b.n + (2 * t + g + 1))
                    bank = score2[g][:, k, :]
                    for pp in range(2):
                        p = 4 * g + 2 * k + pp
                        ins = pe.matmul(bank[0:w, 2 * S * pp:2 * S * (pp + 1)],
                                        k_pack[b.nk][:, p, t * KT:t * KT + w],
                                        q2_blk[b.v][:, p, :, :].rearrange("r a q -> r (a q)"),
                                        start=pp == 0, stop=query_mask is None and pp == 1, skip_group_check=True)
                    if query_mask is not None:
                        ins = pe.matmul(bank[0:w, 0:4 * S], qm_bias[:, t * KT:t * KT + w],
                                        ident_b[:, :, :].rearrange("q k c -> q (k c)"),
                                        start=False, stop=True, skip_group_check=True)
                    if k == 1:
                        ins.then_inc(scored, 1)

                def weighted_values(b, t, s):
                    w = keys_of(t)
                    if t == 0 and s == 0:
                        pe.wait_ge(acc_out, b.n + 1)
                    if s == 0:
                        pe.wait_ge(exps, 2 * nt * b.n + (2 * t + 4))
                    for g in range(4):
                        h = 4 * s + g
                        ins = pe.matmul(acc[32 * g:32 * g + HD + 1, S * s:S * s + S], v_ext[b.v][0:w, t, h, :],
                                        probs[0:w, 2 * (t % 2) + h // 8, (h % 8) * S:(h % 8 + 1) * S],
                                        start=t == 0 and s == 0, stop=t == nt - 1 and s == 3, skip_group_check=True)
                    if s == 3:
                        ins.then_inc(avs, 1)

                def denominators(b):
                    pe.wait_ge(acc_out, b.n + 2)
                    for s in range(4):
                        ins = pe.matmul(misc[0:S, 4 * s:4 * s + 4], acc_sb[:, S * s:S * s + S], den_col[:, :], start=True, stop=True)
                    ins.then_inc(den_ready, 1)

                def spread_inverses(b):
                    pe.wait_ge(den_made, b.n + 1)
                    for s in range(4):
                        ins = pe.matmul(misc[:, S * s:S * s + S], den_wide[:, 4 * s:4 * s + 4, :].rearrange("q g e -> q (g e)"),
                                        self.ident[0:S, 0:S], start=True, stop=True)
                    ins.then_inc(spread, 1)

                def output(b):
                    pe.wait_ge(heads_made, b.n + 2)
                    for s in range(4):
                        ins = pe.matmul(misc[:, 0:S], wo[:, s, :], heads_out[:, s, :], start=s == 0, stop=s == 3)
                    ins.then_inc(out_ready, 1)

                def turn(b):
                    p, n, m = b.later(-1), b.later(1), b.later(2)
                    for t in range(nt):
                        if t < ncc and m.within():
                            if t == 0:
                                pe.wait_ge(max_rows_made, b.n + 1)
                            else:
                                pe.wait_ge(r1_made, ncc * m.n + t)
                            keys(m, t)
                        first = range(share[t], share[t + 1]) if n.within() else range(0)
                        if t == 0 and n.within():
                            first_product(n, first[:HEAD])
                            first = first[HEAD:]
                        for piece in range(8):
                            if piece < 4:
                                second_product(b, t, piece // 2, piece % 2)
                            elif t:
                                weighted_values(b, t - 1, piece - 4)
                            elif p.within():
                                weighted_values(p, nt - 1, piece - 4)
                            if piece == 3 and ncc <= t < 2 * ncc and n.within():
                                if t > ncc:
                                    pe.wait_ge(v_made, ncc * n.n + (t - ncc))
                                elif m.within():
                                    pe.wait_ge(r1_made, ncc * m.n + ncc)
                                else:
                                    pe.wait_ge(max_rows_made, b.n + 1)
                                values(n, t - ncc)
                            if piece == 3 and t == SLOT_DEN and p.within():
                                if n.within():
                                    pe.wait_ge(v_made, ncc * n.n + ncc)
                                denominators(p)
                            if piece == PIECE_SPREAD and t == SLOT_DEN and p.within():
                                spread_inverses(p)
                            if piece == 3 and t == SLOT_OUT and p.within():
                                output(p)
                            if piece == 5 and t == SLOT_TURN and n.within():
                                if p.within():
                                    pe.wait_ge(added, b.n + 1)
                                else:
                                    pe.wait_ge(v_made, ncc * n.n + ncc)
                                max_transpose(n)
                            c = len(first)
                            if c:
                                first_product(n, first[c * piece // 8:c * (piece + 1) // 8])

                pe.sem_inc(exps, 2)
                pe.sem_inc(avs, 2)
                pe.sem_inc(acc_out, 1)
                pe.sem_inc(scored, 1)
                pe.sem_inc(added, 1)
                pe.sem_inc(heads_made, 1)
                s0, s1 = Seq(0, 0), Seq(0, 1)
                for k in range(ncc):
                    if k:
                        pe.wait_ge(r1_made, k)
                    keys(s0, k)
                for k in range(ncc):
                    if k:
                        pe.wait_ge(v_made, k)
                    else:
                        pe.wait_ge(r1_made, ncc)
                    values(s0, k)
                for k in range(ncc):
                    if k:
                        pe.wait_ge(r1_made, ncc + k)
                    else:
                        pe.wait_ge(v_made, ncc)
                    keys(s1, k)
                first_product(s0, range(NQ), prologue=True)
                pe.wait_ge(r1_made, 2 * ncc)
                max_transpose(s0)
                all_turns(pe, turn)
                last = Seq((B - 1) // U, (B - 1) % U)
                for s in range(4):
                    weighted_values(last, nt - 1, s)
                pe.wait_ge(added, B)
                denominators(last)
                spread_inverses(last)
                output(last)

            @block.scalar
            def _(act):
                def k1(q, k):
                    w = keys_in_chunk(k)
                    if not isinstance(q.n, int) or q.n > 0:
                        last = q.later(-1) if q.j else Seq(q.i - 1, U - 1)
                        act.wait_ge(packed[last.nk][k], n_pack * last.fill_k + n_pack)
                    act.wait_ge(k_ready, ncc * q.n + (k + 1))
                    act.activation(k_parts[0][:, k * KC:k * KC + w], misc[:, 0:w], ACT.Identity,
                                   bias=0.0 if bk is None else bk[:, 0:1]).then_inc(k1_made, 1)

                def v_out(q, g):
                    act.wait_ge(v_ready, ncc * q.n + (g + 1))
                    full = TG if keys_of(TG * g + TG - 1) == KT else TG - 1
                    ins = act.activation(v_ext[q.v][:, TG * g:TG * g + full, :, 0:HD],
                                         misc[0:KT, 0:full * P].rearrange("p (t h d) -> p t h d", t=full, h=H), ACT.Copy)
                    if full < TG:
                        w = keys_of(TG * g + full)
                        ins = act.activation(v_ext[q.v][0:w, TG * g + full, :, 0:HD],
                                             misc[0:w, full * P:TG * P].rearrange("p (h d) -> p h d", h=H), ACT.Copy)
                    ins.then_inc(v_made, 1)

                def exp_tile(b, t):
                    w = keys_of(t)
                    act.wait_ge(avs, nt * b.n + (t + 1))
                    for g in range(2):
                        act.wait_ge(scored, 2 * nt * b.n + (2 * t + g + 2))
                        act.activation(probs[0:w, 2 * (t % 2) + g, :].rearrange("p (k c) -> p k c", k=2),
                                       score2[g][0:w, :, 0:4 * S], ACT.Exp).then_inc(exps, 1)

                def sums_out(b):
                    act.wait_ge(avs, nt * b.n + (nt + 2))
                    act.wait_ge(heads_made, b.n + 1)
                    act.activation(acc_sb[:, :], acc[:, 0:4 * S], ACT.Copy).then_inc(acc_out, 1)

                def turn(b):
                    p, n, m = b.later(-1), b.later(1), b.later(2)
                    for t in range(nt):
                        if t < ncc and m.within():
                            k1(m, t)
                        exp_tile(b, t)
                        if t == 0 and p.within():
                            sums_out(p)
                        if ncc <= t < 2 * ncc and n.within():
                            v_out(n, t - ncc)

                s0, s1 = Seq(0, 0), Seq(0, 1)
                for k in range(ncc):
                    k1(s0, k)
                for k in range(ncc):
                    v_out(s0, k)
                for k in range(ncc):
                    k1(s1, k)
                all_turns(act, turn)
                sums_out(Seq((B - 1) // U, (B - 1) % U))

            @block.gpsimd
            def _(pool):
                def split(q, k):
                    w = keys_in_chunk(k)
                    k2, k3, r = (x[:, k * KC:k * KC + w] for x in (k_parts[1], k_parts[2], k_rest))
                    if not isinstance(q.n, int) or q.n > 0:
                        last = q.later(-1) if q.j else Seq(q.i - 1, U - 1)
                        pool.wait_ge(packed[last.nk][k], n_pack * last.fill_k + n_pack)
                    pool.wait_ge(r1_made, ncc * q.n + (k + 1))
                    pool.sem_inc(pool_seen, 1)
                    pool.tensor_scalar(k2, r, 1.0, 0.0, ALU.mult, ALU.add).then_inc(k2_made, 1)
                    pool.wait_ge(k2_made, ncc * q.n + (k + 1))
                    pool.tensor_tensor(k3, r, k2, ALU.subtract).then_inc(k_split, 1)

                def turn(b):
                    m = b.later(2)
                    if m.within():
                        for k in range(ncc):
                            split(m, k)

                for k in range(ncc):
                    split(Seq(0, 0), k)
                for k in range(ncc):
                    split(Seq(0, 1), k)
                all_turns(pool, turn)

            @block.vector
            def _(dve):
                def r1(q, k):
                    w = keys_in_chunk(k)
                    if not isinstance(q.n, int) or q.n > 0:
                        dve.wait_ge(k_split, ncc * (q.n - 1) + (k + 1))
                    dve.wait_ge(k1_made, ncc * q.n + (k + 1))
                    out, k1_ = k_rest[:, k * KC:k * KC + w], k_parts[0][:, k * KC:k * KC + w]
                    if bk is None:
                        ins = dve.tensor_tensor(out, misc[:, 0:w], k1_, ALU.subtract)
                    else:
                        ins = dve.scalar_tensor_tensor(out, misc[:, 0:w], bk[:, 0:1], k1_, ALU.add, ALU.subtract)
                    ins.then_inc(r1_made, 1)

                def copy_q(q, prologue=False):
                    dve.wait_ge(q_in[q.v], n_q * q.fill + n_q)
                    if not prologue:
                        dve.wait_ge(scored, 2 * nt * (q.n - 1) + 1)
                    dve.tensor_copy(q2_blk[q.v][0:R_MASK, :, :, :], q1_blk[q.v][0:R_MASK, :, :, :]).then_inc(q2_made, 1)

                def chunk_max(q, x):
                    k, h = divmod(x, H)
                    w = keys_in_chunk(k)
                    dve.wait_ge(score1_ready, NQ * q.n + (x + 1))
                    to = row_max3[:, h % 2, h // 2, k:k + 1]
                    if query_mask is not None:
                        dve.sem_inc(seen, 1)
                        bank = score1[x % 2][0:S, 0:w]
                        ins = dve.tensor_tensor_reduce(bank, bank, qm_bias[:, k * KC:k * KC + w], 1.0, -3e38, ALU.add, ALU.max, to)
                    else:
                        ins = dve.tensor_reduce(to, score1[x % 2][0:S, 0:w], AX.X, ALU.max)
                    ins.then_inc(score1_used, 1)

                def max_chain(q):
                    done = Tally(chain, CHAIN * q.n)
                    dve.wait_ge(score1_used, NQ * q.n + NQ)
                    done.inc(dve.tensor_reduce(neg_max[:, :, :], row_max3[:, :, :, :], AX.X, ALU.max, negate=True))
                    done.wait(dve)
                    done.inc(dve.tensor_scalar(neg_max[:, :, :], neg_max[:, :, :], 1e20, None, ALU.min))
                    done.wait(dve)
                    done.inc(dve.tensor_copy(max_parts[:, :, 0, :], neg_max[:, :, :]))
                    done.wait(dve)
                    done.inc(dve.tensor_tensor(max_rest[:, :, :], neg_max[:, :, :], max_parts[:, :, 0, :], ALU.subtract))
                    done.wait(dve)
                    done.inc(dve.tensor_copy(max_parts[:, :, 1, :], max_rest[:, :, :]))
                    done.wait(dve)
                    dve.tensor_tensor(max_parts[:, :, 2, :], max_rest[:, :, :], max_parts[:, :, 1, :], ALU.subtract)\
                        .then_inc(maxed, 1)

                def rows_out(q):
                    dve.wait_ge(max_turned, q.n + 1)
                    dve.tensor_copy(max_rows[:, :], misc[0:6 * NP, 0:S]).then_inc(max_rows_made, 1)

                def invert(b):
                    dve.wait_ge(den_ready, b.n + 1)
                    dve.reciprocal(den_inv[:, :], misc[0:S, 0:H]).then_inc(inverted, 1)
                    dve.wait_ge(inverted, b.n + 1)
                    dve.tensor_copy(den_wide[:, :, :], den_inv[:, :].unsqueeze(2).to_broadcast([S, H, 32])).then_inc(den_made, 1)

                def divide(b):
                    dve.wait_ge(spread, b.n + 1)
                    dve.tensor_tensor(heads_out[:, :, :].rearrange("p s q -> p (s q)"), acc_sb[:, :], misc[:, 0:4 * S], ALU.mult)\
                        .then_inc(heads_made, 1)

                def add_output(b):
                    dve.wait_ge(out_ready, b.n + 1)
                    x = xT[:, bass.ds(b.n * S, S)]
                    dve.scalar_tensor_tensor(x, misc[:, 0:S], bo[:, 0:1], x, ALU.add, ALU.add).then_inc(added, 1)

                def turn(b):
                    p, n, m = b.later(-1), b.later(1), b.later(2)
                    if n.within():
                        copy_q(n)
                    for t in range(nt):
                        first = range(share[t], share[t + 1]) if n.within() else range(0)
                        rest = iter(first)

                        def chunks(count):
                            for _, x in zip(range(count), rest):
                                chunk_max(n, x)

                        c = len(first)
                        if t < ncc and m.within():
                            chunks(2)
                            r1(m, t)
                        if t == SLOT_DEN and p.within():
                            chunks(c * 3 // 8)
                            invert(p)
                            if t == SLOT_MAX and n.within():
                                max_chain(n)
                            chunks(c * PIECE_SPREAD // 8 - c * 3 // 8)
                            divide(p)
                        if t == SLOT_OUT and p.within():
                            chunks(c * 4 // 8)
                            add_output(p)
                        chunks(c)
                        if t == SLOT_MAX and n.within() and not (t == SLOT_DEN and p.within()):
                            max_chain(n)
                        if t == SLOT_TURN and n.within():
                            rows_out(n)

                s0, s1 = Seq(0, 0), Seq(0, 1)
                for q in (s0, s1):
                    for k in range(ncc):
                        r1(q, k)
                copy_q(s0, prologue=True)
                for x in range(NQ):
                    chunk_max(s0, x)
                max_chain(s0)
                rows_out(s0)
                all_turns(dve, turn)
                last = Seq((B - 1) // U, (B - 1) % U)
                invert(last)
                divide(last)
                add_output(last)

    def on_vector(self, steps):
        with ExitStack() as c:
            stepped = self.sem(c, "stepped")
            block = c.enter_context(self.nc.Block())

            @block.vector
            def _(dve):
                done = Tally(stepped)
                for step in steps:
                    done.inc(step(dve))
                    done.wait(dve)

    def on_scalar(self, dst, src, func):
        with ExitStack() as c:
            block = c.enter_context(self.nc.Block())

            @block.scalar
            def _(act):
                act.activation(dst, src, func)

    def global_scale(self, x, part, whole, scale, inv, op, reduce, finish):
        with ExitStack() as c:
            reduced, joined, stepped = (self.sem(c, n) for n in ("reduced", "joined", "stepped"))
            block = c.enter_context(self.nc.Block())

            @block.vector
            def _(dve):
                dve.tensor_reduce(part, x, AX.X, op, apply_absolute_value=True).then_inc(reduced, 1)
                dve.wait_ge(joined, 1)
                done = Tally(stepped)
                done.inc(finish(dve, scale, whole))
                done.wait(dve)
                done.inc(dve.reciprocal(inv, scale))

            @block.gpsimd
            def _(pool):
                pool.wait_ge(reduced, 1)
                pool.partition_all_reduce(whole, part, P, reduce).then_inc(joined, 1)

    def act_qdq(self, c, x):
        part, whole, scale, inv = (self.sb(c, n, [P, 1])[:, :] for n in ("part", "whole", "scale", "inv"))
        self.global_scale(x, part, whole, scale, inv, ALU.max, RMAX,
                          lambda dve, s, w: dve.tensor_scalar(s, w, 1.0 / 32767.0, 1e-12, ALU.mult, ALU.max))
        self.on_vector([
            lambda dve: dve.tensor_scalar(x, x, inv, ROUND, ALU.mult, ALU.add),
            lambda dve: dve.tensor_scalar(x, x, ROUND, 32767.0, ALU.subtract, ALU.min),
            lambda dve: dve.tensor_scalar(x, x, -32768.0, scale, ALU.max, ALU.mult)])

    def turn_weights(self, jobs):
        with ExitStack() as c:
            ps = self.banks(c, "turn", 2)
            turned, moved = self.sem(c, "turned"), self.sem(c, "moved")
            block = c.enter_context(self.nc.Block())

            @block.tensor
            def _(pe):
                for n, (out, pairs) in enumerate(jobs):
                    rows, cols = out.shape
                    if n >= 2:
                        pe.wait_ge(moved, n - 1)
                    for k, (a, b) in enumerate(pairs):
                        ins = pe.matmul(ps[n % 2][0:rows, 0:cols], a, b, start=k == 0, stop=k == len(pairs) - 1)
                    ins.then_inc(turned, 1)

            @block.scalar
            def _(act):
                for n, (out, pairs) in enumerate(jobs):
                    rows, cols = out.shape
                    act.wait_ge(turned, n + 1)
                    act.activation(out, ps[n % 2][0:rows, 0:cols], ACT.Copy).then_inc(moved, 1)

    def fold_bias(self, total, w, b, bias):
        with ExitStack() as c:
            ps = self.banks(c, "fold", 1)[0]
            product = self.sem(c, "product")
            block = c.enter_context(self.nc.Block())

            @block.tensor
            def _(pe):
                pe.matmul(ps[:, 0:1], w, b, start=True, stop=True).then_inc(product, 1)

            @block.vector
            def _(dve):
                dve.wait_ge(product, 1)
                dve.tensor_tensor(total, bias, ps[:, 0:1], ALU.add)

    def ffn0(self, x3, y3):
        d = self.d
        with ExitStack() as c:
            sb = lambda name, shape, dt=F32: self.sb(c, name, shape, dt)
            F = 3
            up_t, gate_t, down_t = sb("up_t", [P, 1, F * P]), sb("gate_t", [P, 1, F * P]), sb("down_t", [P, F, P])
            with ExitStack() as c2:
                nat = self.sb(c2, "nat", [P, 3, F * P])
                step, inv = self.sb(c2, "step", [P, 36]), self.sb(c2, "inv", [P, 36])
                tiles = lambda w: w.rearrange("(t o) i -> o t i", o=P)
                split = lambda x: x.rearrange("o (t i) -> o t i", t=F)
                self.loads([(split(nat[:, 0, :]), tiles(d["w_up"])), (split(nat[:, 1, :]), tiles(d["w_gate"])),
                            (nat[:, 2, :], d["w_down"])])
                w = nat[:, :, :].rearrange("o k (n e) -> o (k n) e", e=32)
                wide = lambda x: x[:, :].unsqueeze(2).to_broadcast([P, 36, 32])
                self.on_vector([
                    lambda dve: dve.tensor_reduce(step[:, :], w, AX.X, ALU.max, apply_absolute_value=True),
                    lambda dve: dve.tensor_scalar(step[:, :], step[:, :], 1.0 / 7.0, 1e-12, ALU.mult, ALU.max),
                    lambda dve: dve.reciprocal(inv[:, :], step[:, :]),
                    lambda dve: dve.tensor_tensor(w, w, wide(inv), ALU.mult),
                    lambda dve: dve.tensor_scalar(w, w, ROUND, ROUND, ALU.add, ALU.subtract),
                    lambda dve: dve.tensor_scalar(w, w, -8.0, 7.0, ALU.max, ALU.min),
                    lambda dve: dve.tensor_tensor(w, w, wide(step), ALU.mult)])
                i_ = self.ident[:, :]
                self.turn_weights(
                    [(up_t[:, 0, t * P:(t + 1) * P], [(nat[:, 0, t * P:(t + 1) * P], i_)]) for t in range(F)]
                    + [(gate_t[:, 0, t * P:(t + 1) * P], [(nat[:, 1, t * P:(t + 1) * P], i_)]) for t in range(F)]
                    + [(down_t[:, t, :], [(nat[:, 2, t * P:(t + 1) * P], i_)]) for t in range(F)])
            self.layernorm(x3, y3)
            self.act_qdq(c, self.yT[:, :])
            up, gate = sb("up", [P, F, N]), sb("gate", [P, F, N])
            sig = sb("sig", [P, F, N])
            flat = lambda x: x[:, :, :].rearrange("p f n -> p (f n)")
            self.linear(y3, up_t, up)
            self.linear(y3, gate_t, gate)
            self.act_qdq(c, flat(up))
            self.act_qdq(c, flat(gate))
            self.on_scalar(flat(sig), flat(gate), ACT.Sigmoid)
            self.on_vector([
                lambda dve: dve.tensor_scalar(flat(sig), flat(sig), 65536.0, ROUND, ALU.mult, ALU.add),
                lambda dve: dve.tensor_scalar(flat(sig), flat(sig), ROUND, 0.0, ALU.subtract, ALU.max),
                lambda dve: dve.tensor_scalar(flat(sig), flat(sig), 65535.0, 1.0 / 65536.0, ALU.min, ALU.mult),
                lambda dve: dve.tensor_tensor(flat(gate), flat(gate), flat(sig), ALU.mult)])
            self.act_qdq(c, flat(gate))
            self.on_vector([lambda dve: dve.tensor_tensor(flat(gate), flat(gate), flat(up), ALU.mult)])
            self.act_qdq(c, flat(gate))
            self.linear(gate, down_t, x3, add=x3)

    def ffn1(self, x3, y3):
        d = self.d
        with ExitStack() as c:
            sb = lambda name, shape, dt=F32: self.sb(c, name, shape, dt)
            wt, bias = sb("wt", [P, 6, P]), sb("bias", [P, 6])
            gamma, beta = sb("gamma", [P, 3]), sb("beta", [P, 3])
            with ExitStack() as c2:
                q, w, sc = self.sb(c2, "q", [P, 6, P], I32), self.sb(c2, "w", [P, 6, P]), self.sb(c2, "sc", [P, 6, 8])
                la, lb = self.sb(c2, "la", [32, 6, P]), self.sb(c2, "lb", [32, 6, P])
                self.loads([(q[:, :, :], d["l1_q"].rearrange("k o i -> o k i")), (sc[:, :, :], d["l1_scales"].rearrange("k o g -> o k g")),
                            (la[:, :, :], d["l1_la"].rearrange("k r i -> r k i")), (lb[:, :, :], d["l1_lbT"].rearrange("k r o -> r k o")),
                            (bias[:, :], d["l1_biasT"]), (gamma[:, :], d["l1_gammaT"]), (beta[:, :], d["l1_betaT"])])
                grouped = w[:, :, :].rearrange("o k (g e) -> o (k g) e", e=16)
                steps = sc[:, :, :].rearrange("o k g -> o (k g)").unsqueeze(2).to_broadcast([P, 48, 16])
                self.on_vector([
                    lambda dve: dve.tensor_scalar(w[:, :, :], q[:, :, :], 1.0 / 7.5, 1.0, ALU.mult, ALU.subtract),
                    lambda dve: dve.tensor_tensor(grouped, grouped, steps, ALU.mult)])
                self.turn_weights([(wt[:, k, :], [(w[:, k, :], self.ident[:, :]), (la[:, k, :], lb[:, k, :])]) for k in range(6)])
            z = sb("z", [P, 1, N])
            self.layernorm(x3, y3)
            for k in range(3):
                self.linear(y3, wt[:, 2 * k:2 * k + 1, :], z, bias=bias[:, 2 * k:2 * k + 1])
                self.layernorm(z, z, gamma=gamma[:, k:k + 1], beta=beta[:, k:k + 1])
                self.on_scalar(z[:, :, :], z[:, :, :], ACT.Gelu)
                self.linear(z, wt[:, 2 * k + 1:2 * k + 2, :], y3, bias=bias[:, 2 * k + 1:2 * k + 2], add=y3)
            self.on_vector([lambda dve: dve.tensor_tensor(self.xT[:, :], self.xT[:, :], self.yT[:, :], ALU.add)])

    def short_attention(self):
        nc, d, xT, yT = self.nc, self.d, self.xT, self.yT
        with ExitStack() as c:
            sb = lambda name, shape, dt=F32: self.sb(c, name, shape, dt)
            wq, wk, wv, wo, wo_full = sb("wq", [P, P]), sb("wk", [P, P]), sb("wv", [P, P]), sb("wo", [P, 4, P]), sb("wo_full", [P, P])
            bq, bk, bv, bo = (sb(n, [P, 1]) for n in ("bq", "bk", "bv", "bo"))
            head_mask, den_col = sb("head_mask", [P, H]), sb("den_col", [P, 4])
            mask_i, bias, causal = sb("mask_i", [S, B, S], I32), sb("bias", [S, B, S]), sb("causal", [S, S])
            key_mask = d["mask_if1"].rearrange("b (a k) -> a b k", a=1)[:, :, 0:S].to_broadcast([S, B, S])
            self.loads([(wq[:, :], d["l2_wq"]), (wk[:, :], d["l2_wk"]), (wv[:, :], d["l2_wv"]),
                        (wo[:, :, :], d["l2_wo"].rearrange("s p o -> p s o")), (wo_full[:, :], d["l2_wo_full"]),
                        (bq[:, :], d["l2_bq"]), (bk[:, :], d["l2_bk"]), (bv[:, :], d["l2_bv"]), (bo[:, :], d["l2_bo"]),
                        (head_mask[:, :], d["head_mask"]), (den_col[:, :], d["den_col"]), (causal[:, :], d["causal"]),
                        (mask_i[:, :, :], key_mask)])
            self.fold_bias(bo[:, :], wo_full[:, :], bv[:, :], bo[:, :])
            q_sb, k_sb, ctx = ([sb(f"{n}{u}", [P, S]) for u in range(2)] for n in ("q_sb", "k_sb", "ctx"))
            q_m = [sb(f"q_m{u}", [P, H, S]) for u in range(2)]
            v_ext = [sb(f"v_ext{u}", [S, H, HD + 1]) for u in range(2)]
            HH = H // 2
            probs = [sb(f"probs{g}", [S, HH, S]) for g in range(2)]
            probs_t = [sb(f"probs_t{g}", [S, HH, S]) for g in range(2)]
            top = [sb(f"top{g}", [S, HH]) for g in range(2)]
            den_inv, den_wide = sb("den_inv", [S, H]), sb("den_wide", [S, H, 32])
            acc_sb, heads_out = sb("acc_sb", [P, 4 * S]), sb("heads_out", [P, 4, S])
            qkv = self.banks(c, "qkv", 2)
            big = [c.enter_context(nc.psum_tensor(f"big{g}_{self.uid}", [P, 2, 512], F32)) for g in range(2)]
            acc = self.banks(c, "acc", 1)[0]
            misc = self.banks(c, "misc", 1)[0]
            self.on_vector([
                lambda dve: dve.tensor_scalar(bias[:, :, :], mask_i[:, :, :], 0.0, NEG, ALU.is_equal, ALU.mult),
                lambda dve: dve.tensor_tensor(bias[:, :, :], bias[:, :, :], causal[:, :].unsqueeze(1).to_broadcast([S, B, S]), ALU.min),
                lambda dve: dve.memset(v_ext[0][:, :, :], 1.0),
                lambda dve: dve.memset(v_ext[1][:, :, :], 1.0),
                lambda dve: dve.memset(acc[:, :], 0.0)])
            ctx_in = [self.sem(c, f"ctx_in{u}") for u in range(2)]
            (qkv_ready, q_made, k_made, v_made, q_masked, scored, steps, lowered, exped, turned, turned_out, summed,
             sums_out, den_ready, inverted, den_made, spread, heads_made, out_ready, added) = (self.sem(c, n) for n in (
                "qkv_ready", "q_made", "k_made", "v_made", "q_masked", "scored", "steps", "lowered", "exped", "turned",
                "turned_out", "summed", "sums_out", "den_ready", "inverted", "den_made", "spread", "heads_made", "out_ready", "added"))
            four = lambda x: x.rearrange("q (k h) s -> q k h s", k=2)
            scores = [big[g][0:S, :, 0:4 * S].rearrange("q k (h s) -> q k h s", h=4) for g in range(2)]

            class Seq:

                def __init__(self, i, j):
                    self.n, self.i, self.j, self.v, self.fill = 2 * i + j, i, j, j % 2, i + j // 2

                def later(self, k):
                    return Seq(self.i, self.j + k)

                def within(self):
                    return not isinstance(self.n, int) or 0 <= self.n < B

            def all_turns(eng, turn):
                for b in range(2):
                    turn(Seq(0, b))
                with eng.Fori(1, B // 2 - 1) as i:
                    for u in range(2):
                        turn(Seq(i, u))
                for b in range(B - 2, B + 2):
                    turn(Seq(b // 2, b % 2))

            block = c.enter_context(nc.Block())

            @block.sync
            def _(sp):
                for q in (Seq(0, 0), Seq(0, 1)):
                    sp.dma_start(ctx[q.v][:, :], d["ctxT"][:, q.n * S2:q.n * S2 + S]).then_inc(ctx_in[q.v], 16)
                with sp.Fori(0, B // 2 - 1) as i:
                    for u in range(2):
                        sp.wait_ge(qkv_ready, 2 * i + (u + 1))
                        sp.dma_start(ctx[u][:, :], d["ctxT"][:, bass.ds((2 * i + (u + 2)) * S2, S)]).then_inc(ctx_in[u], 16)

            @block.tensor
            def _(pe):
                def project(q):
                    pe.wait_ge(ctx_in[q.v], 16 * q.fill + 16)
                    if not isinstance(q.n, int) or q.n > 1:
                        pe.wait_ge(v_made, q.n - 1)
                    bank = qkv[q.v]
                    pe.matmul(bank[:, 0:S], wq[:, :], yT[:, bass.ds(q.n * S, S)], start=True, stop=True)
                    pe.matmul(bank[:, P:P + S], wk[:, :], ctx[q.v][:, :], start=True, stop=True)
                    pe.matmul(bank[0:S, 2 * P:3 * P], ctx[q.v][:, :], wv[:, :], start=True, stop=True).then_inc(qkv_ready, 1)

                def score(q, g):
                    if g == 0:
                        pe.wait_ge(k_made, q.n + 1)
                        pe.wait_ge(q_masked, q.n + 1)
                    pe.wait_ge(turned_out, 2 * q.n + (g + 1))
                    for h in range(HH):
                        ins = pe.matmul(big[g][0:S, h // 4, (h % 4) * S:(h % 4 + 1) * S], q_m[q.v][:, HH * g + h, :],
                                        k_sb[q.v][:, :], start=True, stop=True)
                    ins.then_inc(scored, 1)

                def turn_probs(q, g):
                    pe.wait_ge(exped, 2 * q.n + (g + 1))
                    for h in range(HH):
                        ins = pe.transpose(big[g][0:S, h // 4, (h % 4) * S:(h % 4 + 1) * S], probs[g][:, h, :], self.ident[0:S, 0:S])
                    ins.then_inc(turned, 1)

                def weighted_values(q, g):
                    pe.wait_ge(turned_out, 2 * q.n + (g + 3))
                    if g == 0:
                        pe.wait_ge(v_made, q.n + 1)
                        pe.wait_ge(sums_out, q.n + 1)
                    for s in range(2 * g, 2 * g + 2):
                        for k in range(4):
                            h = 4 * s + k
                            ins = pe.matmul(acc[32 * k:32 * k + HD + 1, S * s:S * s + S], v_ext[q.v][:, h, :],
                                            probs_t[g][:, h % HH, :], start=s == 0, stop=s == 3, skip_group_check=True)
                    ins.then_inc(summed, 1)

                def denominators(q):
                    pe.wait_ge(sums_out, q.n + 2)
                    pe.wait_ge(added, q.n + 1)
                    for s in range(4):
                        ins = pe.matmul(misc[0:S, 4 * s:4 * s + 4], acc_sb[:, S * s:S * s + S], den_col[:, :], start=True, stop=True)
                    ins.then_inc(den_ready, 1)

                def spread_inverses(q):
                    pe.wait_ge(den_made, q.n + 1)
                    for s in range(4):
                        ins = pe.matmul(misc[:, S * s:S * s + S], den_wide[:, 4 * s:4 * s + 4, :].rearrange("q g e -> q (g e)"),
                                        self.ident[0:S, 0:S], start=True, stop=True)
                    ins.then_inc(spread, 1)

                def output(q):
                    pe.wait_ge(heads_made, q.n + 1)
                    for s in range(4):
                        ins = pe.matmul(misc[:, 0:S], wo[:, s, :], heads_out[:, s, :], start=s == 0, stop=s == 3)
                    ins.then_inc(out_ready, 1)

                def turn(b):
                    o, p, n = b.later(-2), b.later(-1), b.later(1)
                    if n.within():
                        project(n)
                    if b.within():
                        score(b, 0)
                    if p.within():
                        turn_probs(p, 1)
                    if o.within():
                        denominators(o)
                    if p.within():
                        weighted_values(p, 0)
                    if b.within():
                        score(b, 1)
                    if b.within():
                        turn_probs(b, 0)
                    if o.within():
                        spread_inverses(o)
                    if p.within():
                        weighted_values(p, 1)
                    if o.within():
                        output(o)

                pe.sem_inc(turned_out, 2)
                pe.sem_inc(sums_out, 1)
                pe.sem_inc(added, 1)
                project(Seq(0, 0))
                all_turns(pe, turn)

            @block.scalar
            def _(act):
                def q_and_k(q):
                    act.wait_ge(qkv_ready, q.n + 1)
                    act.activation(q_sb[q.v][:, :], qkv[q.v][:, 0:S], ACT.Identity, bias=bq[:, 0:1]).then_inc(q_made, 1)
                    act.activation(k_sb[q.v][:, :], qkv[q.v][:, P:P + S], ACT.Identity, bias=bk[:, 0:1]).then_inc(k_made, 1)

                def exp(q, g):
                    act.wait_ge(lowered, 2 * q.n + (g + 1))
                    act.activation(probs[g][:, :, :], probs[g][:, :, :], ACT.Exp).then_inc(exped, 1)

                def take_turned(q, g):
                    act.wait_ge(turned, 2 * q.n + (g + 1))
                    act.activation(four(probs_t[g][:, :, :]), scores[g], ACT.Copy).then_inc(turned_out, 1)

                def take_sums(q):
                    act.wait_ge(summed, 2 * q.n + 2)
                    if not isinstance(q.n, int) or q.n > 0:
                        act.wait_ge(heads_made, q.n)
                    act.activation(acc_sb[:, :], acc[:, 0:4 * S], ACT.Copy).then_inc(sums_out, 1)

                def turn(b):
                    o, p, n = b.later(-2), b.later(-1), b.later(1)
                    if p.within():
                        exp(p, 1)
                    if o.within():
                        take_sums(o)
                    if n.within():
                        q_and_k(n)
                    if b.within():
                        act.activation(v_ext[b.v][:, :, 0:HD], qkv[b.v][0:S, 2 * P:3 * P].rearrange("p (h d) -> p h d", h=H), ACT.Copy)\
                            .then_inc(v_made, 1)
                    if p.within():
                        take_turned(p, 1)
                    if b.within():
                        exp(b, 0)
                        take_turned(b, 0)

                q_and_k(Seq(0, 0))
                all_turns(act, turn)

            @block.gpsimd
            def _(pool):
                with pool.Fori(0, B // 2) as i:
                    for u in range(2):
                        pool.wait_ge(q_made, 2 * i + (u + 1))
                        pool.tensor_tensor(q_m[u][:, :, :], q_sb[u][:, :].unsqueeze(1).to_broadcast([P, H, S]),
                                           head_mask[:, :].unsqueeze(2).to_broadcast([P, H, S]), ALU.mult).then_inc(q_masked, 1)

            @block.vector
            def _(dve):
                def lower(q, g):
                    done = Tally(steps, 6 * q.n + 3 * g)
                    m = bias[:, bass.ds(q.n, 1), :].to_broadcast([S, HH, S])
                    dve.wait_ge(scored, 2 * q.n + (g + 1))
                    done.inc(dve.tensor_tensor(four(probs[g][:, :, :]), scores[g], four(m), ALU.add))
                    done.wait(dve)
                    done.inc(dve.tensor_reduce(top[g][:, :], probs[g][:, :, :], AX.X, ALU.max))
                    done.wait(dve)
                    done.inc(dve.tensor_scalar(top[g][:, :], top[g][:, :], -1e20, None, ALU.max))
                    done.wait(dve)
                    dve.tensor_tensor(probs[g][:, :, :], probs[g][:, :, :], top[g][:, :].unsqueeze(2).to_broadcast([S, HH, S]),
                                      ALU.subtract).then_inc(lowered, 1)

                def turn(b):
                    o = b.later(-2)
                    if b.within():
                        lower(b, 0)
                    if o.within():
                        dve.wait_ge(den_ready, o.n + 1)
                        dve.reciprocal(den_inv[:, :], misc[0:S, 0:H]).then_inc(inverted, 1)
                    if b.within():
                        lower(b, 1)
                    if o.within():
                        dve.wait_ge(inverted, o.n + 1)
                        dve.tensor_copy(den_wide[:, :, :], den_inv[:, :].unsqueeze(2).to_broadcast([S, H, 32])).then_inc(den_made, 1)
                        dve.wait_ge(spread, o.n + 1)
                        dve.tensor_tensor(heads_out[:, :, :].rearrange("p s q -> p (s q)"), acc_sb[:, :], misc[:, 0:4 * S], ALU.mult)\
                            .then_inc(heads_made, 1)
                        dve.wait_ge(out_ready, o.n + 1)
                        x = xT[:, bass.ds(o.n * S, S)]
                        dve.scalar_tensor_tensor(x, misc[:, 0:S], bo[:, 0:1], x, ALU.add, ALU.add).then_inc(added, 1)

                all_turns(dve, turn)

    def ffn2(self, x3, y3):
        nc, d, xT, yT = self.nc, self.d, self.xT, self.yT
        E = 16
        self.layernorm(x3, y3)
        with ExitStack() as c:
            sb = lambda name, shape, dt=F32: self.sb(c, name, shape, dt)
            w1, b1, w2, b2 = sb("w1", [P, P]), sb("b1", [P, 1]), sb("w2", [P, E + 1]), sb("b2", [1, E + 1])
            scales, biases, rank, ones = sb("scales", [E, P]), sb("biases", [E, P]), sb("rank", [S, E]), sb("ones", [1, S])
            self.loads([(w1[:, :], d["l2f_w1"]), (b1[:, :], d["l2f_b1"]), (w2[:, :], d["l2f_w2"]), (b2[:, :], d["l2f_b2"]),
                        (scales[:, :], d["l2f_scales"]), (biases[:, :], d["l2f_biases"]), (rank[:, :], d["rank"]),
                        (ones[:, :], d["ones"])])
            hid = [sb(f"hid{u}", [P, CH]) for u in range(2)]
            gate = [sb(f"gate{u}", [S, 4]) for u in range(2)]
            score = [sb(f"score{u}", [S, 4, E]) for u in range(2)]
            cand = [sb(f"cand{u}", [S, 4, E]) for u in range(2)]
            top = [sb(f"top{u}", [S, 4]) for u in range(2)]
            chosen = [sb(f"chosen{u}", [E, CH]) for u in range(2)]
            routed = [sb(f"routed{u}", [P, CH]) for u in range(2)]
            hp = self.banks(c, "hp", 2)
            sp_ = self.banks(c, "scores", 2)
            one = self.banks(c, "one", 2)
            gain, shift = self.banks(c, "gain", 2)
            (hid_ready, relu_made, tanh_made, scored, gated, steps, chosen_made, turned, turned_out, expert_ready,
             routed_made) = (self.sem(c, n) for n in (
                "hid_ready", "relu_made", "tanh_made", "scored", "gated", "steps", "chosen_made", "turned", "turned_out",
                "expert_ready", "routed_made"))
            R_ = P // 2
            block = c.enter_context(nc.Block())

            @block.tensor
            def _(pe):
                pe.sem_inc(routed_made, 1)
                with pe.Fori(0, NPAIR) as i:
                    for u in range(2):
                        pe.matmul(hp[u][:, 0:CH], w1[:, :], yT[:, bass.ds(i * (2 * CH) + u * CH, CH)], start=True, stop=True)\
                            .then_inc(hid_ready, 1)
                    for u in range(2):
                        pe.wait_ge(relu_made, 2 * i + (u + 1))
                        pe.wait_ge(tanh_made, 2 * i + (u + 1))
                        for k in range(4):
                            o = sp_[u][0:S, 32 * k:32 * k + E + 1]
                            pe.matmul(o, hid[u][:, S * k:S * (k + 1)], w2[:, :], start=True, stop=False)
                            ins = pe.matmul(o, ones[:, :], b2[:, :], start=False, stop=True)
                        ins.then_inc(scored, 1)
                    for u in range(2):
                        pe.wait_ge(chosen_made, 2 * i + (u + 1))
                        for k in range(4):
                            ins = pe.transpose(one[u][0:E, S * k:S * (k + 1)], cand[u][:, k, :], self.ident[0:S, 0:S])
                        ins.then_inc(turned, 1)
                    for u in range(2):
                        pe.wait_ge(turned_out, 2 * i + (u + 1))
                        pe.wait_ge(routed_made, 6 * i + (3 * u + 1))
                        pe.matmul(gain[:, 0:CH], scales[:, :], chosen[u][:, :], start=True, stop=True)
                        pe.matmul(shift[:, 0:CH], biases[:, :], chosen[u][:, :], start=True, stop=True).then_inc(expert_ready, 1)

            @block.scalar
            def _(act):
                with act.Fori(0, NPAIR) as i:
                    for u in range(2):
                        act.wait_ge(hid_ready, 2 * i + (u + 1))
                        act.activation(hid[u][0:R_, :], hp[u][0:R_, 0:CH], ACT.Relu, bias=b1[0:R_, 0:1]).then_inc(relu_made, 1)
                        act.activation(hid[u][R_:P, :], hp[u][R_:P, 0:CH], ACT.Tanh, bias=b1[R_:P, 0:1]).then_inc(tanh_made, 1)
                    for u in range(2):
                        act.wait_ge(scored, 2 * i + (u + 1))
                        act.activation(gate[u][:, :], sp_[u][0:S, 0:128].rearrange("q (k e) -> q k e", k=4)[:, :, E],
                                       ACT.Sigmoid).then_inc(gated, 1)
                    for u in range(2):
                        act.wait_ge(turned, 2 * i + (u + 1))
                        act.activation(chosen[u][:, :], one[u][0:E, 0:CH], ACT.Copy).then_inc(turned_out, 1)

            @block.vector
            def _(dve):
                with dve.Fori(0, NPAIR) as i:
                    for u in range(2):
                        done = Tally(steps, 10 * i + 5 * u)
                        wide = top[u][:, :].unsqueeze(2).to_broadcast([S, 4, E])
                        dve.wait_ge(gated, 2 * i + (u + 1))
                        done.inc(dve.tensor_tensor(score[u][:, :, :], sp_[u][0:S, 0:128].rearrange("q (k e) -> q k e", k=4)[:, :, 0:E],
                                                   gate[u][:, :].unsqueeze(2).to_broadcast([S, 4, E]), ALU.mult))
                        done.wait(dve)
                        done.inc(dve.tensor_reduce(top[u][:, :], score[u][:, :, :], AX.X, ALU.max))
                        done.wait(dve)
                        done.inc(dve.tensor_tensor(cand[u][:, :, :], score[u][:, :, :], wide, ALU.is_ge))
                        done.wait(dve)
                        done.inc(dve.tensor_tensor(cand[u][:, :, :], cand[u][:, :, :], rank[:, :].unsqueeze(1).to_broadcast([S, 4, E]), ALU.mult))
                        done.wait(dve)
                        done.inc(dve.tensor_reduce(top[u][:, :], cand[u][:, :, :], AX.X, ALU.max))
                        done.wait(dve)
                        dve.tensor_tensor(cand[u][:, :, :], cand[u][:, :, :], wide, ALU.is_ge).then_inc(chosen_made, 1)
                    for u in range(2):
                        done = Tally(routed_made, 6 * i + (3 * u + 1))
                        y, x = (t[:, bass.ds(i * (2 * CH) + u * CH, CH)] for t in (yT, xT))
                        dve.wait_ge(expert_ready, 2 * i + (u + 1))
                        done.inc(dve.tensor_tensor(routed[u][:, :], y, gain[:, 0:CH], ALU.mult))
                        done.wait(dve)
                        done.inc(dve.tensor_tensor(routed[u][:, :], routed[u][:, :], shift[:, 0:CH], ALU.add))
                        done.wait(dve)
                        done.inc(dve.tensor_tensor(x, x, routed[u][:, :], ALU.add))

    def context_sums(self, a2, wkv, diag):
        nc, d = self.nc, self.d
        with ExitStack() as c:
            sb = lambda name, shape, dt=F32: self.sb(c, name, shape, dt)
            ctx = [sb(f"ctx{u}", [P, S2]) for u in range(2)]
            G = NT // TG
            K = 2 * G
            keys, vals = ([sb(f"{n}{k}", [KT, TG, 8, 16]) for k in range(G)] for n in ("keys", "vals"))
            top, total = ([sb(f"{n}{k}", [KT, TG, 8]) for k in range(G)] for n in ("top", "total"))
            kv = [c.enter_context(nc.psum_tensor(f"kv{k}_{self.uid}", [P, TG, 2, P], F32)) for k in range(G)]
            acc = self.banks(c, "acc", 2)
            ctx_in = [self.sem(c, f"ctx_in{u}") for u in range(2)]
            kv_ready, topped, lowered, exped, summed, inverted, vals_made, acc_ready, acc_out = (self.sem(c, n) for n in (
                "kv_ready", "topped", "lowered", "exped", "summed", "inverted", "vals_made", "acc_ready", "acc_out"))
            block = c.enter_context(nc.Block())

            heads = lambda x: x.rearrange("q t (h e) -> q t h e", h=8)
            wide = lambda x: x[:, :, :].unsqueeze(3).to_broadcast([KT, TG, 8, 16])

            def all_steps(eng, step):
                with eng.Fori(0, B // 2 - 1) as i:
                    for k in range(K):
                        step(i, k, False)
                for k in range(K):
                    step(B // 2 - 1, k, True)

            @block.sync
            def _(sp):
                for u in range(2):
                    sp.dma_start(ctx[u][:, :], d["ctxT"][:, u * S2:(u + 1) * S2]).then_inc(ctx_in[u], 16)
                with sp.Fori(0, B // 2 - 1) as i:
                    for u in range(2):
                        sp.wait_ge(kv_ready, K * i + G * (u + 1))
                        sp.dma_start(ctx[u][:, :], d["ctxT"][:, bass.ds((2 * i + (u + 2)) * S2, S2)]).then_inc(ctx_in[u], 16)

            @block.tensor
            def _(pe):
                def project(i, k):
                    turn, g, u = k // K, k % G, (k // G) % 2
                    if g == 0:
                        pe.wait_ge(ctx_in[u], 16 * i + (16 * turn + 16))
                    pe.wait_ge(vals_made, K * i + (k + 1))
                    for t in range(TG):
                        w = keys_of(TG * g + t)
                        s = (TG * g + t) * KT
                        ins = pe.matmul(kv[g][0:w, t, :, :], ctx[u][:, s:s + w], wkv[:, :], start=True, stop=True)
                    ins.then_inc(kv_ready, 1)

                def step(i, k, last):
                    if not last or k + 2 < K:
                        project(i, k + 2)
                    g, u = k % G, k // G
                    pe.wait_ge(vals_made, K * i + (k + G + 1))
                    for t in range(TG):
                        w = keys_of(TG * g + t)
                        ins = pe.matmul(acc[u][:, 0:P], keys[g][0:w, t, :, :].rearrange("q h e -> q (h e)"),
                                        vals[g][0:w, t, :, :].rearrange("q h e -> q (h e)"),
                                        start=g == 0 and t == 0, stop=g == G - 1 and t == TG - 1)
                    if g == G - 1:
                        ins.then_inc(acc_ready, 1)

                project(0, 0)
                project(0, 1)
                all_steps(pe, step)

            @block.scalar
            def _(act):
                with act.Fori(0, B // 2) as i:
                    for k in range(K):
                        act.wait_ge(lowered, K * i + (k + 1))
                        act.activation(keys[k % G][:, :, :, :], keys[k % G][:, :, :, :], ACT.Exp, scale=0.5).then_inc(exped, 1)

            @block.vector
            def _(dve):
                def maxima(i, k):
                    g = k % G
                    dve.wait_ge(kv_ready, K * i + (k + 1))
                    dve.tensor_reduce(top[g][:, :, :], heads(kv[g][0:KT, :, 0, :]), AX.X, ALU.max).then_inc(topped, 1)

                def lower(i, k):
                    g = k % G
                    dve.wait_ge(topped, K * i + (k + 1))
                    dve.tensor_tensor(keys[g][:, :, :, :], heads(kv[g][0:KT, :, 0, :]), wide(top[g]), ALU.subtract).then_inc(lowered, 1)

                def step(i, k, last):
                    ahead = not last or k + 1 < K
                    n, g, u = K * i + (k + 1), k % G, k // G
                    if ahead:
                        maxima(i, k + 1)
                    dve.wait_ge(exped, n)
                    dve.tensor_reduce(total[g][:, :, :], keys[g][:, :, :, :], AX.X, ALU.add).then_inc(summed, 1)
                    if ahead:
                        lower(i, k + 1)
                    dve.wait_ge(summed, n)
                    dve.reciprocal(total[g][:, :, :], total[g][:, :, :]).then_inc(inverted, 1)
                    if g == 0:
                        take(i, u - 1)
                    dve.wait_ge(inverted, n)
                    dve.tensor_tensor(vals[g][:, :, :, :], heads(kv[g][0:KT, :, 1, :]), wide(total[g]), ALU.mult).then_inc(vals_made, 1)

                def take(i, u):
                    dve.wait_ge(acc_ready, 2 * i + (u + 2))
                    dve.tensor_tensor(a2[:, bass.ds(2 * i + (u + 1), 1), :].rearrange("p a e -> p (a e)"), acc[u % 2][:, 0:P],
                                      diag[:, :], ALU.mult).then_inc(acc_out, 1)

                for g in range(G):
                    dve.memset(kv[g][:, :, :, :], 0.0).then_inc(vals_made, 1)
                dve.memset(acc[1][:, :], 0.0).then_inc(acc_ready, 1)
                maxima(0, 0)
                lower(0, 0)
                all_steps(dve, step)
                take(B // 2 - 1, 1)

    def linear_attention(self, w, nh, mask, a2, wo, diag):
        nc, yT = self.nc, self.yT
        with ExitStack() as c:
            sb = lambda name, shape, dt=F32: self.sb(c, name, shape, dt)
            y_b, qk = [sb(f"y_b{u}", [P, S]) for u in range(2)], [sb(f"qk{u}", [S, nh, 16]) for u in range(2)]
            v_sb = [sb(f"v_sb{u}", [S, P]) for u in range(2)]
            top = [sb(f"top{u}", [S, nh]) for u in range(2)]
            q_t = [sb(f"q_t{u}", [P, S]) for u in range(2)]
            a_m = [sb(f"a_m{u}", [P, P]) for u in range(2)]
            mixed = [sb(f"mixed{u}", [16, 2, 4 * S]) for u in range(2)]
            ps, op = self.banks(c, "proj", 2), self.banks(c, "outp", 2)
            tr, ap = self.banks(c, "tr", 2)
            self.uid += 1
            bm = c.enter_context(nc.psum_tensor(f"bm_{self.uid}", [P, 2, 512], F32))
            (y_made, proj, steps, norm_steps, lowered, exped, v_made, normed, q_turned, a_ready, q_out, a_made, bm_ready, bm_out,
             out_ready, added) = (self.sem(c, n) for n in (
                "y_made", "proj", "steps", "norm_steps", "lowered", "exped", "v_made", "normed", "q_turned", "a_ready", "q_out",
                "a_made", "bm_ready", "bm_out", "out_ready", "added"))
            cols = w.shape[1]

            def all_turns(eng, front, turn):
                front(0)
                with eng.Fori(0, B // 2 - 1) as i:
                    turn(2 * i, True)
                turn(B - 2, False)

            block = c.enter_context(nc.Block())

            @block.tensor
            def _(pe):
                def front(n):
                    for u in range(2):
                        pe.wait_ge(y_made, n + (u + 1))
                        pe.matmul(ps[u][0:S, 0:cols], y_b[u][:, :], w[:, :], start=True, stop=True).then_inc(proj, 1)

                def turn(n, more):
                    for u in range(2):
                        pe.wait_ge(normed, n + (u + 1))
                        if u:
                            pe.wait_ge(q_out, n + 1)
                            pe.wait_ge(a_made, n + 1)
                        if a2 is None:
                            pe.wait_ge(v_made, n + (u + 1))
                            pe.matmul(ap[:, 0:P], qk[u][:, 8:16, :].rearrange("q h e -> q (h e)"), v_sb[u][:, :],
                                      start=True, stop=True).then_inc(a_ready, 1)
                        pe.transpose(tr[:, 0:S], qk[u][:, 0:8, :].rearrange("q h e -> q (h e)"), self.ident[0:S, 0:S])\
                            .then_inc(q_turned, 1)
                    if more:
                        front(n + 2)
                    for u in range(2):
                        pe.wait_ge(q_out, n + (u + 1))
                        pe.wait_ge(a_made, n + (u + 1))
                        pe.wait_ge(bm_out, n + (u + 1))
                        for h in range(8):
                            ins = pe.matmul(bm[0:16, h // 4, (h % 4) * S:(h % 4 + 1) * S], a_m[u][:, 16 * h:16 * h + 16], q_t[u][:, :],
                                            start=True, stop=True)
                        ins.then_inc(bm_ready, 1)
                    for u in range(2):
                        pe.wait_ge(bm_out, n + (u + 2))
                        pe.wait_ge(added, n + (u + 1))
                        flat = mixed[u][:, :, :].rearrange("e k s -> e (k s)").rearrange("e (w k) -> e k w", k=8)
                        for k in range(8):
                            ins = pe.matmul(op[u][:, 0:S], wo[:, k, :], flat[:, k, :], start=k == 0, stop=k == 7)
                        ins.then_inc(out_ready, 1)

                pe.sem_inc(bm_out, 1)
                pe.sem_inc(added, 2)
                all_turns(pe, front, turn)

            @block.scalar
            def _(act):
                def fixed_place(n):
                    for u in range(2):
                        act.activation(y_b[u][:, :], yT[:, bass.ds((n + u) * S, S)], ACT.Copy).then_inc(y_made, 1)

                def exp(n, u):
                    act.wait_ge(lowered, n + (u + 1))
                    act.activation(qk[u][:, :, :], qk[u][:, :, :], ACT.Exp, scale=0.5).then_inc(exped, 1)
                    if a2 is None:
                        act.activation(v_sb[u][:, :], ps[u][0:S, 2 * P:3 * P], ACT.Copy).then_inc(v_made, 1)

                def front(n):
                    fixed_place(n)
                    for u in range(2):
                        exp(n, u)

                def turn(n, more):
                    for u in range(2):
                        if a2 is not None:
                            act.activation(a_m[u][:, :], a2[:, bass.ds(n + (u + 1), 1), :].rearrange("p a e -> p (a e)"), ACT.Copy)\
                                .then_inc(a_made, 1)
                        act.wait_ge(q_turned, n + (u + 1))
                        act.activation(q_t[u][:, :], tr[:, 0:S], ACT.Copy).then_inc(q_out, 1)
                    if more:
                        fixed_place(n + 2)
                    for u in range(2):
                        if more:
                            exp(n + 2, u)
                        act.wait_ge(bm_ready, n + (u + 1))
                        act.activation(mixed[u][:, :, :], bm[0:16, :, 0:4 * S], ACT.Copy).then_inc(bm_out, 1)

                all_turns(act, front, turn)

            @block.vector
            def _(dve):
                def front(n):
                    for u in range(2):
                        done = Tally(steps, 2 * n + 2 * u)
                        raw = ps[u][0:S, 0:16 * nh].rearrange("q (h e) -> q h e", e=16)
                        dve.wait_ge(proj, n + (u + 1))
                        if mask is not None:
                            done.inc(dve.tensor_tensor(qk[u][:, :, :], raw, mask[:, :, :], ALU.add))
                        else:
                            done.inc(dve.tensor_copy(qk[u][:, :, :], raw))
                        done.wait(dve)
                        done.inc(dve.tensor_reduce(top[u][:, :], qk[u][:, :, :], AX.X, ALU.max))
                        done.wait(dve)
                        dve.tensor_tensor(qk[u][:, :, :], qk[u][:, :, :], top[u][:, :].unsqueeze(2).to_broadcast([S, nh, 16]),
                                          ALU.subtract).then_inc(lowered, 1)
                    for u in range(2):
                        done = Tally(norm_steps, 2 * n + 2 * u)
                        dve.wait_ge(exped, n + (u + 1))
                        done.inc(dve.tensor_reduce(top[u][:, :], qk[u][:, :, :], AX.X, ALU.add))
                        done.wait(dve)
                        done.inc(dve.reciprocal(top[u][:, :], top[u][:, :]))
                        done.wait(dve)
                        dve.tensor_tensor(qk[u][:, :, :], qk[u][:, :, :], top[u][:, :].unsqueeze(2).to_broadcast([S, nh, 16]),
                                          ALU.mult).then_inc(normed, 1)

                def turn(n, more):
                    if a2 is None:
                        for u in range(2):
                            dve.wait_ge(a_ready, n + (u + 1))
                            dve.tensor_tensor(a_m[u][:, :], ap[:, 0:P], diag[:, :], ALU.mult).then_inc(a_made, 1)
                    if more:
                        front(n + 2)
                    for u in range(2):
                        dve.wait_ge(out_ready, n + (u + 1))
                        y = yT[:, bass.ds((n + u) * S, S)]
                        dve.tensor_tensor(y, y, op[u][:, 0:S], ALU.add).then_inc(added, 1)

                all_turns(dve, front, turn)

    def attention3(self, x3, y3):
        d = self.d
        with ExitStack() as c:
            sb = lambda name, shape, dt=F32: self.sb(c, name, shape, dt)
            w1, w2q, w2kv = sb("w1", [P, 3 * P]), sb("w2q", [P, P]), sb("w2kv", [P, 2 * P])
            wo1, wo2 = sb("wo1", [16, 8, P]), sb("wo2", [16, 8, P])
            diag, mask = sb("diag", [P, P]), sb("mask", [S, 16, 16])
            gains = sb("gains", [P, 6])
            e1, e2 = sb("e1", [P // 2, P]), sb("e2", [P // 2, P])
            d1, d2 = sb("d1", [P // 2, P]), sb("d2", [P // 2, P])
            f1, f2 = sb("f1", [P, 1, P]), sb("f2", [P, 1, P])
            a2 = sb("a2", [P, B + 1, P])
            h = sb("h", [P, 1, N])
            self.loads([(w1[:, :], d["l3_w1"]), (w2q[:, :], d["l3_w2q"]), (w2kv[:, :], d["l3_w2kv"]),
                        (wo1[:, :, :], d["l3_wo1"].rearrange("(k e) o -> e k o", e=16)),
                        (wo2[:, :, :], d["l3_wo2"].rearrange("(k e) o -> e k o", e=16)),
                        (diag[:, :], d["diag"]), (mask[:, :, :], d["mask3"]), (gains[:, :], d["l3_gains"]),
                        (e1[:, :], d["l3_e1"]), (e2[:, :], d["l3_e2"]), (d1[:, :], d["l3_d1T"]), (d2[:, :], d["l3_d2T"])])
            self.turn_weights([(f1[:, 0, :], [(e1[:, :], d1[:, :])]), (f2[:, 0, :], [(e2[:, :], d2[:, :])])])
            self.context_sums(a2, w2kv, diag)
            self.layernorm(x3, y3)
            self.linear_attention(w1, 16, mask, None, wo1, diag)
            self.layernorm(y3, y3, gamma=gains[:, 0:1], beta=gains[:, 1:2])
            self.linear_attention(w2q, 8, None, a2, wo2, diag)
            self.layernorm(y3, y3, gamma=gains[:, 2:3], beta=gains[:, 3:4])
            self.linear(y3, f1, h, func=ACT.Silu)
            self.linear(h, f2, y3, add=y3)
            self.layernorm(y3, y3, gamma=gains[:, 4:5], beta=gains[:, 5:6])
            self.on_vector([lambda dve: dve.tensor_tensor(self.xT[:, :], self.xT[:, :], self.yT[:, :], ALU.add)])

    def ffn3(self, x3, y3):
        d = self.d
        F = 4
        with ExitStack() as c:
            sb = lambda name, shape, dt=F32: self.sb(c, name, shape, dt)
            w = [sb("w_fc", [P, 1, F * P]), sb("w_proj", [P, F, P])]
            gain, bias = sb("gain", [P, F]), sb("bias", [P, F])
            mean4 = sb("mean4", [P, P])
            part, whole, scale, inv = (sb(n, [P, 1])[:, :] for n in ("part", "whole", "scale", "inv"))
            self.loads([(w[0][:, 0, :], d["l3f_fcT"]), (w[1][:, :, :], d["l3f_projT"].rearrange("(t h) o -> h t o", h=P)),
                        (gain[:, :], d["l3f_w"]), (bias[:, :], d["l3f_b"])])
            for t in w:
                x = t[:, :, :].rearrange("p a b -> p (a b)")
                self.global_scale(x, part, whole, scale, inv, ALU.add, bass.bass_isa.ReduceOp.add,
                                  lambda dve, s, v: dve.tensor_scalar(s, v, 1.0 / (F * P * P), 1e-6, ALU.mult, ALU.add))
                self.on_vector([
                    lambda dve: dve.tensor_scalar(x, x, inv, ROUND, ALU.mult, ALU.add),
                    lambda dve: dve.tensor_scalar(x, x, ROUND, 1.0, ALU.subtract, ALU.min),
                    lambda dve: dve.tensor_scalar(x, x, -1.0, None, ALU.max),
                    lambda dve: dve.memset(mean4[:, :], 1.0 / (F * P))])
            h = sb("h", [P, F, N])
            self.layernorm(x3, y3)
            self.linear(y3, w[0], h, func=ACT.Gelu)
            self.layernorm(h, h, tiles=F, mean=mean4, gamma=gain, beta=bias)
            self.linear(h, w[1], x3, add=x3)

    def build(self, upto=99, first=0):
        nc, d = self.nc, self.d
        with ExitStack() as ctx:
            self.load_all(ctx)
            x3 = self.xT[:, :].unsqueeze(1)
            y3 = self.yT[:, :].unsqueeze(1)
            stages = [self.attention0, self.ffn0, self.attention1, self.ffn1, self.attention2, self.ffn2, self.attention3,
                      self.ffn3]
            for n, stage in enumerate(stages):
                if first <= n < upto:
                    stage(x3, y3)
                    self.clear_semaphores()
            self.store_out()

    def attention0(self, x3, y3):
        d = self.d
        self.layernorm(x3, y3)
        self.long_attention(d["l0_wq"], d["l0_wk"], d["l0_wv"], d["l0_wo"], d["l0_bo"], query_mask=d["query_mask"])

    def attention1(self, x3, y3):
        d = self.d
        self.layernorm(x3, y3)
        self.long_attention(d["l1_wq"], d["l1_wk"], d["l1_wv"], d["l1_wo"], d["l1_bo"], d["l1_bq"], d["l1_bk"],
                            d["l1_bv"], d["l1_wo_full"], key_mask=d["key_mask"])

    def attention2(self, x3, y3):
        self.layernorm(x3, y3)
        self.short_attention()


def _layout(inputs):
    import numpy as np

    g = {k: np.asarray(v) for k, v in inputs.items()}
    a = {}
    order = np.array([(2 * p + q) * HD + dd for q in range(2) for dd in range(HD) for p in range(NP)])

    def col(x):
        return np.ascontiguousarray(x.reshape(-1, 1))

    def out_rows(w_io):
        o = np.zeros((4, P, w_io.shape[1]), w_io.dtype)
        for h in range(H):
            o[h // 4, 32 * (h % 4):32 * (h % 4) + HD] = w_io[h * HD:(h + 1) * HD]
        return o

    a["xT"] = g["x"].reshape(N, P).T
    a["ctxT"] = g["ctx_1024"].reshape(B * S2, P).T
    a["ident"] = np.eye(P, dtype=np.float32)
    a["den_col"] = np.zeros((P, 4), np.float32)
    for k in range(4):
        a["den_col"][32 * k + HD, k] = 1.0
    a["query_mask"] = g["mask_1x1xSxS2_bk0"].reshape(S, S2)
    a["key_mask"] = g["mask_BxS2_bk0"]
    a["l0_wq"] = g["L0_xattn_Wq"].T[:, order]
    a["l0_wk"] = g["L0_xattn_Wk"].T[:, order]
    a["l0_wv"] = g["L0_xattn_Wv"].T
    a["l0_wo"] = out_rows(g["L0_xattn_Wo"].T)
    a["l0_bo"] = col(g["L0_xattn_bo"])

    def bias_rows(prefix, bq, bk, bv, bo, order_):
        for n, b in (("bq", bq[order_]), ("bk", bk[order_]), ("bv", bv), ("bo", bo)):
            a[f"{prefix}_{n}"] = col(b)

    a["w_up"], a["w_gate"], a["w_down"] = g["L0_ffn_w_up"], g["L0_ffn_w_gate"], g["L0_ffn_w_down"]
    a["l1_wq"] = g["L1_xattn_Wq"][:, order]
    a["l1_wk"] = g["L1_xattn_Wkv"][:, :P][:, order]
    a["l1_wv"] = g["L1_xattn_Wkv"][:, P:]
    a["l1_wo"], a["l1_wo_full"] = out_rows(g["L1_xattn_Wo"]), g["L1_xattn_Wo"]
    bias_rows("l1", g["L1_xattn_bq"], g["L1_xattn_bkv"][:P], g["L1_xattn_bkv"][P:], g["L1_xattn_bo"], order)
    a["l1_q"], a["l1_scales"], a["l1_la"] = g["L1_ffn_qweights"], g["L1_ffn_scales"], g["L1_ffn_lora_a"]
    a["l1_lbT"] = g["L1_ffn_lora_b"].transpose(0, 2, 1)
    a["l1_biasT"], a["l1_gammaT"], a["l1_betaT"] = (g[f"L1_ffn_{n}"].T for n in ("biases", "ln_gamma", "ln_beta"))
    for n in "qkv":
        a[f"l2_w{n}"] = g[f"L2_xattn_W{n}"].T
    a["l2_wo"], a["l2_wo_full"] = out_rows(g["L2_xattn_Wo"].T), g["L2_xattn_Wo"].T
    bias_rows("l2", *(g[f"L2_xattn_b{n}"] for n in "qkvo"), np.arange(P))
    a["mask_if1"] = g["mask_BxS2_if1"]
    head = np.arange(P) // HD
    a["head_mask"] = np.where(head[:, None] == np.arange(H)[None, :], SCALE, 0.0).astype(np.float32)
    a["causal"] = np.where(np.arange(S)[None, :] <= np.arange(S)[:, None], 0.0, NEG).astype(np.float32)
    a["l2f_w1"] = np.concatenate([g["L2_ffn_W1"], g["L2_ffn_Wg1"]], 1)
    a["l2f_b1"] = col(np.concatenate([g["L2_ffn_b1"], g["L2_ffn_bg1"]]))
    w2 = np.zeros((P, 17), np.float32)
    w2[:64, :16], w2[64:, 16:] = g["L2_ffn_W2"], g["L2_ffn_Wg2"]
    a["l2f_w2"] = w2
    a["l2f_b2"] = np.concatenate([g["L2_ffn_b2"], g["L2_ffn_bg2"]]).reshape(1, 17)
    a["l2f_scales"], a["l2f_biases"] = g["L2_ffn_expert_scales"], g["L2_ffn_expert_biases"]
    a["rank"] = np.broadcast_to(16.0 - np.arange(16), (S, 16)).astype(np.float32)
    a["ones"] = np.ones((1, S), np.float32)
    heads_in = lambda w: w.transpose(1, 0, 2).reshape(P, P)
    a["l3_w1"] = np.concatenate([heads_in(g[f"L3_xattn_W{n}1"]) for n in "qkv"], 1)
    a["l3_w2q"] = heads_in(g["L3_xattn_Wq2"])
    a["l3_w2kv"] = np.concatenate([heads_in(g[f"L3_xattn_W{n}2"]) for n in "kv"], 1)
    a["l3_wo1"], a["l3_wo2"] = g["L3_xattn_Wo1"].T, g["L3_xattn_Wo2"].T
    block = np.arange(P) // 16
    a["diag"] = (block[:, None] == block[None, :]).astype(np.float32)
    mask3 = np.zeros((S, 16, 16), np.float32)
    mask3[:, :8] = np.where(np.arange(16)[None, :] <= np.arange(S)[:, None], 0.0, NEG)[:, None, :]
    a["mask3"] = mask3
    a["l3_gains"] = np.stack([g[f"L3_xattn_{n}"] for n in ("g1", "b1", "g2", "b2", "g3", "b3")], 1)
    a["l3_e1"], a["l3_e2"] = g["L3_xattn_E1"], g["L3_xattn_E2"]
    a["l3_d1T"], a["l3_d2T"] = g["L3_xattn_D1"].T, g["L3_xattn_D2"].T
    a["l3f_fcT"], a["l3f_projT"] = g["L3_ffn_W_fc"].T, g["L3_ffn_W_proj"].T
    a["l3f_w"], a["l3f_b"] = g["L3_ffn_ln_w"].reshape(4, P).T, g["L3_ffn_ln_b"].reshape(4, P).T
    return {k: np.ascontiguousarray(v) for k, v in a.items()}


def kernel(**inputs):
    import numpy as _np
    import concourse.bacc as _bacc
    from concourse import mybir as _mybir
    from concourse.bass_utils import run_bass_kernel_spmd as _run

    nc = _bacc.Bacc("TRN2", target_bir_lowering=False, num_devices=1)
    arrays, args = {}, {}
    for name, a in _layout(inputs).items():
        arrays[f"in_{name}"] = a
        args[name] = nc.dram_tensor(f"in_{name}", a.shape, _mybir.dt.from_np(a.dtype), kind="ExternalInput").ap()
    out = nc.dram_tensor("out_xT", (P, N), F32, kind="ExternalOutput").ap()
    Kernel(nc, args, out).build()
    r = _run(nc, [arrays], core_ids=[0])
    return _np.ascontiguousarray(r.results[0]["out_xT"].T).reshape(B, S, P)
```
